# Optimizing a Trainium2 kernel written in Bass

```python
import numpy as np
import jax
import jax.numpy as jnp

def _softmax(x, axis=-1):
    return jax.nn.softmax(x, axis=axis)

def _gelu(x):
    return jax.nn.gelu(x, approximate=True)

def _silu(x):
    return jax.nn.silu(x)

def _sigmoid(x):
    return jax.nn.sigmoid(x)

def _layernorm(x, axis=-1, eps=1e-05):
    m = jnp.mean(x, axis=axis, keepdims=True)
    v = jnp.var(x, axis=axis, keepdims=True)
    return (x - m) / jnp.sqrt(v + eps)

def _scatter_add(tgt, idx, src, axis=0):
    return tgt.at[idx].add(src)

def _segment_sum(src, seg, n):
    return jax.ops.segment_sum(src, seg, n)
kernel_name = 'mk_seq_preln_d2_jaxref_r8_9247a7'

def setup_inputs(seed: int=0):
    np.random.seed(seed)
    _w = jnp.asarray

    def _L0_attn_setup():
        import jax, jax.numpy as jnp
        import numpy as np
        import math
        EMBED_DIM = 128
        NUM_HEADS = 16
        HEAD_DIM = EMBED_DIM // NUM_HEADS

        def alibi_slopes(num_heads: int) -> np.ndarray:

            def slopes_pow2(n):
                start = 2.0 ** (-2.0 ** (-(math.log2(n) - 3)))
                return [start * start ** i for i in range(n)]
            if math.log2(num_heads).is_integer():
                return np.array(slopes_pow2(num_heads), dtype=np.float32)
            closest = 2 ** math.floor(math.log2(num_heads))
            extra = slopes_pow2(2 * closest)[closest:]
            return np.array(slopes_pow2(closest) + extra[:num_heads - closest], dtype=np.float32)
        key = jax.random.key(seed)
        ks = jax.random.split(key, 9)
        B, S, E = (2, 256, EMBED_DIM)
        scale = 1.0 / math.sqrt(E)
        x = jax.random.normal(ks[0], (B, S, E), dtype=jnp.float32)
        Wq = jax.random.normal(ks[1], (E, E), dtype=jnp.float32) * scale
        Wk = jax.random.normal(ks[2], (E, E), dtype=jnp.float32) * scale
        Wv = jax.random.normal(ks[3], (E, E), dtype=jnp.float32) * scale
        Wo = jax.random.normal(ks[4], (E, E), dtype=jnp.float32) * scale
        bq = jax.random.normal(ks[5], (E,), dtype=jnp.float32) * 0.01
        bk = jax.random.normal(ks[6], (E,), dtype=jnp.float32) * 0.01
        bv = jax.random.normal(ks[7], (E,), dtype=jnp.float32) * 0.01
        bo = jax.random.normal(ks[8], (E,), dtype=jnp.float32) * 0.01
        return {'x': x, 'Wq': Wq, 'bq': bq, 'Wk': Wk, 'bk': bk, 'Wv': Wv, 'bv': bv, 'Wo': Wo, 'bo': bo}
    _L0_attn_in = _L0_attn_setup()

    def _L0_ffn_setup():
        import jax, jax.numpy as jnp
        import numpy as np
        EMBED = 128
        D_FF = 4 * EMBED
        N_EXPERTS = 8
        TOP_K = 2
        B, S = (2, 128)
        key = jax.random.key(seed)
        ks = jax.random.split(key, 10)
        sc_d = 1.0 / np.sqrt(EMBED)
        sc_h = 1.0 / np.sqrt(D_FF)
        return {'inputs': jax.random.normal(ks[0], (B, S, EMBED), jnp.float32), 'rw1': jax.random.normal(ks[1], (EMBED, D_FF), jnp.float32) * sc_d, 'rb1': jnp.zeros((D_FF,), jnp.float32), 'rw2': jax.random.normal(ks[2], (D_FF, N_EXPERTS), jnp.float32) * sc_h, 'rb2': jnp.zeros((N_EXPERTS,), jnp.float32), 'W1': jax.random.normal(ks[3], (N_EXPERTS, EMBED, D_FF), jnp.float32) * sc_d, 'b1': jnp.zeros((N_EXPERTS, D_FF), jnp.float32), 'W2': jax.random.normal(ks[4], (N_EXPERTS, D_FF, EMBED), jnp.float32) * sc_h, 'b2': jnp.zeros((N_EXPERTS, EMBED), jnp.float32)}
    _L0_ffn_in = _L0_ffn_setup()

    def _L1_attn_setup():
        import jax, jax.numpy as jnp
        import numpy as np
        B, N, DIM, H, DH = (2, 256, 128, 16, 64)
        INNER = H * DH
        EPS = 1e-12
        MAX_LOG_SCALE = np.log(1.0 / 0.01)
        key = jax.random.key(seed)
        k1, k2, k3, k4 = jax.random.split(key, 4)
        x = jax.random.normal(k1, (B, N, DIM), dtype=jnp.float32)
        w_qkv = jax.random.normal(k2, (DIM, 3 * INNER), dtype=jnp.float32) * DIM ** (-0.5)
        w_out = jax.random.normal(k3, (INNER, DIM), dtype=jnp.float32) * INNER ** (-0.5)
        b_out = jax.random.normal(k4, (DIM,), dtype=jnp.float32) * 0.01
        logit_scale = jnp.full((H, 1, 1), jnp.log(10.0), dtype=jnp.float32)
        return {'x': x, 'w_qkv': w_qkv, 'w_out': w_out, 'b_out': b_out, 'logit_scale': logit_scale}
    _L1_attn_in = _L1_attn_setup()

    def _L1_ffn_setup():
        import jax, jax.numpy as jnp
        import numpy as np
        T, Z, D_DIM = (8, 256, 128)
        N_EXP, P_SLOT, H = (64, 32, 128)
        LN_EPS = 1e-05
        key = jax.random.key(seed)
        k = jax.random.split(key, 5)
        s = 0.02
        return {'x': jax.random.normal(k[0], (T, Z, D_DIM), dtype=jnp.float32), 'phi_w': jax.random.normal(k[1], (N_EXP * P_SLOT, D_DIM), dtype=jnp.float32) * s, 'phi_b': jax.random.normal(k[2], (N_EXP * P_SLOT,), dtype=jnp.float32) * s, 'expert_w': jax.random.normal(k[3], (N_EXP, D_DIM, H), dtype=jnp.float32) * s, 'expert_b': jax.random.normal(k[4], (N_EXP, H), dtype=jnp.float32) * s}
    _L1_ffn_in = _L1_ffn_setup()
    _d = {'L0_attn_x': _L0_attn_in['x'], 'L0_attn_Wq': _L0_attn_in['Wq'], 'L0_attn_bq': _L0_attn_in['bq'], 'L0_attn_Wk': _L0_attn_in['Wk'], 'L0_attn_bk': _L0_attn_in['bk'], 'L0_attn_Wv': _L0_attn_in['Wv'], 'L0_attn_bv': _L0_attn_in['bv'], 'L0_attn_Wo': _L0_attn_in['Wo'], 'L0_attn_bo': _L0_attn_in['bo'], 'L0_ffn_rw1': _L0_ffn_in['rw1'], 'L0_ffn_rb1': _L0_ffn_in['rb1'], 'L0_ffn_rw2': _L0_ffn_in['rw2'], 'L0_ffn_rb2': _L0_ffn_in['rb2'], 'L0_ffn_W1': _L0_ffn_in['W1'], 'L0_ffn_b1': _L0_ffn_in['b1'], 'L0_ffn_W2': _L0_ffn_in['W2'], 'L0_ffn_b2': _L0_ffn_in['b2'], 'L1_attn_w_qkv': _L1_attn_in['w_qkv'], 'L1_attn_w_out': _L1_attn_in['w_out'], 'L1_attn_b_out': _L1_attn_in['b_out'], 'L1_attn_logit_scale': _L1_attn_in['logit_scale'], 'L1_ffn_phi_w': _L1_ffn_in['phi_w'], 'L1_ffn_phi_b': _L1_ffn_in['phi_b'], 'L1_ffn_expert_w': _L1_ffn_in['expert_w'], 'L1_ffn_expert_b': _L1_ffn_in['expert_b']}
    _x0 = _d['L0_attn_x']
    _d['L0_attn_x'] = jax.random.normal(jax.random.fold_in(jax.random.key(seed), 1), (16, 512, 128), dtype=_x0.dtype)
    del _x0
    return _d

def reference(L0_attn_x, L0_attn_Wq, L0_attn_bq, L0_attn_Wk, L0_attn_bk, L0_attn_Wv, L0_attn_bv, L0_attn_Wo, L0_attn_bo, L0_ffn_rw1, L0_ffn_rb1, L0_ffn_rw2, L0_ffn_rb2, L0_ffn_W1, L0_ffn_b1, L0_ffn_W2, L0_ffn_b2, L1_attn_w_qkv, L1_attn_w_out, L1_attn_b_out, L1_attn_logit_scale, L1_ffn_phi_w, L1_ffn_phi_b, L1_ffn_expert_w, L1_ffn_expert_b):

    def _L0_attn_ref(x, Wq, bq, Wk, bk, Wv, bv, Wo, bo):
        import jax, jax.numpy as jnp
        import numpy as np
        import math
        EMBED_DIM = 128
        NUM_HEADS = 16
        HEAD_DIM = EMBED_DIM // NUM_HEADS

        def alibi_slopes(num_heads: int) -> np.ndarray:

            def slopes_pow2(n):
                start = 2.0 ** (-2.0 ** (-(math.log2(n) - 3)))
                return [start * start ** i for i in range(n)]
            if math.log2(num_heads).is_integer():
                return np.array(slopes_pow2(num_heads), dtype=np.float32)
            closest = 2 ** math.floor(math.log2(num_heads))
            extra = slopes_pow2(2 * closest)[closest:]
            return np.array(slopes_pow2(closest) + extra[:num_heads - closest], dtype=np.float32)
        B, S, E = x.shape
        H, D = (NUM_HEADS, HEAD_DIM)
        q = (x @ Wq.T + bq).reshape(B, S, H, D).transpose(0, 2, 1, 3)
        k = (x @ Wk.T + bk).reshape(B, S, H, D).transpose(0, 2, 1, 3)
        v = (x @ Wv.T + bv).reshape(B, S, H, D).transpose(0, 2, 1, 3)
        slopes = jnp.asarray(alibi_slopes(H))
        pos = jnp.arange(S, dtype=jnp.float32)
        rel = jnp.abs(pos[None, :] - pos[:, None])
        bias = -slopes[:, None, None] * rel[None, :, :]
        scores = jnp.einsum('bhqd,bhkd->bhqk', q, k) / math.sqrt(D)
        scores = scores + bias[None]
        causal = jnp.tril(jnp.ones((S, S), dtype=bool))
        scores = jnp.where(causal[None, None], scores, -jnp.inf)
        probs = jax.nn.softmax(scores, axis=-1)
        out = jnp.einsum('bhqk,bhkd->bhqd', probs, v)
        out = out.transpose(0, 2, 1, 3).reshape(B, S, E)
        return out @ Wo.T + bo

    def _L0_ffn_ref(inputs, rw1, rb1, rw2, rb2, W1, b1, W2, b2):
        import jax, jax.numpy as jnp
        import numpy as np
        EMBED = 128
        D_FF = 4 * EMBED
        N_EXPERTS = 8
        TOP_K = 2
        B, S = (2, 128)
        Bb, Ss, D = inputs.shape
        T = Bb * Ss
        xf = inputs.reshape(T, D)
        score = jax.nn.relu(xf @ rw1 + rb1) @ rw2 + rb2
        _, topi = jax.lax.top_k(score, TOP_K)
        mask = jnp.zeros(score.shape, bool).at[jnp.arange(T)[:, None], topi].set(True)
        gate = jax.nn.softmax(jnp.where(mask, score, -jnp.inf), axis=-1)
        out = jnp.zeros_like(xf)
        for e in range(N_EXPERTS):
            h = jax.nn.relu(xf @ W1[e] + b1[e])
            y = h @ W2[e] + b2[e]
            out = out + gate[:, e:e + 1] * y
        return out.reshape(Bb, Ss, D)

    def _L1_attn_ref(x, w_qkv, w_out, b_out, logit_scale):
        import jax, jax.numpy as jnp
        import numpy as np
        B, N, DIM, H, DH = (2, 256, 128, 16, 64)
        INNER = H * DH
        EPS = 1e-12
        MAX_LOG_SCALE = np.log(1.0 / 0.01)
        b, n, dim = x.shape
        h = logit_scale.shape[0]
        qkv = x @ w_qkv
        q, k, v = jnp.split(qkv, 3, axis=-1)
        split_heads = lambda t: t.reshape(b, n, h, -1).transpose(0, 2, 1, 3)
        q, k, v = (split_heads(q), split_heads(k), split_heads(v))
        qn = q / jnp.maximum(jnp.linalg.norm(q, axis=-1, keepdims=True), EPS)
        kn = k / jnp.maximum(jnp.linalg.norm(k, axis=-1, keepdims=True), EPS)
        scale = jnp.exp(jnp.minimum(logit_scale, MAX_LOG_SCALE))
        cos_dots = jnp.einsum('bhid,bhjd->bhij', qn, kn) * scale
        attn = jax.nn.softmax(cos_dots, axis=-1)
        out = jnp.einsum('bhij,bhjd->bhid', attn, v)
        out = out.transpose(0, 2, 1, 3).reshape(b, n, -1)
        return out @ w_out + b_out

    def _L1_ffn_ref(x, phi_w, phi_b, expert_w, expert_b):
        import jax, jax.numpy as jnp
        import numpy as np
        T, Z, D_DIM = (8, 256, 128)
        N_EXP, P_SLOT, H = (64, 32, 128)
        LN_EPS = 1e-05
        t, z, d = x.shape
        n = expert_w.shape[0]
        p = phi_w.shape[0] // n
        logits = (jnp.einsum('tzd,ed->tze', x, phi_w) + phi_b).reshape(t, z, n, p)
        D = jax.nn.softmax(logits, axis=3)
        C = jax.nn.softmax(logits, axis=2)
        X_tilde = jnp.einsum('tznp,tzd->npd', D, x)
        X_tilde = jnp.clip(X_tilde, -33000.0, 65000.0)
        mu = jnp.mean(X_tilde, axis=-1, keepdims=True)
        var = jnp.mean(jnp.square(X_tilde - mu), axis=-1, keepdims=True)
        X_tilde = (X_tilde - mu) * jax.lax.rsqrt(var + LN_EPS)
        X_tilde = jnp.tanh(X_tilde)
        Y_tilde = jnp.einsum('npd,ndH->npH', X_tilde, expert_w) + expert_b[:, None, :]
        Y = jnp.einsum('tznp,npH->tzH', C, Y_tilde)
        return Y
    x = L0_attn_x
    x = x + _L0_attn_ref(_layernorm(x, axis=-1), L0_attn_Wq, L0_attn_bq, L0_attn_Wk, L0_attn_bk, L0_attn_Wv, L0_attn_bv, L0_attn_Wo, L0_attn_bo)
    x = x + _L0_ffn_ref(_layernorm(x, axis=-1), L0_ffn_rw1, L0_ffn_rb1, L0_ffn_rw2, L0_ffn_rb2, L0_ffn_W1, L0_ffn_b1, L0_ffn_W2, L0_ffn_b2)
    x = x + _L1_attn_ref(_layernorm(x, axis=-1), L1_attn_w_qkv, L1_attn_w_out, L1_attn_b_out, L1_attn_logit_scale)
    x = x + _L1_ffn_ref(_layernorm(x, axis=-1), L1_ffn_phi_w, L1_ffn_phi_b, L1_ffn_expert_w, L1_ffn_expert_b)
    return x

_drawn_inputs = setup_inputs


def setup_inputs(seed=0):
    import zlib

    import numpy as np

    out = dict(_drawn_inputs(seed))
    spreads = {'L0_ffn_rb1': (0.0, 0.1),
     'L0_ffn_rb2': (0.0, 0.1),
     'L0_ffn_b1': (0.0, 0.1),
     'L0_ffn_b2': (0.0, 0.1),
     'L1_attn_logit_scale': (2.3025851249694824, 0.2)}
    factors = {'L0_attn_bq': 4.44,
     'L0_attn_bk': 64.0,
     'L1_attn_b_out': 3.485,
     'L1_ffn_phi_w': 3.264,
     'L1_ffn_phi_b': 30.311}
    for name, (base, spread) in spreads.items():
        noise = np.random.default_rng([zlib.crc32(name.encode()), seed]).standard_normal(out[name].shape)
        drawn = base * np.exp(spread * noise) if base else spread * noise
        out[name] = jnp.asarray(drawn.astype(out[name].dtype))
    for name, factor in factors.items():
        out[name] = (out[name] * factor).astype(out[name].dtype)
    return out
```

```python
import math
from contextlib import ExitStack

import concourse.bass as bass
from concourse import mybir

ALU = mybir.AluOpType
ACT = mybir.ActivationFunctionType
AX = mybir.AxisListType
F32 = mybir.dt.float32
BF16 = mybir.dt.bfloat16
F16 = mybir.dt.float16
F32R = mybir.dt.float32r

P = 128
D = 128
BATCHES = 16
SEQ = 512
TILES = SEQ // P
HEADS = 16
LN_EPS = 1e-5

HD = D // HEADS
PARTS_Q = (0, 0, 0, 1, 1, 2)
PARTS_K = (0, 1, 2, 0, 1, 0)
ROW_ALIBI = len(PARTS_Q) * HD
ROW_MAX = ROW_ALIBI + 3
ROWS = ROW_MAX + 2
ST_AT = {0: 0, 1: 512, 3: 896, 2: 1024}
ST_COLS = 1280
VW = HD + 1
GROUP = 4
GROUPS = HEADS // GROUP
GW = P // GROUP
REPLICAS = len(PARTS_Q) + len(PARTS_K)
WEIGHT_LOADS = 11 + 1 + 4
FIRST_MAX_HEAD = 4
MAX_UNITS = [(qt, h, max(1, 4 // (qt + 1))) for qt in range(TILES) for h in range(0, HEADS, max(1, 4 // (qt + 1)))]


def order_of_work(front, back):
    units = iter(range(len(MAX_UNITS)))
    if not back:
        return [("max", u) for u in units]
    work = []
    for h in range(HEADS):
        work.append(("scores", h))
        if h % GROUP == 0 and h:
            work.append(("attend", h // GROUP - 1))
        if h % GROUP == 2 and h > GROUP:
            work.append(("turn", h // GROUP - 1))
        if front and h >= FIRST_MAX_HEAD:
            done, left = h + 1 - FIRST_MAX_HEAD, HEADS - FIRST_MAX_HEAD
            for _ in range(done * len(MAX_UNITS) // left - (done - 1) * len(MAX_UNITS) // left):
                work.append(("max", next(units)))
    return work + [("attend", GROUPS - 1), ("turn", GROUPS - 1)]


def above_zero(eng, sem, value):
    if not isinstance(value, int) or value > 0:
        eng.wait_ge(sem, value)


class Memory:

    def __init__(self, nc, ctx):
        self.nc, self.ctx, self.sems = nc, ctx, []
        ctx.callback(self.give_back_semaphores)

    def sb(self, name, shape, dt=F32):
        return self.ctx.enter_context(self.nc.sbuf_tensor(name, shape, dt))

    def ps(self, name, shape, dt=F32):
        return self.ctx.enter_context(self.nc.psum_tensor(name, shape, dt))

    def sem(self, name):
        self.sems.append(self.nc.alloc_semaphore(name))
        return self.sems[-1]

    def give_back_semaphores(self):
        if self.sems:
            self.nc.clear_and_free_semaphores(self.sems)
            self.nc.all_engine_barrier()


class LayerNorm:

    def __init__(self, mem, tag, tiles=TILES):
        self.tiles = tiles
        self.stats = mem.sb(f"{tag}_stats", [P, tiles, 6])
        self.mv = mem.sb(f"{tag}_mv", [P, tiles, 2])
        self.rstd = mem.sb(f"{tag}_rstd", [P, tiles])
        self.stats_ready = mem.sem(f"{tag}_stats_ready")
        self.mv_ready = mem.sem(f"{tag}_mv_ready")
        self.var = mem.sb(f"{tag}_var", [P, tiles])
        self.power = mem.sb(f"{tag}_power", [P, tiles])
        self.eps = mem.sb(f"{tag}_eps", [P, tiles])
        self.carrier = mem.sb(f"{tag}_carrier", [P, 1])
        self.power_ready = mem.sem(f"{tag}_power_ready")
        self.var_ready = mem.sem(f"{tag}_var_ready")
        self.rstd_ready = mem.sem(f"{tag}_rstd_ready")
        self.ready = mem.sem(f"{tag}_ready")

    def set_up(self, nc, pool):
        nc.gpsimd.memset(self.power[:, :], -0.5).then_inc(self.power_ready, 1)
        nc.gpsimd.memset(self.eps[:, :], LN_EPS).then_inc(self.power_ready, 1)
        pool.wait_ge(self.power_ready, 2)

    def take_rstd(self, nc, pool, b):
        pool.wait_ge(self.mv_ready, b + 1)
        nc.gpsimd.tensor_tensor(self.var[:, :], self.mv[:, :, 1], self.eps[:, :], ALU.add).then_inc(self.var_ready, 1)
        pool.wait_ge(self.var_ready, b + 1)
        nc.gpsimd.tensor_tensor(self.rstd[:, :], self.var[:, :], self.power[:, :], ALU.pow).then_inc(self.rstd_ready, 1)

    def run(self, nc, dve, rows, out, b):
        self.take_statistics(nc, dve, rows, b)
        self.normalise(nc, dve, rows, out, b)

    def take_statistics(self, nc, dve, rows, b):
        for t in range(self.tiles):
            last = nc.vector.bn_stats(self.stats[:, t, :], rows(t))
        last.then_inc(self.stats_ready, 1)
        dve.wait_ge(self.stats_ready, b + 1)
        nc.vector.tensor_copy(self.carrier[:, :], self.stats[:, 0, 0:1])
        for t in range(self.tiles):
            last = nc.vector.bn_aggr(self.mv[:, t, :], self.stats[:, t, :])
        last.then_inc(self.mv_ready, 1)

    def normalise(self, nc, dve, rows, out, b):
        dve.wait_ge(self.rstd_ready, b + 1)
        for t in range(self.tiles):
            last = nc.vector.tensor_scalar(out[:, t, :], rows(t), self.mv[:, t, 0:1], self.rstd[:, t:t + 1],
                                           ALU.subtract, ALU.mult)
        last.then_inc(self.ready, 1)


def stage_causal_attention(nc, X, ident, x_in, w, c):
    with ExitStack() as ctx:
        mem = Memory(nc, ctx)
        sb, ps, sem = mem.sb, mem.ps, mem.sem
        wq, wk, wo = (sb(n, [D, D]) for n in ("a_wq", "a_wk", "a_wo"))
        wv = sb("a_wv", [D, HEADS * VW])
        bq, bk = sb("a_bq", [P, 1]), sb("a_bk", [P, 1])
        bv = sb("a_bv", [P, HEADS * VW])
        bo = sb("a_bo", [1, D])
        ones = sb("a_ones", [1, P])
        identb = sb("a_identb", [P, P], BF16)
        mask_qk = sb("a_mask_qk", [P, P], BF16)
        mask_kq = sb("a_mask_kq", [P, P], BF16)
        xn = sb("a_xn", [P, TILES, D])
        xnT = sb("a_xnT", [D, SEQ])
        full = [sb(f"a_full_{n}", [P, SEQ]) for n in "qk"]
        rest = [sb(f"a_rest_{n}", [P, SEQ]) for n in "qk"]
        parts = [sb(f"a_parts_{n}", [P, 3, SEQ], BF16) for n in "qk"]
        heads_q = [sb(f"a_heads_q{i}", [ROWS, HEADS, SEQ], BF16) for i in range(2)]
        heads_k = [sb(f"a_heads_k{i}", [ROWS, HEADS, SEQ], BF16) for i in range(2)]
        parts_dram = nc.dram_tensor("a_parts_dram", [2, P, 3, SEQ], BF16).ap()
        v = sb("a_v", [P, TILES, HEADS * GW])
        neg_max = sb("a_neg_max", [P, TILES, HEADS])
        max_parts = sb("a_max_parts", [P, TILES, 2, HEADS], BF16)
        maxT = sb("a_maxT", [2 * HEADS, SEQ], BF16)
        probs = [sb(f"a_probs{i}", [P, GROUP, ST_COLS]) for i in range(2)]
        group_out = [sb(f"a_group_out{i}", [P, SEQ]) for i in range(2)]
        rsum = sb("a_rsum", [P, TILES, GROUP])
        heads_out = sb("a_heads_out", [P, TILES, D])
        outT = sb("a_outT", [D, SEQ])
        ps_st = ps("a_ps_st", [P, 3 * 512])
        ps_max = ps("a_ps_max", [P, 2, 512])
        ps_out = ps("a_ps_out", [P, 2, 512])
        ps_misc = ps("a_ps_misc", [P, 512])

        ln = LayerNorm(mem, "a_ln")
        x0_loaded, x_loaded, w_loaded = sem("a_x0_loaded"), sem("a_x_loaded"), sem("a_w_loaded")
        ones_ready = sem("a_ones_ready")
        xnT_made, xnT_ready = sem("a_xnT_made"), sem("a_xnT_ready")
        q_made, k_made = sem("a_q_made"), sem("a_k_made")
        made = [q_made, k_made]
        full_ready = [sem(f"a_full_{n}_ready") for n in "qk"]
        hi_ready = [sem(f"a_hi_{n}_ready") for n in "qk"]
        rest_ready = [sem(f"a_rest_{n}_ready") for n in "qk"]
        mid_ready = [sem(f"a_mid_{n}_ready") for n in "qk"]
        lo_ready = [sem(f"a_lo_{n}_ready") for n in "qk"]
        parts_stored = sem("a_parts_stored")
        heads_loaded = [sem(f"a_heads_loaded{i}") for i in range(2)]
        max_made, max_taken = sem("a_max_made"), sem("a_max_taken")
        max_hi_ready, max_parts_ready = sem("a_max_hi_ready"), sem("a_max_parts_ready")
        maxT_made, maxT_ready = sem("a_maxT_made"), sem("a_maxT_ready")
        max_rows_loaded = [sem(f"a_max_rows_loaded{i}") for i in range(2)]
        v_made, v_ready = sem("a_v_made"), sem("a_v_ready")
        st_a_made, st_b_made = sem("a_st_a_made"), sem("a_st_b_made")
        exp_a_done, exp_b_done = sem("a_exp_a_done"), sem("a_exp_b_done")
        av_done = sem("a_av_done")
        v_zeroed = sem("a_v_zeroed")
        group_out_ready, group_turned = sem("a_group_out_ready"), sem("a_group_turned")
        rsum_ready, heads_out_ready = sem("a_rsum_ready"), sem("a_heads_out_ready")
        outT_made, outT_ready = sem("a_outT_made"), sem("a_outT_ready")
        proj_made, x_added = sem("a_proj_made"), sem("a_x_added")

        loads = [(wq, w["wqT"]), (wk, w["wkT"]), (wo, w["woT"]), (wv, w["wvT"]), (bq, w["bq"]), (bk, w["bk"]),
                 (bo, w["bo"]), (identb, c["ident_bf16"]), (mask_qk, c["mask_qk"]), (mask_kq, c["mask_kq"]),
                 (ident, c["ident"])]
        x_view = x_in.rearrange("b (t p) d -> p (b t) d", p=P)

        with nc.Block() as block:

            def pipeline(eng, step):
                step(0, None, 0, 0, None)
                step(1, 0, 1, 0, 0)
                with eng.Fori(0, (BATCHES - 2) // 2) as i:
                    step(2 * i + 2, 2 * i + 1, 0, i + 1, i)
                    step(2 * i + 3, 2 * i + 2, 1, i + 1, i + 1)
                step(None, BATCHES - 1, 0, None, BATCHES // 2 - 1)

            @block.sync
            def _(sp):
                sp.dma_start(X[:, 0:TILES, :], x_view[:, 0:TILES, :]).then_inc(x0_loaded, 16)
                for dst, src in loads:
                    sp.dma_start(dst[:, :], src).then_inc(w_loaded, 16)
                sp.dma_start(bv[:, :], w["bv"].partition_broadcast(P)).then_inc(w_loaded, 16)
                for i in range(2):
                    sp.dma_start(heads_k[i][ROW_ALIBI:ROWS, :, :], c["rows_k"]).then_inc(w_loaded, 16)
                    sp.dma_start(heads_q[i][ROW_ALIBI:ROW_MAX, :, :], c["rows_q"]).then_inc(w_loaded, 16)
                sp.dma_start(X[:, TILES:, :], x_view[:, TILES:, :]).then_inc(x_loaded, 16)

                def step(b, bb, par, kb, kbb):
                    if bb is not None:
                        sp.wait_ge(maxT_ready, bb + 1)
                        for part in range(2):
                            sp.dma_start(heads_q[1 - par][ROW_MAX + part:ROW_MAX + part + 1, :, :],
                                         maxT[part * HEADS:(part + 1) * HEADS, :])\
                                .then_inc(max_rows_loaded[1 - par], 16)
                    if b is not None:
                        for n in range(2):
                            sp.wait_ge(lo_ready[n], b + 1)
                            sp.dma_start(parts_dram[n], parts[n][:, :, :]).then_inc(parts_stored, 16)
                        sp.wait_ge(parts_stored, 32 * (b + 1))
                        for n, which in enumerate((PARTS_Q, PARTS_K)):
                            dst = (heads_q, heads_k)[n][par]
                            for g, part in enumerate(which):
                                sp.dma_start(dst[g * HD:(g + 1) * HD, :, :],
                                             parts_dram[n, :, part, :].rearrange("(h d) t -> d h t", d=HD))\
                                    .then_inc(heads_loaded[par], 16)

                pipeline(sp, step)

            @block.gpsimd
            def _(pool):
                nc.gpsimd.memset(ones[:, :], 1.0).then_inc(ones_ready, 1)
                nc.gpsimd.memset(v[:, :, :], 0.0).then_inc(v_zeroed, 1)
                ln.set_up(nc, pool)

                def step(b, bb, par, kb, kbb):
                    if b is None:
                        return
                    ln.take_rstd(nc, pool, b)
                    for n in range(2):
                        pool.wait_ge(hi_ready[n], b + 1)
                        nc.gpsimd.tensor_tensor(rest[n][:, :], full[n][:, :], parts[n][:, 0, :], ALU.subtract)\
                            .then_inc(rest_ready[n], 1)
                    if bb is not None:
                        pool.wait_ge(heads_loaded[1 - par], 16 * REPLICAS * (kbb + 1))
                        above_zero(pool, av_done, GROUPS * bb)
                    for n in range(2):
                        pool.wait_ge(mid_ready[n], b + 1)
                        nc.gpsimd.tensor_tensor(parts[n][:, 2, :], rest[n][:, :], parts[n][:, 1, :], ALU.subtract)\
                            .then_inc(lo_ready[n], 1)

                pipeline(pool, step)

            @block.vector
            def _(dve):
                dve.wait_ge(x0_loaded, 16)
                dve.wait_ge(w_loaded, 16 * WEIGHT_LOADS)
                dve.wait_ge(v_zeroed, 1)

                def norm_group(b, j):
                    seen = GROUPS * b + j
                    dve.wait_ge(group_turned, seen + 1)
                    out = ps_misc[:, :].rearrange("p (t g c) -> p t g c", g=GROUP, c=GW)
                    nc.vector.reciprocal(rsum[:, :, :], out[:, :, :, HD]).then_inc(rsum_ready, 1)
                    dve.wait_ge(rsum_ready, seen + 1)
                    if j == 0:
                        above_zero(dve, outT_made, b)
                    dst = heads_out[:, :, j * GROUP * HD:(j + 1) * GROUP * HD].rearrange("p t (g d) -> p t g d", d=HD)
                    nc.vector.tensor_tensor(dst, out[:, :, :, 0:HD],
                                            rsum[:, :, :].unsqueeze(3).to_broadcast([P, TILES, GROUP, HD]),
                                            ALU.mult).then_inc(heads_out_ready, 1)

                def add_to_x(b):
                    dve.wait_ge(proj_made, b + 1)
                    rows = X[:, bass.ds(TILES * b, TILES), :]
                    nc.vector.tensor_tensor(rows, ps_misc[:, :].rearrange("p (t d) -> p t d", t=TILES), rows, ALU.add)\
                        .then_inc(x_added, 1)

                def step(b, bb, par, kb, kbb):
                    if bb is not None:
                        dve.wait_ge(max_taken, len(MAX_UNITS) * (bb + 1))
                        above_zero(dve, maxT_made, bb)
                        nc.vector.tensor_copy(max_parts[:, :, 0, :], neg_max[:, :, :]).then_inc(max_hi_ready, 1)
                        dve.wait_ge(max_hi_ready, bb + 1)
                        nc.vector.tensor_tensor(max_parts[:, :, 1, :], neg_max[:, :, :], max_parts[:, :, 0, :],
                                                ALU.subtract).then_inc(max_parts_ready, 1)
                    if b is not None:
                        if isinstance(b, int) and b == 1:
                            dve.wait_ge(x_loaded, 16)
                        above_zero(dve, xnT_made, b)
                        ln.run(nc, dve, lambda t: X[:, bass.ds(TILES * b + t, 1), :].rearrange("p o d -> p (o d)"), xn, b)
                    if bb is not None:
                        if not (isinstance(bb, int) and bb == 0):
                            add_to_x(bb - 1)
                        dve.wait_ge(v_made, bb + 1)
                        for half in range(2):
                            for t in range(2):
                                last = nc.vector.tensor_tensor(
                                    v[:, 2 * half + t, :].rearrange("p (h c) -> p h c", c=GW)[:, :, 0:VW],
                                    ps_out[:, half, t * HEADS * VW:(t + 1) * HEADS * VW].rearrange("p (h c) -> p h c", c=VW),
                                    bv[:, :].rearrange("p (h c) -> p h c", c=VW), ALU.add)
                        last.then_inc(v_ready, 1)
                    if b is not None:
                        for n, (bias, scale) in enumerate(((bq, HD ** -0.5), (bk, 1.0))):
                            dve.wait_ge(made[n], b + 1)
                            above_zero(dve, rest_ready[n], b)
                            nc.vector.tensor_scalar(full[n][:, :], ps_max[:, n, :], bias[:, 0:1], scale, ALU.add, ALU.mult)\
                                .then_inc(full_ready[n], 1)
                    for what, u in order_of_work(b is not None, bb is not None):
                        if what == "max":
                            qt, h, k = MAX_UNITS[u]
                            dve.wait_ge(max_made, len(MAX_UNITS) * b + u + 1)
                            cols = (qt + 1) * P
                            nc.vector.tensor_reduce(
                                neg_max[:, qt, h:h + k],
                                ps_max[:, u % 2, 0:k * cols].rearrange("p (h c) -> p h c", c=cols),
                                AX.X, ALU.max, negate=True).then_inc(max_taken, 1)
                        if what == "turn":
                            norm_group(bb, u)

                pipeline(dve, step)
                add_to_x(BATCHES - 1)

            @block.scalar
            def _(act):
                def group_to_sbuf(b, j):
                    seen = GROUPS * b + j
                    act.wait_ge(av_done, seen + 1)
                    above_zero(act, group_turned, seen - 1)
                    nc.scalar.activation(group_out[j % 2][:, :], ps_out[:, j % 2, :], ACT.Copy).then_inc(group_out_ready, 1)

                def outT_to_sbuf(b):
                    act.wait_ge(outT_made, b + 1)
                    above_zero(act, proj_made, b)
                    nc.scalar.activation(outT[:, :], ps_misc[:, :], ACT.Copy).then_inc(outT_ready, 1)

                def step(b, bb, par, kb, kbb):
                    if bb is not None:
                        act.wait_ge(maxT_made, bb + 1)
                        if not (isinstance(bb, int) and bb == 0):
                            act.wait_ge(max_rows_loaded[par], 32 * (kbb + 1 - par))
                        nc.scalar.activation(maxT[:, :], ps_misc[0:2 * HEADS, 0:SEQ // 2].bitcast(BF16), ACT.Copy)\
                            .then_inc(maxT_ready, 1)
                        if not (isinstance(bb, int) and bb == 0):
                            outT_to_sbuf(bb - 1)
                    if b is not None:
                        act.wait_ge(xnT_made, b + 1)
                        above_zero(act, k_made, b)
                        if bb is not None:
                            act.wait_ge(v_made, bb + 1)
                        nc.scalar.activation(xnT[:, :], ps_misc[:, :], ACT.Copy).then_inc(xnT_ready, 1)
                        for n in range(2):
                            act.wait_ge(full_ready[n], b + 1)
                            above_zero(act, parts_stored, 32 * b)
                            nc.scalar.activation(parts[n][:, 0, :], full[n][:, :], ACT.Copy).then_inc(hi_ready[n], 1)
                        for n in range(2):
                            act.wait_ge(rest_ready[n], b + 1)
                            nc.scalar.activation(parts[n][:, 1, :], rest[n][:, :], ACT.Copy).then_inc(mid_ready[n], 1)
                    if bb is not None:
                        for h in range(HEADS):
                            seen, j = HEADS * bb + h, h // GROUP
                            if h % GROUP == 0:
                                above_zero(act, av_done, GROUPS * bb + j - 1)
                            if h % GROUP == 2 and h > GROUP:
                                group_to_sbuf(bb, j - 1)
                            dst = probs[j % 2][:, h % GROUP, :]
                            act.wait_ge(st_a_made, seen + 1)
                            nc.scalar.activation(dst[:, 0:512], ps_st[:, 0:512], ACT.Exp).then_inc(exp_a_done, 1)
                            act.wait_ge(st_b_made, seen + 1)
                            nc.scalar.activation(dst[:, 512:ST_COLS], ps_st[:, 512:ST_COLS], ACT.Exp)\
                                .then_inc(exp_b_done, 1)
                        group_to_sbuf(bb, GROUPS - 1)

                pipeline(act, step)
                outT_to_sbuf(BATCHES - 1)

            @block.tensor
            def _(pe):
                mm = nc.tensor.matmul
                pe.wait_ge(w_loaded, 16 * WEIGHT_LOADS)
                pe.wait_ge(ones_ready, 1)
                pe.wait_ge(v_zeroed, 1)

                def project(b):
                    pe.wait_ge(heads_out_ready, GROUPS * (b + 1))
                    for t in range(TILES):
                        last = nc.tensor.transpose(ps_misc[:, t * P:(t + 1) * P], heads_out[:, t, :], ident[:, :])
                    last.then_inc(outT_made, 1)
                    pe.wait_ge(outT_ready, b + 1)
                    for t in range(TILES):
                        dst = ps_misc[:, t * D:(t + 1) * D]
                        mm(dst, outT[:, t * P:(t + 1) * P], wo[:, :], start=True, stop=False)
                        last = mm(dst, ones[0:1, :], bo[:, :], start=False, stop=True)
                    last.then_inc(proj_made, 1)

                def take_max(b, par, u):
                    qt, h0, k = MAX_UNITS[u]
                    cols = (qt + 1) * P
                    if u >= 2:
                        pe.wait_ge(max_taken, len(MAX_UNITS) * b + u - 1)
                    for j in range(k):
                        h, at = h0 + j, j * cols
                        mm(ps_max[:, u % 2, at:at + cols], heads_q[par][0:ROW_MAX, h, qt * P:(qt + 1) * P],
                           heads_k[par][0:ROW_MAX, h, 0:cols], start=True, stop=False)
                        last = mm(ps_max[:, u % 2, at + cols - P:at + cols], identb[:, :], mask_qk[:, :],
                                  start=False, stop=True)
                    last.then_inc(max_made, 1)

                def transposed_scores(bb, par, h):
                    seen = HEADS * bb + h
                    q, k = heads_q[par], heads_k[par]

                    def tile(kt):
                        at, cols = ST_AT[kt], SEQ - kt * P
                        mm(ps_st[:, at:at + cols], k[0:ROWS, h, kt * P:(kt + 1) * P], q[0:ROWS, h, kt * P:SEQ],
                           start=True, stop=False)
                        return mm(ps_st[:, at:at + P], identb[:, :], mask_kq[:, :], start=False, stop=True)

                    above_zero(pe, exp_a_done, seen)
                    tile(0).then_inc(st_a_made, 1)
                    above_zero(pe, exp_b_done, seen)
                    tile(1)
                    tile(3)
                    tile(2).then_inc(st_b_made, 1)

                def attend(bb, j):
                    seen = GROUPS * bb + j
                    pe.wait_ge(exp_a_done, HEADS * bb + (j + 1) * GROUP)
                    pe.wait_ge(exp_b_done, HEADS * bb + (j + 1) * GROUP)
                    above_zero(pe, group_out_ready, seen - 1)
                    for kt in range(TILES):
                        for g in range(GROUP):
                            h = j * GROUP + g
                            last = mm(ps_out[g * GW:(g + 1) * GW, j % 2, kt * P:SEQ], v[:, kt, h * GW:(h + 1) * GW],
                                      probs[j % 2][:, g, ST_AT[kt]:ST_AT[kt] + SEQ - kt * P],
                                      start=(kt == 0), stop=(kt == TILES - 1))
                    last.then_inc(av_done, 1)

                def turn(bb, j):
                    seen = GROUPS * bb + j
                    pe.wait_ge(group_out_ready, seen + 1)
                    above_zero(pe, heads_out_ready, seen)
                    for t in range(TILES):
                        last = nc.tensor.transpose(ps_misc[:, t * P:(t + 1) * P], group_out[j % 2][:, t * P:(t + 1) * P],
                                                   ident[:, :])
                    last.then_inc(group_turned, 1)

                def step(b, bb, par, kb, kbb):
                    if bb is not None:
                        pe.wait_ge(max_parts_ready, bb + 1)
                        pe.wait_ge(xnT_ready, bb + 1)
                        above_zero(pe, heads_out_ready, GROUPS * bb)
                        for t in range(TILES):
                            last = nc.tensor.transpose(
                                ps_misc[0:2 * HEADS, t * P // 2:(t + 1) * P // 2].bitcast(BF16),
                                max_parts[:, t, :, :].rearrange("p a h -> p (a h)"), identb[:, :])
                        last.then_inc(maxT_made, 1)
                        pe.wait_ge(maxT_ready, bb + 1)
                        if not (isinstance(bb, int) and bb == 0):
                            project(bb - 1)
                        above_zero(pe, group_out_ready, GROUPS * bb)
                        for t in range(TILES):
                            at = (t % 2) * HEADS * VW
                            last = mm(ps_out[:, t // 2, at:at + HEADS * VW], xnT[:, t * P:(t + 1) * P], wv[:, :],
                                      start=True, stop=True)
                        last.then_inc(v_made, 1)
                    if b is not None:
                        pe.wait_ge(ln.ready, b + 1)
                        if bb is not None:
                            above_zero(pe, x_added, bb)
                        for t in range(TILES):
                            last = nc.tensor.transpose(ps_misc[:, t * P:(t + 1) * P], xn[:, t, :], ident[:, :])
                        last.then_inc(xnT_made, 1)
                        pe.wait_ge(xnT_ready, b + 1)
                        above_zero(pe, max_taken, len(MAX_UNITS) * b)
                        mm(ps_max[:, 0, :], wq[:, :], xnT[:, :], start=True, stop=True).then_inc(q_made, 1)
                        mm(ps_max[:, 1, :], wk[:, :], xnT[:, :], start=True, stop=True).then_inc(k_made, 1)
                    if bb is not None:
                        pe.wait_ge(v_ready, bb + 1)
                        pe.wait_ge(max_rows_loaded[1 - par], 32 * (kbb + 1))
                    for what, n in order_of_work(b is not None, bb is not None):
                        if what == "scores":
                            transposed_scores(bb, 1 - par, n)
                        elif what == "attend":
                            attend(bb, n)
                        elif what == "turn":
                            turn(bb, n)
                        else:
                            if n == 0:
                                operands_there(b, par, kb)
                            take_max(b, par, n)

                def operands_there(b, par, kb):
                    pe.wait_ge(heads_loaded[par], 16 * REPLICAS * (kb + 1))
                    for n in range(2):
                        pe.wait_ge(full_ready[n], b + 1)

                pipeline(pe, step)
                project(BATCHES - 1)


EXPERTS = 8
FF = 512
FF_TILES = FF // P
UNITS = 1 + EXPERTS
HIDDEN_RING = 3
ACT_TILES = 3
TOP_K = 2


def stage_experts(nc, X, ident, w, c):
    with ExitStack() as ctx:
        mem = Memory(nc, ctx)
        sb, ps, sem = mem.sb, mem.ps, mem.sem
        w1 = [sb(f"b_w1{n}", [D, UNITS, FF], F32R) for n in ("_high", "_low")]
        w1_in = sb("b_w1_in", [D, UNITS, FF])
        b1 = sb("b_b1", [P, UNITS, FF_TILES])
        w2 = sb("b_w2", [P, EXPERTS, FF_TILES, D])
        b2 = sb("b_b2", [EXPERTS, D])
        rw2 = sb("b_rw2", [P, FF_TILES, EXPERTS])
        rb2 = sb("b_rb2", [1, EXPERTS])
        earlier = sb("b_earlier", [P, EXPERTS, EXPERTS])
        ones = sb("b_ones", [1, P])
        xn = sb("b_xn", [P, TILES, D])
        xnT = [sb(f"b_xnT{n}", [D, SEQ], F32R) for n in ("_high", "_low")]
        hidden = [sb(f"b_hidden{i}", [P, FF_TILES, SEQ]) for i in range(HIDDEN_RING)]
        score = sb("b_score", [P, TILES, EXPERTS])
        above = sb("b_above", [P, TILES, EXPERTS, EXPERTS])
        tied = sb("b_tied", [P, TILES, EXPERTS, EXPERTS])
        rank = sb("b_rank", [P, TILES, EXPERTS])
        best = sb("b_best", [P, TILES])
        shifted = sb("b_shifted", [P, TILES, EXPERTS])
        expd = sb("b_expd", [P, TILES, EXPERTS])
        chosen = sb("b_chosen", [P, TILES, EXPERTS])
        total = sb("b_total", [P, TILES])
        gate = sb("b_gate", [P, TILES, EXPERTS])
        gateT = sb("b_gateT", [EXPERTS, SEQ])

        ps_hidden = ps("b_ps_hidden", [P, FF_TILES, 512])
        ps_y = ps("b_ps_y", [P, 2, 512])
        ps_rows = ps("b_ps_rows", [P, 512])
        ps_score = ps("b_ps_score", [P, 512])

        ln = LayerNorm(mem, "b_ln")
        w_loaded, ones_ready = sem("b_w_loaded"), sem("b_ones_ready")
        router_loaded, w1_loaded = sem("b_router_loaded"), sem("b_w1_loaded")
        w_high_ready, w_ready = sem("b_w_high_ready"), sem("b_w_ready")
        xnT_made, xnT_high_ready, xnT_ready = sem("b_xnT_made"), sem("b_xnT_high_ready"), sem("b_xnT_ready")
        hidden_made = sem("b_hidden_made")
        act_rectified, dve_rectified = sem("b_act_rectified"), sem("b_dve_rectified")
        unit_done = sem("b_unit_done")
        score_ready, compared, ties_broken, rank_ready = (
            sem("b_score_ready"), sem("b_compared"), sem("b_ties_broken"), sem("b_rank_ready"))
        ties_broken_added = sem("b_ties_broken_added")
        best_ready, shifted_ready, exp_done = sem("b_best_ready"), sem("b_shifted_ready"), sem("b_exp_done")
        chosen_ready, total_ready, inverse_ready, gate_ready = (
            sem("b_chosen_ready"), sem("b_total_ready"), sem("b_inverse_ready"), sem("b_gate_ready"))
        gateT_made, gateT_ready, bias_made = sem("b_gateT_made"), sem("b_gateT_ready"), sem("b_bias_made")
        added = sem("b_added")
        ADDS = EXPERTS + 1

        router_loads = [(w1_in[:, 0, :], w["rw1"]), (b1[:, :, :], w["b1"])]
        loads = [(w2[:, :, :, :].rearrange("p e f d -> p (e f) d"), w["W2"].rearrange("e (f p) d -> p (e f) d", p=P)),
                 (b2[:, :], w["b2"]), (rw2[:, :, :], w["rw2"].rearrange("(f p) e -> p f e", p=P)), (rb2[:, :], w["rb2"]),
                 (earlier[:, :, :], c["earlier"].partition_broadcast(P))]

        BIAS_AFTER, ROWS_AFTER = 2, 4

        with nc.Block() as block:

            @block.sync
            def _(sp):
                for dst, src in router_loads:
                    sp.dma_start(dst, src).then_inc(router_loaded, 16)
                sp.dma_start(w1_in[:, 1:, :], w["W1"].rearrange("e d f -> d e f")).then_inc(w1_loaded, 16)
                for dst, src in loads:
                    sp.dma_start(dst, src).then_inc(w_loaded, 16)

            @block.gpsimd
            def _(pool):
                nc.gpsimd.memset(ones[:, :], 1.0).then_inc(ones_ready, 1)
                ln.set_up(nc, pool)
                ln.take_rstd(nc, pool, 0)
                with pool.Fori(1, BATCHES) as b:
                    ln.take_rstd(nc, pool, b)

            @block.vector
            def _(dve):
                def rows(b):
                    return lambda t: X[:, bass.ds(TILES * b + t, 1), :].rearrange("p o d -> p (o d)")

                def rectify(b, u):
                    above_zero(dve, unit_done, UNITS * b + u - 2)
                    for f in range(ACT_TILES, FF_TILES):
                        dve.wait_ge(hidden_made, FF_TILES * (UNITS * b + u) + f + 1)
                        nc.vector.tensor_scalar(hidden[u % HIDDEN_RING][:, f, :], ps_hidden[:, f, :], b1[:, u, f:f + 1],
                                                0.0, ALU.add, ALU.max).then_inc(dve_rectified, 1)

                def take_gate(b):
                    shape = [P, TILES, EXPERTS, EXPERTS]
                    dve.wait_ge(unit_done, UNITS * b + 1)
                    nc.vector.tensor_copy(score[:, :, :],
                                          ps_score[:, 0:TILES * EXPERTS].rearrange("p (t e) -> p t e", t=TILES))\
                        .then_inc(score_ready, 1)
                    dve.wait_ge(score_ready, b + 1)
                    other = score[:, :, :].unsqueeze(2).to_broadcast(shape)
                    own = score[:, :, :].unsqueeze(3).to_broadcast(shape)
                    nc.vector.tensor_tensor(above[:, :, :, :], other, own, ALU.is_gt)
                    nc.vector.tensor_tensor(tied[:, :, :, :], other, own, ALU.is_equal).then_inc(compared, 1)
                    nc.vector.tensor_reduce(best[:, :], score[:, :, :], AX.X, ALU.max).then_inc(best_ready, 1)
                    if isinstance(b, int) and b == 0:
                        dve.wait_ge(w_loaded, 16 * len(loads))
                    dve.wait_ge(compared, b + 1)
                    nc.vector.tensor_tensor(tied[:, :, :, :], tied[:, :, :, :],
                                            earlier[:, :, :].unsqueeze(1).to_broadcast(shape), ALU.mult)\
                        .then_inc(ties_broken, 1)
                    dve.wait_ge(best_ready, b + 1)
                    nc.vector.tensor_tensor(shifted[:, :, :], score[:, :, :],
                                            best[:, :].unsqueeze(2).to_broadcast([P, TILES, EXPERTS]),
                                            ALU.subtract).then_inc(shifted_ready, 1)
                    dve.wait_ge(ties_broken, b + 1)
                    nc.vector.tensor_tensor(above[:, :, :, :], above[:, :, :, :], tied[:, :, :, :], ALU.add)\
                        .then_inc(ties_broken_added, 1)
                    dve.wait_ge(ties_broken_added, b + 1)
                    nc.vector.tensor_reduce(rank[:, :, :], above[:, :, :, :], AX.X, ALU.add).then_inc(rank_ready, 1)
                    dve.wait_ge(rank_ready, b + 1)
                    dve.wait_ge(exp_done, b + 1)
                    nc.vector.scalar_tensor_tensor(chosen[:, :, :], rank[:, :, :], TOP_K - 0.5, expd[:, :, :],
                                                   ALU.is_lt, ALU.mult).then_inc(chosen_ready, 1)
                    dve.wait_ge(chosen_ready, b + 1)
                    nc.vector.tensor_reduce(total[:, :], chosen[:, :, :], AX.X, ALU.add).then_inc(total_ready, 1)
                    dve.wait_ge(total_ready, b + 1)
                    nc.vector.reciprocal(total[:, :], total[:, :]).then_inc(inverse_ready, 1)
                    dve.wait_ge(inverse_ready, b + 1)
                    above_zero(dve, gateT_made, b)
                    nc.vector.tensor_tensor(gate[:, :, :], chosen[:, :, :],
                                            total[:, :].unsqueeze(2).to_broadcast([P, TILES, EXPERTS]), ALU.mult)\
                        .then_inc(gate_ready, 1)

                def add_expert(b, e):
                    if e == 0:
                        dve.wait_ge(gate_ready, b + 1)
                    dve.wait_ge(unit_done, UNITS * b + e + 2)
                    above_zero(dve, added, ADDS * b + e + (1 if e > BIAS_AFTER else 0))
                    for t in range(TILES):
                        x = rows(b)(t)
                        last = nc.vector.scalar_tensor_tensor(x, ps_y[:, e % 2, t * D:(t + 1) * D], gate[:, t, e:e + 1],
                                                              x, ALU.mult, ALU.add)
                    last.then_inc(added, 1)

                def add_bias(b):
                    dve.wait_ge(bias_made, b + 1)
                    dve.wait_ge(added, ADDS * b + BIAS_AFTER + 1)
                    x = X[:, bass.ds(TILES * b, TILES), :]
                    nc.vector.tensor_tensor(x, ps_rows[:, :].rearrange("p (t d) -> p t d", t=TILES), x, ALU.add)\
                        .then_inc(added, 1)

                def batch(b, last):
                    rectify(b, 0)
                    rectify(b, 1)
                    take_gate(b)
                    for e in range(EXPERTS):
                        if e + 2 < UNITS:
                            rectify(b, e + 2)
                        add_expert(b, e)
                        if e == BIAS_AFTER:
                            add_bias(b)
                        if e == ROWS_AFTER and not last:
                            dve.wait_ge(xnT_made, b + 1)
                            ln.run(nc, dve, rows(b + 1), xn, b + 1)
                    if not last:
                        rows_rest(b + 1)

                def rows_rest(b):
                    dve.wait_ge(xnT_high_ready, b + 1)
                    nc.vector.tensor_tensor(xnT[1][:, :], ps_rows[:, :], xnT[0][:, :], ALU.subtract).then_inc(xnT_ready, 1)

                ln.run(nc, dve, rows(0), xn, 0)
                rows_rest(0)
                dve.wait_ge(router_loaded, 16 * len(router_loads))
                for u in range(UNITS):
                    if u == 1:
                        dve.wait_ge(w1_loaded, 16)
                    nc.vector.tensor_copy(w1[0][:, u, :], w1_in[:, u, :]).then_inc(w_high_ready, 1)
                    dve.wait_ge(w_high_ready, u + 1)
                    nc.vector.tensor_tensor(w1[1][:, u, :], w1_in[:, u, :], w1[0][:, u, :], ALU.subtract).then_inc(w_ready, 1)
                batch(0, False)
                with dve.Fori(1, BATCHES - 1) as b:
                    batch(b, False)
                batch(BATCHES - 1, True)

            @block.scalar
            def _(act):
                def rectify(b, u):
                    above_zero(act, unit_done, UNITS * b + u - 2)
                    for f in range(ACT_TILES):
                        act.wait_ge(hidden_made, FF_TILES * (UNITS * b + u) + f + 1)
                        nc.scalar.activation(hidden[u % HIDDEN_RING][:, f, :], ps_hidden[:, f, :], ACT.Relu,
                                             bias=b1[:, u, f:f + 1]).then_inc(act_rectified, 1)

                def rows_to_sbuf(b):
                    act.wait_ge(xnT_made, b + 1)
                    above_zero(act, hidden_made, FF_TILES * UNITS * b)
                    nc.scalar.activation(xnT[0][:, :], ps_rows[:, :], ACT.Copy).then_inc(xnT_high_ready, 1)

                def batch(b, last):
                    rectify(b, 0)
                    rectify(b, 1)
                    act.wait_ge(shifted_ready, b + 1)
                    nc.scalar.activation(expd[:, :, :], shifted[:, :, :], ACT.Exp).then_inc(exp_done, 1)
                    for u in range(2, UNITS):
                        rectify(b, u)
                        if u == BIAS_AFTER + 2:
                            act.wait_ge(gateT_made, b + 1)
                            nc.scalar.activation(gateT[:, :], ps_rows[0:EXPERTS, :], ACT.Copy).then_inc(gateT_ready, 1)
                    if not last:
                        rows_to_sbuf(b + 1)

                rows_to_sbuf(0)
                act.wait_ge(router_loaded, 16 * len(router_loads))
                batch(0, False)
                with act.Fori(1, BATCHES - 1) as b:
                    batch(b, False)
                batch(BATCHES - 1, True)

            @block.tensor
            def _(pe):
                mm = nc.tensor.matmul

                def turn_rows(b):
                    pe.wait_ge(ln.ready, b + 1)
                    above_zero(pe, added, ADDS * (b - 1) + BIAS_AFTER + 2 if not isinstance(b, int) or b else 0)
                    for t in range(TILES):
                        last = nc.tensor.transpose(ps_rows[:, t * P:(t + 1) * P], xn[:, t, :], ident[:, :])
                    last.then_inc(xnT_made, 1)

                def first_layer(b, u):
                    if isinstance(b, int) and b == 0:
                        pe.wait_ge(w_ready, u + 1)
                    for f in range(FF_TILES):
                        if f < ACT_TILES:
                            above_zero(pe, act_rectified, ACT_TILES * (UNITS * b + u - 1) + f + 1 if not (isinstance(b, int) and b == 0 and u == 0) else 0)
                        else:
                            above_zero(pe, dve_rectified, (FF_TILES - ACT_TILES) * (UNITS * b + u - 1) + f - ACT_TILES + 1)
                        left = [part[:, u, f * P:(f + 1) * P] for part in w1]
                        mm(ps_hidden[:, f, :], left[0], xnT[0][:, :], start=True, stop=False)
                        mm(ps_hidden[:, f, :], left[0], xnT[1][:, :], start=False, stop=False)
                        mm(ps_hidden[:, f, :], left[1], xnT[0][:, :], start=False, stop=True).then_inc(hidden_made, 1)

                def second_layer(b, u):
                    pe.wait_ge(act_rectified, ACT_TILES * (UNITS * b + u + 1))
                    pe.wait_ge(dve_rectified, (FF_TILES - ACT_TILES) * (UNITS * b + u + 1))
                    h, e = hidden[u % HIDDEN_RING], u - 1
                    if u == 0:
                        above_zero(pe, score_ready, b)
                    else:
                        if e >= 2:
                            above_zero(pe, added, ADDS * b + e - 1 + (1 if e - 2 > BIAS_AFTER else 0))
                        else:
                            above_zero(pe, added, ADDS * b)
                    for t in range(TILES):
                        for f in range(FF_TILES):
                            if u == 0:
                                mm(ps_score[:, t * EXPERTS:(t + 1) * EXPERTS], h[:, f, t * P:(t + 1) * P], rw2[:, f, :],
                                   start=(f == 0), stop=False)
                            else:
                                last = mm(ps_y[:, e % 2, t * D:(t + 1) * D], h[:, f, t * P:(t + 1) * P], w2[:, e, f, :],
                                          start=(f == 0), stop=(f == FF_TILES - 1))
                        if u == 0:
                            last = mm(ps_score[:, t * EXPERTS:(t + 1) * EXPERTS], ones[:, :], rb2[:, :],
                                      start=False, stop=True)
                    last.then_inc(unit_done, 1)

                def gated_bias(b):
                    pe.wait_ge(gate_ready, b + 1)
                    for t in range(TILES):
                        last = nc.tensor.transpose(ps_rows[0:EXPERTS, t * P:(t + 1) * P], gate[:, t, :], ident[:, :])
                    last.then_inc(gateT_made, 1)
                    pe.wait_ge(gateT_ready, b + 1)
                    for t in range(TILES):
                        last = mm(ps_rows[:, t * D:(t + 1) * D], gateT[:, t * P:(t + 1) * P], b2[:, :], start=True, stop=True)
                    last.then_inc(bias_made, 1)

                def batch(b, last):
                    pe.wait_ge(xnT_ready, b + 1)
                    first_layer(b, 0)
                    for u in range(1, UNITS):
                        first_layer(b, u)
                        if isinstance(b, int) and b == 0 and u == 1:
                            pe.wait_ge(w_loaded, 16 * len(loads))
                        if u == UNITS - 1 and not last:
                            turn_rows(b + 1)
                        second_layer(b, u - 1)
                        if u - 2 == BIAS_AFTER:
                            gated_bias(b)
                    second_layer(b, UNITS - 1)

                pe.wait_ge(ones_ready, 1)
                turn_rows(0)
                batch(0, False)
                with pe.Fori(1, BATCHES - 1) as b:
                    batch(b, False)
                batch(BATCHES - 1, True)


CHEADS = 16
CHD = 64
CINNER = CHEADS * CHD
PAIR_TILES = CINNER // P
NORM_FLOOR = 1e-12
MAX_SCALE = 100.0
LOG_MAX_SCALE = math.log(MAX_SCALE)
EXP_ROOM = 75.0
BANK_HEADS = 512 // CHD
BANK_PAIRS = 512 // P
RAWS = 4
QK_TILES = 2 * PAIR_TILES
QK_BANKS = 2 * CINNER // 512
V_BANKS = TILES * CINNER // 512
VC = CHD + 1
STEPS = CHEADS
LEAD = 2
UNIT = 256.0
STATISTICS_STEP = 7
NORMALISE_STEP = 9
TURN_STEP = STEPS - LEAD - 1


def stage_cosine_attention(nc, X, ident, w, c):
    with ExitStack() as ctx:
        mem = Memory(nc, ctx)
        sb, ps, sem = mem.sb, mem.ps, mem.sem
        w_qk = [sb(f"c_w_qk{n}", [D, 2 * CINNER], F32R) for n in ("_high", "_low")]
        w_v = [sb(f"c_w_v{n}", [D, CINNER], F32R) for n in ("_high", "_low")]
        w_out = sb("c_w_out", [VC, CHEADS, D + 1])
        b_out = sb("c_b_out", [P, D])
        log_scale = sb("c_log_scale", [P, CHEADS])
        scale = sb("c_scale", [P, CHEADS])
        unit_scale = sb("c_unit_scale", [P, CHEADS])
        shift = sb("c_shift", [P, CHEADS])
        xn = sb("c_xn", [P, TILES, D])
        xnT = [[sb(f"c_xnT{i}{n}", [D, SEQ], F32R) for n in ("_high", "_low")] for i in range(2)]
        raw = [sb(f"c_raw{i}", [P, SEQ]) for i in range(RAWS)]
        square = [sb(f"c_square{i}", [P, SEQ]) for i in range(2)]
        norm2 = [sb(f"c_norm2{i}", [P, BANK_HEADS]) for i in range(2)]
        power = sb("c_power", [P, BANK_HEADS])
        inverse = [sb(f"c_inverse{i}", [P, BANK_HEADS]) for i in range(2)]
        keys = [sb(f"c_keys{i}", [P, PAIR_TILES, 2, SEQ], F16) for i in range(2)]
        queries = [sb(f"c_queries{i}", [P, PAIR_TILES, 2, SEQ], F16) for i in range(2)]
        queries_low = [sb(f"c_queries_low{i}", [P, PAIR_TILES, SEQ], F16) for i in range(2)]
        v = sb("c_v", [P, TILES, CHEADS, VC])
        probs = [sb(f"c_probs{i}", [P, TILES, SEQ]) for i in range(2)]
        w_qk_in, w_v_in = probs[0][:, :, :].rearrange("p t k -> p (t k)"), probs[1][:, 0:2, :].rearrange("p t k -> p (t k)")
        outT = [sb(f"c_outT{i}", [VC, SEQ]) for i in range(2)]
        rsum = sb("c_rsum", [P, 2])

        ps_scores = ps("c_ps_scores", [P, TILES, 512])
        ps_out = ps("c_ps_out", [P, 512])
        ps_front = ps("c_ps_front", [P, 512])
        ps_y = ps("c_ps_y", [P, 2, 512])

        ln = LayerNorm(mem, "c_ln")
        w_loaded, set_up = sem("c_w_loaded"), sem("c_set_up")
        w_high_ready, w_ready = sem("c_w_high_ready"), sem("c_w_ready")
        xnT_high_ready, qkT_high_ready = sem("c_xnT_high_ready"), sem("c_qkT_high_ready")
        queries_doubled = sem("c_queries_doubled")
        limited, scale_ready, shifted, shift_ready = sem("c_limited"), sem("c_scale_ready"), sem("c_shifted"), sem("c_shift_ready")
        xnT_made, xnT_ready, bias_added = sem("c_xnT_made"), sem("c_xnT_ready"), sem("c_bias_added")
        tile_made, raw_ready, square_ready = sem("c_tile_made"), sem("c_raw_ready"), sem("c_square_ready")
        norm2_ready, limited_ready, inverse_ready, unit_ready, turned, qkT_ready = (
            sem("c_norm2_ready"), sem("c_limited_ready"), sem("c_inverse_ready"), sem("c_unit_ready"), sem("c_turned"), sem("c_qkT_ready"))
        v_made, v_ready = sem("c_v_made"), sem("c_v_ready")
        scores_made, exp_done = sem("c_scores_made"), sem("c_exp_done")
        out_made, outT_ready = sem("c_out_made"), sem("c_outT_ready")
        act_outT_ready = sem("c_act_outT_ready")
        y_made, rsum_ready, y_added = sem("c_y_made"), sem("c_rsum_ready"), sem("c_y_added")

        loads = [(w_qk_in, w["qkv"][:, 0:2 * CINNER]), (w_v_in, w["qkv"][:, 2 * CINNER:]),
                 (w_out[:, :, :], w["out"]), (b_out[:, :], w["b_out"].partition_broadcast(P)),
                 (log_scale[:, :], w["log_scale"].partition_broadcast(P))]

        ROWS_OF = (slice(0, CHD), slice(CHD, P))

        def place(i):
            t, g = i // QK_BANKS, i % QK_BANKS
            is_key, g = g >= QK_BANKS // 2, g % (QK_BANKS // 2)
            return slice(g * BANK_PAIRS, (g + 1) * BANK_PAIRS), slice(t * P, (t + 1) * P), is_key

        def values_piece(front, back, s):
            half = 1 if s < STEPS // 2 else 0
            b = back if half else front
            if s % 2 == 0 or b is None:
                return None
            t = s % (STEPS // 2) // 2
            return b, t, half, V_BANKS * b + TILES * half + t

        def pipeline(eng, step):
            step(0, None, None, None, 1)
            step(1, 0, None, None, 0)
            step(2, 1, 0, None, 1)
            with eng.Fori(0, (BATCHES - 4) // 2) as i:
                step(2 * i + 3, 2 * i + 2, 2 * i + 1, 2 * i, 0)
                step(2 * i + 4, 2 * i + 3, 2 * i + 2, 2 * i + 1, 1)
            step(BATCHES - 1, BATCHES - 2, BATCHES - 3, BATCHES - 4, 0)
            step(None, BATCHES - 1, BATCHES - 2, BATCHES - 3, 1)
            step(None, None, BATCHES - 1, BATCHES - 2, 0)
            step(None, None, None, BATCHES - 1, 1)

        def piece(after, front, i):
            b, i = (front, i) if i < QK_TILES else (after, i - QK_TILES)
            return None if b is None else (b, i, QK_TILES * b + i)

        def head(back, old, h):
            b, h = (back, h) if h >= 0 else (old, h + CHEADS)
            return None if b is None else (b, h, CHEADS * b + h)

        with nc.Block() as block:

            @block.sync
            def _(sp):
                for dst, src in loads:
                    sp.dma_start(dst, src).then_inc(w_loaded, 16)

            @block.gpsimd
            def _(pool):
                nc.gpsimd.memset(power[:, :], -0.5).then_inc(set_up, 1)
                nc.gpsimd.memset(v[:, :, :, CHD:VC], 1.0).then_inc(set_up, 1)
                ln.set_up(nc, pool)
                pool.wait_ge(set_up, 2)
                pool.wait_ge(w_loaded, 16 * len(loads))

                def add_bias(b):
                    pool.wait_ge(ln.ready, b + 1)
                    x = X[:, bass.ds(TILES * b, TILES), :]
                    nc.gpsimd.tensor_tensor(x, x, b_out[:, :].unsqueeze(1).to_broadcast([P, TILES, D]), ALU.add)\
                        .then_inc(bias_added, 1)

                def step(after, b, bb, old, par):
                    for s in range(STEPS):
                        if after is not None and s == STATISTICS_STEP:
                            ln.take_rstd(nc, pool, after)
                        if after is not None and s == NORMALISE_STEP + 1:
                            add_bias(after)
                        made, summed = piece(after, b, s + LEAD), piece(after, b, s + 1)
                        if made:
                            _, i, seen = made
                            pool.wait_ge(raw_ready, seen + 1)
                            above_zero(pool, norm2_ready, seen - 1)
                            nc.gpsimd.tensor_tensor(square[i % 2][:, :], raw[i % RAWS][:, :],
                                                    raw[i % RAWS][:, :], ALU.mult).then_inc(square_ready, 1)
                        if summed:
                            _, i, seen = summed
                            pool.wait_ge(limited_ready, seen + 1)
                            above_zero(pool, unit_ready, seen - 1)
                            nc.gpsimd.tensor_tensor(inverse[i % 2][:, :], norm2[i % 2][:, :], power[:, :], ALU.pow)\
                                .then_inc(inverse_ready, 1)

                pipeline(pool, step)

            @block.vector
            def _(dve):
                def rows_of(b):
                    return lambda t: X[:, bass.ds(TILES * b + t, 1), :].rearrange("p o d -> p (o d)")

                def step(after, b, bb, old, par):
                    for s in range(STEPS):
                        done, summed = head(bb, old, s - 2), piece(after, b, s + 1)
                        if summed:
                            square_sum(*summed)
                        if b is not None:
                            unit_length(b, s)
                        if done:
                            add_head(*done, 0)
                            add_head(*done, 1)
                        if b is not None:
                            piece_to_sbuf(b, par, s)
                        if done:
                            add_head(*done, 2)
                            add_head(*done, 3)
                        if s % 2 == 0 and head(bb, old, s - 1):
                            head_to_sbuf(*head(bb, old, s - 1))
                        if after is not None and s == STATISTICS_STEP:
                            ln.take_statistics(nc, dve, rows_of(after), after)
                        if after is not None and s == NORMALISE_STEP:
                            above_zero(dve, xnT_made, after)
                            ln.normalise(nc, dve, rows_of(after), xn, after)
                        if after is not None and s == TURN_STEP:
                            low, high = xnT[1 - par][1], xnT[1 - par][0]
                            dve.wait_ge(xnT_high_ready, after + 1)
                            nc.vector.tensor_tensor(low[:, :], ps_front[:, :], high[:, :], ALU.subtract).then_inc(xnT_ready, 1)

                def square_sum(b, i, seen):
                    dve.wait_ge(square_ready, seen + 1)
                    above_zero(dve, inverse_ready, seen - 1)
                    nc.vector.tensor_reduce(norm2[i % 2][:, :], square[i % 2][:, :].rearrange("p (h d) -> p h d", d=CHD),
                                            AX.X, ALU.add).then_inc(norm2_ready, 1)
                    dve.wait_ge(norm2_ready, seen + 1)
                    nc.vector.tensor_scalar(norm2[i % 2][:, :], norm2[i % 2][:, :], NORM_FLOOR ** 2, UNIT ** -2, ALU.max, ALU.mult)\
                        .then_inc(limited_ready, 1)

                def unit_length(b, i):
                    dve.wait_ge(inverse_ready, QK_TILES * b + i + 1)
                    rows = raw[i % RAWS][:, :].rearrange("p (h d) -> p h d", d=CHD)
                    nc.vector.tensor_tensor(rows, rows, inverse[i % 2][:, :].unsqueeze(2).to_broadcast([P, BANK_HEADS, CHD]),
                                            ALU.mult).then_inc(unit_ready, 1)

                def piece_to_sbuf(b, par, i):
                    pairs, tokens, is_key = place(i)
                    whole = ps_front[:, :].rearrange("p (j t) -> p j t", j=BANK_PAIRS)
                    high = (keys if is_key else queries)[par]
                    dve.wait_ge(qkT_high_ready, QK_TILES * b + i + 1)
                    for odd in range(2):
                        own, other = ROWS_OF[odd], ROWS_OF[1 - odd]
                        low = keys[par][other, pairs, odd, tokens] if is_key else queries_low[par][own, pairs, tokens]
                        last = nc.vector.tensor_tensor(low, whole[own, :, :], high[own, pairs, odd, tokens], ALU.subtract)
                    last.then_inc(qkT_ready, 1)
                    if not is_key:
                        for odd in range(2):
                            last = nc.vector.tensor_copy(high[ROWS_OF[1 - odd], pairs, odd, tokens],
                                                         high[ROWS_OF[odd], pairs, odd, tokens])
                        last.then_inc(queries_doubled, 1)

                def add_head(b, h, number, t):
                    seen = TILES * number + t
                    if h == 0 and t == 0:
                        dve.wait_ge(bias_added, b + 1)
                    dve.wait_ge(y_made, seen + 1)
                    nc.vector.reciprocal(rsum[:, t % 2:t % 2 + 1], ps_y[:, t % 2, D:D + 1]).then_inc(rsum_ready, 1)
                    dve.wait_ge(rsum_ready, seen + 1)
                    x = X[:, bass.ds(TILES * b + t, 1), :].rearrange("p o d -> p (o d)")
                    above_zero(dve, y_added, seen - TILES + 1)
                    nc.vector.scalar_tensor_tensor(x, ps_y[:, t % 2, 0:D], rsum[:, t % 2:t % 2 + 1], x, ALU.mult, ALU.add)\
                        .then_inc(y_added, 1)

                def head_to_sbuf(b, h, number):
                    dve.wait_ge(out_made, number + 1)
                    above_zero(dve, y_made, TILES * (number - 1))
                    nc.vector.tensor_copy(outT[h % 2][:, :], ps_out[0:VC, :]).then_inc(outT_ready, 1)

                dve.wait_ge(w_loaded, 16 * len(loads))
                for i, (part, whole) in enumerate(((w_qk, w_qk_in), (w_v, w_v_in))):
                    nc.vector.tensor_copy(part[0][:, :], whole).then_inc(w_high_ready, 1)
                    dve.wait_ge(w_high_ready, i + 1)
                    nc.vector.tensor_tensor(part[1][:, :], whole, part[0][:, :], ALU.subtract).then_inc(w_ready, 1)
                nc.vector.tensor_scalar(log_scale[:, :], log_scale[:, :], LOG_MAX_SCALE, None, ALU.min).then_inc(limited, 1)
                dve.wait_ge(scale_ready, 1)
                nc.vector.tensor_scalar(unit_scale[:, :], scale[:, :], UNIT ** -2, None, ALU.mult).then_inc(shifted, 1)
                nc.vector.tensor_scalar(shift[:, :], scale[:, :], -1.0, EXP_ROOM, ALU.mult, ALU.add).then_inc(shifted, 1)
                dve.wait_ge(shifted, 2)
                nc.vector.tensor_scalar(shift[:, :], shift[:, :], 0.0, None, ALU.min).then_inc(shift_ready, 1)
                pipeline(dve, step)

            @block.scalar
            def _(act):
                act.wait_ge(limited, 1)
                nc.scalar.activation(scale[:, :], log_scale[:, :], ACT.Exp).then_inc(scale_ready, 1)
                act.wait_ge(scale_ready, 1)
                act.wait_ge(shift_ready, 1)
                act.wait_ge(w_ready, 2)

                def piece_to_sbuf(b, par, i):
                    pairs, tokens, is_key = place(i)
                    whole = ps_front[:, :].rearrange("p (j t) -> p j t", j=BANK_PAIRS)
                    high = (keys if is_key else queries)[par]
                    act.wait_ge(turned, QK_TILES * b + i + 1)
                    for odd in range(2):
                        own = ROWS_OF[odd]
                        last = nc.scalar.activation(high[own, pairs, odd, tokens], whole[own, :, :], ACT.Copy)
                    last.then_inc(qkT_high_ready, 1)

                def exponentials(bb, h, half):
                    act.wait_ge(scores_made, 2 * (CHEADS * bb + h) + half + 1)
                    above_zero(act, out_made, CHEADS * bb + h - 1)
                    nc.scalar.activation(probs[h % 2][:, 2 * half:2 * half + 2, :], ps_scores[:, 2 * half:2 * half + 2, :],
                                         ACT.Exp, bias=shift[:, h:h + 1], scale=unit_scale[:, h:h + 1]).then_inc(exp_done, 1)

                def step(after, b, bb, old, par):
                    for s in range(STEPS):
                        made = piece(after, b, s + LEAD)
                        if bb is not None:
                            exponentials(bb, s, 0)
                        if made:
                            _, i, seen = made
                            act.wait_ge(tile_made, seen + 1)
                            above_zero(act, turned, seen - RAWS + 1)
                            nc.scalar.activation(raw[i % RAWS][:, :], ps_front[:, :], ACT.Copy).then_inc(raw_ready, 1)
                        if bb is not None:
                            exponentials(bb, s, 1)
                        if b is not None:
                            piece_to_sbuf(b, par, s)
                        if bb is not None and s % 2 == 1:
                            seen = CHEADS * bb + s - 1
                            act.wait_ge(out_made, seen + 1)
                            above_zero(act, y_made, TILES * (seen - 1))
                            nc.scalar.activation(outT[(s - 1) % 2][:, :], ps_out[0:VC, :], ACT.Copy).then_inc(act_outT_ready, 1)
                        values = values_piece(b, bb, s)
                        if values:
                            _, t, half, seen = values
                            act.wait_ge(v_made, seen + 1)
                            if half:
                                above_zero(act, out_made, CHEADS * bb)
                            elif bb is not None:
                                act.wait_ge(out_made, CHEADS * bb + CHEADS // 2)
                            heads = slice(half * BANK_HEADS, (half + 1) * BANK_HEADS)
                            nc.scalar.activation(v[:, t, heads, 0:CHD], ps_front[:, :].rearrange("p (h d) -> p h d", d=CHD),
                                                 ACT.Copy).then_inc(v_ready, 1)
                        if after is not None and s == TURN_STEP:
                            act.wait_ge(xnT_made, after + 1)
                            nc.scalar.activation(xnT[1 - par][0][:, :], ps_front[:, :], ACT.Copy).then_inc(xnT_high_ready, 1)

                pipeline(act, step)

            @block.tensor
            def _(pe):
                mm = nc.tensor.matmul
                pe.wait_ge(w_loaded, 16 * len(loads))
                pe.wait_ge(set_up, 2)
                pe.wait_ge(w_ready, 2)

                def in_parts(out, left, right):
                    mm(out, left[0], right[0], start=True, stop=False)
                    mm(out, left[0], right[1], start=False, stop=False)
                    return mm(out, left[1], right[0], start=False, stop=True)

                def scores(bb, par, h, half):
                    own, pair, odd = ROWS_OF[h % 2], h // 2, h % 2
                    above_zero(pe, exp_done, 2 * (CHEADS * bb + h) + half - 1)
                    for kt in range(2 * half, 2 * half + 2):
                        key, out = keys[par][:, pair, odd, kt * P:(kt + 1) * P], ps_scores[:, kt, :]
                        mm(out, key, queries[par][:, pair, odd, :], start=True, stop=False)
                        last = mm(out, keys[par][own, pair, odd, kt * P:(kt + 1) * P], queries_low[par][own, pair, :],
                                  start=False, stop=True)
                    last.then_inc(scores_made, 1)

                def attend(bb, h):
                    pe.wait_ge(exp_done, 2 * (CHEADS * bb + h + 1))
                    if h % BANK_HEADS == 0:
                        pe.wait_ge(v_ready, V_BANKS * bb + TILES * (h // BANK_HEADS + 1))
                    head_there(bb, h - 1)
                    for kt in range(TILES):
                        last = mm(ps_out[0:VC, :], v[:, kt, h, :], probs[h % 2][:, kt, :],
                                  start=(kt == 0), stop=(kt == TILES - 1))
                    last.then_inc(out_made, 1)

                def head_there(bb, h):
                    half = CHEADS // 2
                    if h < 0:
                        above_zero(pe, outT_ready, half * bb)
                    elif h % 2:
                        pe.wait_ge(outT_ready, half * bb + h // 2 + 1)
                    else:
                        pe.wait_ge(act_outT_ready, half * bb + h // 2 + 1)

                def project(bb, h, number, t):
                    seen = TILES * number + t
                    if t == 0:
                        head_there(bb, h)
                    above_zero(pe, y_added, seen - 1)
                    mm(ps_y[:, t % 2, 0:D + 1], outT[h % 2][:, t * P:(t + 1) * P], w_out[:, h, :], start=True, stop=True)\
                        .then_inc(y_made, 1)

                def after_odd_step(b, bb, s):
                    before = values_piece(b, bb, s - 1)
                    if before:
                        pe.wait_ge(v_ready, before[3] + 1)
                    else:
                        pe.wait_ge(qkT_ready, QK_TILES * b + s)

                def make_piece(after, b, bb, par, s):
                    owner, i, _ = piece(after, b, s + LEAD)
                    source = xnT[par] if owner is b else xnT[1 - par]
                    if s == 0:
                        pe.wait_ge(raw_ready, QK_TILES * b + LEAD)
                        if bb is not None:
                            pe.wait_ge(v_ready, V_BANKS * bb + TILES)
                    elif s == TURN_STEP + 1:
                        pe.wait_ge(xnT_ready, after + 1)
                    elif b is None:
                        pe.wait_ge(raw_ready, QK_TILES * after + i)
                    elif s % 2 == 0:
                        after_odd_step(b, bb, s)
                    else:
                        pe.wait_ge(qkT_ready, QK_TILES * b + s)
                    t, g = i // QK_BANKS, i % QK_BANKS
                    in_parts(ps_front[:, :], [part[:, t * P:(t + 1) * P] for part in source],
                             [part[:, g * 512:(g + 1) * 512] for part in w_qk]).then_inc(tile_made, 1)

                def turn_piece(after, b, bb, s):
                    pe.wait_ge(unit_ready, QK_TILES * b + s + 1)
                    if piece(after, b, s + LEAD):
                        pe.wait_ge(raw_ready, QK_TILES * b + s + LEAD + 1)
                    elif s % 2 == 0:
                        after_odd_step(b, bb, s)
                    else:
                        pe.wait_ge(qkT_ready, QK_TILES * b + s)
                    for j in range(BANK_PAIRS):
                        last = nc.tensor.transpose(ps_front[:, j * P:(j + 1) * P], raw[s % RAWS][:, j * P:(j + 1) * P], ident[:, :])
                    last.then_inc(turned, 1)

                def step(after, b, bb, old, par):
                    for s in range(STEPS):
                        projected, attended = head(bb, old, s - 2), head(bb, old, s - 1)
                        if bb is not None and s == 0:
                            pe.wait_ge(qkT_ready, QK_TILES * (bb + 1))
                            pe.wait_ge(queries_doubled, QK_TILES // 2 * (bb + 1))
                        if bb is not None:
                            scores(bb, 1 - par, s, 0)
                        if piece(after, b, s + LEAD):
                            make_piece(after, b, bb, par, s)
                        if projected:
                            project(*projected, 0)
                        if bb is not None:
                            scores(bb, 1 - par, s, 1)
                        if projected:
                            project(*projected, 1)
                        if b is not None:
                            turn_piece(after, b, bb, s)
                        if projected:
                            project(*projected, 2)
                        if attended:
                            attend(attended[0], attended[1])
                        if projected:
                            project(*projected, 3)
                        values = values_piece(b, bb, s)
                        if values:
                            _, t, half, _ = values
                            source = xnT[1 - par if half else par]
                            if b is not None:
                                pe.wait_ge(qkT_ready, QK_TILES * b + s + 1)
                            elif s > 1:
                                pe.wait_ge(v_ready, V_BANKS * bb + TILES + t)
                            in_parts(ps_front[:, :], [part[:, t * P:(t + 1) * P] for part in source],
                                     [part[:, half * 512:(half + 1) * 512] for part in w_v]).then_inc(v_made, 1)
                        if after is not None and s == TURN_STEP:
                            pe.wait_ge(ln.ready, after + 1)
                            if b is not None:
                                pe.wait_ge(v_ready, values[3] + 1)
                            for t in range(TILES):
                                last = nc.tensor.transpose(ps_front[:, t * P:(t + 1) * P], xn[:, t, :], ident[:, :])
                            last.then_inc(xnT_made, 1)

                pipeline(pe, step)


SEXPERTS = 64
SLOTS = 32
ALL_SLOTS = SEXPERTS * SLOTS
SLOT_TILES = ALL_SLOTS // P
TILE_EXPERTS = P // SLOTS
ROW_TILES = BATCHES * TILES
HALF = ALL_SLOTS // 2
BANK = 512
BANKS = ALL_SLOTS // BANK
BANK_TILES = BANK // P
SLOT_LOW, SLOT_HIGH = -33000.0, 65000.0


def stage_slots(nc, X, ident, w, c, out):
    with ExitStack() as whole:
        mem = Memory(nc, whole)
        sb, ps, sem = mem.sb, mem.ps, mem.sem
        phiT = [sb(f"d_phiT{n}", [D, ALL_SLOTS], F32R) for n in ("_high", "_low")]
        bias = sb("d_bias", [3, ALL_SLOTS], BF16)
        ones = sb("d_ones", [3, P], BF16)
        xnT = sb("d_xnT", [D, ROW_TILES * P])
        rowsT = [[sb(f"d_rowsT{i}{n}", [D, P], F32R) for n in ("_high", "_low")] for i in range(3)]
        expd = [sb(f"d_expd{i}", [P, ALL_SLOTS]) for i in range(2)]
        slot_out = sb("d_slot_out", [P, SLOT_TILES, D])
        bias_row, bias_rest = expd[0][0:1, :], expd[1][0:1, :]
        peak = sb("d_peak", [P, 2, SEXPERTS // 2])
        total = sb("d_total", [P, 2, SEXPERTS // 2])
        w_loaded, experts_loaded = sem("d_w_loaded"), sem("d_experts_loaded")
        bias_split, bias_loaded = sem("d_bias_split"), sem("d_bias_loaded")
        ones_ready = sem("d_ones_ready")

        def logits(mm, ps_logits, rows, bank):
            cols = slice(bank * BANK, (bank + 1) * BANK)
            mm(ps_logits[:, cols], rows[0][:, :], phiT[0][:, cols], start=True, stop=False)
            mm(ps_logits[:, cols], rows[0][:, :], phiT[1][:, cols], start=False, stop=False)
            mm(ps_logits[:, cols], rows[1][:, :], phiT[0][:, cols], start=False, stop=False)
            return mm(ps_logits[:, cols], ones[:, :], bias[:, cols], start=False, stop=True)

        def tiles_in_pairs(eng, step, lag):
            for n in range(4):
                step(n, n % 2)
            with eng.Fori(2, ROW_TILES // 2 - 1) as i:
                step(2 * i, 0)
                step(2 * i + 1, 1)
            for n in range(ROW_TILES - 2, ROW_TILES + lag):
                step(n, n % 2)

        def tiles_in_threes(eng, step, lag):
            for n in range(4):
                step(n, n % 3)
            with eng.Fori(0, (ROW_TILES - 7) // 3) as i:
                for j in range(4, 7):
                    step(3 * i + j, j % 3)
            for n in range(ROW_TILES - 3, ROW_TILES + lag):
                step(n, n % 3)

        def rows_rest(pool, sems, n, i):
            high_ready, ready = sems
            pool.wait_ge(high_ready, n + 1)
            nc.gpsimd.tensor_tensor(rowsT[i][1][:, :], xnT[:, bass.ds(P * n, P)], rowsT[i][0][:, :], ALU.subtract)\
                .then_inc(ready, 1)

        def there(n):
            return not isinstance(n, int) or 0 <= n < ROW_TILES

        with ExitStack() as ctx:
            mem = Memory(nc, ctx)
            sb, ps, sem = mem.sb, mem.ps, mem.sem
            xn_all = sb("d_xn_all", [P, ROW_TILES, D])
            expert_w = sb("d_expert_w", [D, SEXPERTS, D])
            expert_b = sb("d_expert_b", [P, SLOT_TILES, D])
            zeros = sb("d_zeros", [P, BANK], BF16)
            slots = sb("d_slots", [P, SLOT_TILES, D])
            expd3 = [*expd, sb("d_expd2", [P, ALL_SLOTS])]
            phiT_in = expd3[2]
            stats = sb("d_slot_stats", [P, SLOT_TILES, 6])
            mv = sb("d_slot_mv", [P, SLOT_TILES, 2])
            var = sb("d_slot_var", [P, SLOT_TILES])
            power = sb("d_slot_power", [P, 2, SLOT_TILES])
            rstd = sb("d_slot_rstd", [P, SLOT_TILES])
            first_parts = slot_out[0:1, :, :].rearrange("p s d -> p (s d)").bitcast(BF16)
            bias_parts = [first_parts[:, 0:ALL_SLOTS], first_parts[:, ALL_SLOTS:2 * ALL_SLOTS],
                          slots[0:1, :, :].rearrange("p s d -> p (s d)").bitcast(BF16)[:, 0:ALL_SLOTS]]
            ps_logits = ps("d_ps_logits", [P, ALL_SLOTS])
            ps_slots = ps("d_ps_slots", [P, SLOT_TILES, D])

            LN_GROUPS = 4
            GROUP_BATCHES = BATCHES // LN_GROUPS
            ln = LayerNorm(mem, "d_ln", GROUP_BATCHES * TILES)
            xnT_made, xnT_ready = sem("d_xnT_made"), sem("d_xnT_ready")
            zeros_ready, rowsT_high_ready, rowsT_ready = sem("d_zeros_ready"), sem("d_rowsT_high_ready"), sem("d_rowsT_ready")
            phiT_high_ready, phiT_ready = sem("d_phiT_high_ready"), sem("d_phiT_ready")
            logits_made, peak_ready, shifted, exp_done = (
                sem("d_logits_made"), sem("d_peak_ready"), sem("d_shifted"), sem("d_exp_done"))
            total_ready, inverse_ready, weights_ready, mixed = (
                sem("d_total_ready"), sem("d_inverse_ready"), sem("d_weights_ready"), sem("d_mixed"))
            slots_made = sem("d_slots_made")
            clipped, slot_stats, slot_mv, slot_var, slot_rstd, slot_normed, slot_tanh = (
                sem(f"d_{n}") for n in ("clipped", "slot_stats_ready", "slot_mv_ready", "slot_var_ready", "slot_rstd_ready",
                                        "slot_normed", "slot_tanh"))
            slotsT_made, slotsT_ready, experts_made, slot_out_ready = (
                sem(f"d_{n}") for n in ("slotsT_made", "slotsT_ready", "experts_made", "slot_out_ready"))
            slotsT = expd[0]

            loads = [(phiT_in[:, :], w["phiT"]), (bias_row, w["phi_b"])]

            with nc.Block() as block:

                @block.sync
                def _(sp):
                    for dst, src in loads:
                        sp.dma_start(dst, src).then_inc(w_loaded, 16)
                    sp.wait_ge(bias_split, 5)
                    for part in range(3):
                        sp.dma_start(bias[part:part + 1, :], bias_parts[part]).then_inc(bias_loaded, 16)
                    for j in range(TILE_EXPERTS):
                        src = w["expert_b"].rearrange("(s j) h -> j s h", j=TILE_EXPERTS)[j]
                        sp.dma_start(expert_b[j * SLOTS:(j + 1) * SLOTS, :, :], src.partition_broadcast(SLOTS))\
                            .then_inc(experts_loaded, 16)
                    sp.dma_start(expert_w[:, :, :], w["expert_w"].rearrange("n d h -> d n h")).then_inc(experts_loaded, 16)

                @block.gpsimd
                def _(pool):
                    nc.gpsimd.memset(ones[:, :], 1.0).then_inc(ones_ready, 1)
                    nc.gpsimd.memset(zeros[:, :], 0.0).then_inc(zeros_ready, 1)
                    nc.gpsimd.memset(power[:, 0, :], -0.5).then_inc(ones_ready, 1)
                    nc.gpsimd.memset(power[:, 1, :], LN_EPS).then_inc(ones_ready, 1)
                    ln.set_up(nc, pool)
                    ln.take_rstd(nc, pool, 0)
                    pool.wait_ge(phiT_high_ready, 1)
                    nc.gpsimd.tensor_tensor(phiT[1][:, :], phiT_in[:, :], phiT[0][:, :], ALU.subtract).then_inc(phiT_ready, 1)
                    pool.wait_ge(bias_split, 1)
                    nc.gpsimd.tensor_tensor(bias_rest, bias_row, bias_parts[0], ALU.subtract).then_inc(bias_split, 1)
                    ln.take_rstd(nc, pool, 1)
                    pool.wait_ge(bias_split, 3)
                    nc.gpsimd.tensor_tensor(bias_row, bias_rest, bias_parts[1], ALU.subtract).then_inc(bias_split, 1)
                    for g in range(2, LN_GROUPS):
                        ln.take_rstd(nc, pool, g)

                    rest = (rowsT_high_ready, rowsT_ready)
                    rows_rest(pool, rest, 0, 0)
                    rows_rest(pool, rest, 1, 1)

                    def step(n, buf):
                        for half in range(2):
                            pool.wait_ge(exp_done, 2 * n + half + 1)
                            pool.wait_ge(inverse_ready, 2 * n + half + 1)
                            e = expd3[buf][:, half * HALF:(half + 1) * HALF].rearrange("p (e s) -> p e s", s=SLOTS)
                            nc.gpsimd.tensor_tensor(e, e, total[:, half, :].unsqueeze(2).to_broadcast([P, SEXPERTS // 2, SLOTS]),
                                                    ALU.mult).then_inc(weights_ready, 1)
                            if half == 0 and there(n + 2 if isinstance(n, int) else n):
                                rows_rest(pool, rest, n + 2, (buf + 2) % 3)

                    tiles_in_threes(pool, step, 0)
                    pool.wait_ge(slot_mv, 1)
                    nc.gpsimd.tensor_tensor(var[:, :], mv[:, :, 1], power[:, 1, :], ALU.add).then_inc(slot_var, 1)
                    pool.wait_ge(slot_var, 1)
                    nc.gpsimd.tensor_tensor(rstd[:, :], var[:, :], power[:, 0, :], ALU.pow).then_inc(slot_rstd, 1)

                @block.vector
                def _(dve):
                    for g in range(LN_GROUPS):
                        first = ln.tiles * g
                        ln.run(nc, dve, lambda t: X[:, first + t, :], xn_all[:, first:first + ln.tiles, :], g)
                    dve.wait_ge(bias_split, 5)
                    dve.wait_ge(bias_loaded, 48)

                    def shift(n, buf, half):
                        seen = 2 * n + half
                        cols = slice(half * HALF, (half + 1) * HALF)
                        experts = ps_logits[:, cols].rearrange("p (e s) -> p e s", s=SLOTS)
                        dve.wait_ge(logits_made, seen + 1)
                        nc.vector.tensor_reduce(peak[:, half, :], experts, AX.X, ALU.max).then_inc(peak_ready, 1)
                        dve.wait_ge(peak_ready, seen + 1)
                        above_zero(dve, mixed, n - 2)
                        nc.vector.tensor_tensor(expd3[buf][:, cols].rearrange("p (e s) -> p e s", s=SLOTS), experts,
                                                peak[:, half, :].unsqueeze(2).to_broadcast([P, SEXPERTS // 2, SLOTS]),
                                                ALU.subtract).then_inc(shifted, 1)

                    def invert(n, buf, half):
                        seen = 2 * n + half
                        dve.wait_ge(exp_done, seen + 1)
                        above_zero(dve, weights_ready, seen - 1)
                        e = expd3[buf][:, half * HALF:(half + 1) * HALF].rearrange("p (e s) -> p e s", s=SLOTS)
                        nc.vector.tensor_reduce(total[:, half, :], e, AX.X, ALU.add).then_inc(total_ready, 1)
                        dve.wait_ge(total_ready, seen + 1)
                        nc.vector.reciprocal(total[:, half, :], total[:, half, :]).then_inc(inverse_ready, 1)

                    def step(n, buf):
                        if there(n):
                            shift(n, buf, 0)
                        if there(n - 1 if isinstance(n, int) else n):
                            invert(n - 1, (buf + 2) % 3, 1)
                        if there(n):
                            shift(n, buf, 1)
                            invert(n, buf, 0)

                    tiles_in_threes(dve, step, 1)

                    dve.wait_ge(slots_made, 1)
                    nc.vector.tensor_scalar(slots[:, :, :], ps_slots[:, :, :], SLOT_LOW, SLOT_HIGH, ALU.max, ALU.min).then_inc(clipped, 1)
                    dve.wait_ge(clipped, 1)
                    for s in range(SLOT_TILES):
                        last = nc.vector.bn_stats(stats[:, s, :], slots[:, s, :])
                    last.then_inc(slot_stats, 1)
                    dve.wait_ge(slot_stats, 1)
                    for s in range(SLOT_TILES):
                        last = nc.vector.bn_aggr(mv[:, s, :], stats[:, s, :])
                    last.then_inc(slot_mv, 1)
                    dve.wait_ge(slot_rstd, 1)
                    for s in range(SLOT_TILES):
                        last = nc.vector.tensor_scalar(slots[:, s, :], slots[:, s, :], mv[:, s, 0:1], rstd[:, s:s + 1],
                                                       ALU.subtract, ALU.mult)
                    last.then_inc(slot_normed, 1)
                    dve.wait_ge(experts_loaded, 16 * (TILE_EXPERTS + 1))
                    for bank in range(BANKS):
                        tiles = slice(bank * BANK_TILES, (bank + 1) * BANK_TILES)
                        dve.wait_ge(experts_made, bank + 1)
                        last = nc.vector.tensor_tensor(slot_out[:, tiles, :], ps_slots[:, tiles, :], expert_b[:, tiles, :], ALU.add)
                    last.then_inc(slot_out_ready, 1)

                @block.scalar
                def _(act):
                    act.wait_ge(w_loaded, 16 * len(loads))
                    nc.scalar.activation(phiT[0][:, :], phiT_in[:, :], ACT.Copy).then_inc(phiT_high_ready, 1)
                    nc.scalar.activation(bias_parts[0], bias_row, ACT.Copy).then_inc(bias_split, 1)
                    for b in range(BATCHES):
                        act.wait_ge(xnT_made, b + 1)
                        nc.scalar.activation(xnT[:, SEQ * b:SEQ * (b + 1)], ps_logits[:, b % BANKS * BANK:(b % BANKS + 1) * BANK],
                                             ACT.Copy).then_inc(xnT_ready, 1)
                        if b == GROUP_BATCHES - 1:
                            act.wait_ge(bias_split, 2)
                            nc.scalar.activation(bias_parts[1], bias_rest, ACT.Copy).then_inc(bias_split, 1)
                        if b == 2 * GROUP_BATCHES - 1:
                            act.wait_ge(bias_split, 4)
                            nc.scalar.activation(bias_parts[2], bias_row, ACT.Copy).then_inc(bias_split, 1)
                    act.wait_ge(xnT_ready, BATCHES)

                    act.wait_ge(phiT_ready, 1)

                    def fetch(n, buf):
                        above_zero(act, logits_made, 2 * (n - 2))
                        nc.scalar.activation(rowsT[buf][0][:, :], xnT[:, bass.ds(P * n, P)], ACT.Copy).then_inc(rowsT_high_ready, 1)

                    def step(n, buf):
                        for half in range(2):
                            cols = slice(half * HALF, (half + 1) * HALF)
                            act.wait_ge(shifted, 2 * n + half + 1)
                            nc.scalar.activation(expd3[buf][:, cols], expd3[buf][:, cols], ACT.Exp).then_inc(exp_done, 1)
                            if half == 0 and there(n + 2 if isinstance(n, int) else n):
                                fetch(n + 2, (buf + 2) % 3)

                    fetch(0, 0)
                    fetch(1, 1)
                    tiles_in_threes(act, step, 0)

                    act.wait_ge(slot_normed, 1)
                    nc.scalar.activation(slots[:, :, :], slots[:, :, :], ACT.Tanh).then_inc(slot_tanh, 1)
                    act.wait_ge(slotsT_made, 1)
                    nc.scalar.activation(slotsT[:, :], ps_logits[:, :], ACT.Copy).then_inc(slotsT_ready, 1)

                @block.tensor
                def _(pe):
                    mm = nc.tensor.matmul

                    for b in range(BATCHES):
                        pe.wait_ge(ln.ready, b // GROUP_BATCHES + 1)
                        above_zero(pe, xnT_ready, b - BANKS + 1)
                        for t in range(TILES):
                            at = b % BANKS * BANK + t * P
                            last = nc.tensor.transpose(ps_logits[:, at:at + P], xn_all[:, TILES * b + t, :], ident[:, :])
                        last.then_inc(xnT_made, 1)
                    pe.wait_ge(xnT_ready, BATCHES)
                    pe.wait_ge(bias_loaded, 48)
                    pe.wait_ge(phiT_ready, 1)
                    pe.wait_ge(ones_ready, 3)
                    pe.wait_ge(zeros_ready, 1)

                    def all_slots_plus_nothing(start, stop):
                        for bank in range(BANKS):
                            last = mm(ps_slots[:, bank * BANK_TILES:(bank + 1) * BANK_TILES, :].rearrange("p s d -> p (s d)"),
                                      zeros[:, 0:P], zeros[:, :], start=start, stop=stop)
                        return last

                    all_slots_plus_nothing(True, False)

                    def step(n, buf):
                        m = n - 2
                        for half in range(2):
                            if there(n):
                                pe.wait_ge(rowsT_ready, n + 1)
                                above_zero(pe, shifted, 2 * n + half - 1)
                                logits(mm, ps_logits, rowsT[buf], 2 * half)
                                logits(mm, ps_logits, rowsT[buf], 2 * half + 1).then_inc(logits_made, 1)
                            if there(m if isinstance(n, int) else n):
                                pe.wait_ge(weights_ready, 2 * m + half + 1)
                                for s in range(half * SLOT_TILES // 2, (half + 1) * SLOT_TILES // 2):
                                    last = mm(ps_slots[:, s, :], expd3[(buf + 1) % 3][:, s * P:(s + 1) * P],
                                              xn_all[:, bass.ds(m, 1), :].rearrange("p o d -> p (o d)"), start=False, stop=False)
                                if half == 1:
                                    last.then_inc(mixed, 1)

                    tiles_in_threes(pe, step, 2)
                    all_slots_plus_nothing(False, True).then_inc(slots_made, 1)
                    pe.wait_ge(slot_tanh, 1)
                    for s in range(SLOT_TILES):
                        last = nc.tensor.transpose(ps_logits[:, s * P:(s + 1) * P], slots[:, s, :], ident[:, :])
                    last.then_inc(slotsT_made, 1)
                    pe.wait_ge(slotsT_ready, 1)
                    pe.wait_ge(experts_loaded, 16 * (TILE_EXPERTS + 1))
                    for n in range(SEXPERTS):
                        s, j = n // TILE_EXPERTS, n % TILE_EXPERTS
                        last = mm(ps_slots[j * SLOTS:(j + 1) * SLOTS, s, :], slotsT[:, n * SLOTS:(n + 1) * SLOTS],
                                  expert_w[:, n, :], start=True, stop=True)
                        if n % (SEXPERTS // BANKS) == SEXPERTS // BANKS - 1:
                            last.then_inc(experts_made, 1)

        with ExitStack() as ctx:
            mem = Memory(nc, ctx)
            sb, ps, sem = mem.sb, mem.ps, mem.sem
            weights = [sb(f"d_weights{i}", [P, ALL_SLOTS]) for i in range(2)]
            weightsT = [sb(f"d_weightsT{i}", [P, SLOT_TILES, P]) for i in range(2)]
            ps_logits = ps("d_ps_logits2", [P, ALL_SLOTS])
            ps_turn = ps("d_ps_turn", [P, 2, BANK])
            ps_out = ps("d_ps_out", [P, BANK])
            rowsT_high_ready, rowsT_ready, logits_made, peak_ready, shifted, exp_done = (
                sem(f"d2_{n}") for n in ("rowsT_high_ready", "rowsT_ready", "logits_made", "peak_ready", "shifted", "exp_done"))
            total_ready, inverse_ready, weights_ready, turned, weightsT_ready, mixed, added = (
                sem(f"d2_{n}") for n in ("total_ready", "inverse_ready", "weights_ready", "turned", "weightsT_ready", "mixed", "added"))
            stored, half_peak_ready = sem("d2_stored"), sem("d2_half_peak_ready")
            out_view = out.rearrange("b (t p) d -> p (b t) d", p=P)

            with nc.Block() as block:

                @block.sync
                def _(sp):
                    def store(n):
                        sp.wait_ge(added, n + 1)
                        sp.dma_start(out_view[:, bass.ds(n, 1), :], X[:, bass.ds(n, 1), :]).then_inc(stored, 16)

                    store(0)
                    with sp.Fori(1, ROW_TILES) as n:
                        store(n)
                    sp.wait_ge(stored, 16 * ROW_TILES)

                @block.gpsimd
                def _(pool):
                    rest = (rowsT_high_ready, rowsT_ready)
                    rows_rest(pool, rest, 0, 0)
                    rows_rest(pool, rest, 1, 1)

                    def step(n, par):
                        if there(n + 2 if isinstance(n, int) else n):
                            rows_rest(pool, rest, n + 2, par)
                        if there(n):
                            pool.wait_ge(inverse_ready, n + 1)
                            pool.wait_ge(exp_done, n + 1)
                            above_zero(pool, turned, BANKS * (n - 1))
                            nc.gpsimd.tensor_tensor(
                                weights[par][:, :].rearrange("p (e s) -> p e s", s=SLOTS),
                                expd[par][:, :].rearrange("p (e s) -> p e s", s=SLOTS),
                                total[:, 0, :].unsqueeze(1).to_broadcast([P, SEXPERTS, SLOTS]), ALU.mult).then_inc(weights_ready, 1)

                    tiles_in_pairs(pool, step, 0)

                @block.vector
                def _(dve):
                    def half_peak(n, half):
                        dve.wait_ge(logits_made, 2 * n + half + 1)
                        nc.vector.tensor_reduce(peak[:, half, :], ps_logits[:, half * HALF:(half + 1) * HALF]
                                                .rearrange("p (e s) -> p s e", s=SLOTS), AX.X, ALU.max).then_inc(half_peak_ready, 1)

                    def shift(n, par):
                        dve.wait_ge(half_peak_ready, 2 * (n + 1))
                        nc.vector.tensor_tensor(peak[:, 0, :], peak[:, 0, :], peak[:, 1, :], ALU.max).then_inc(peak_ready, 1)
                        dve.wait_ge(peak_ready, n + 1)
                        above_zero(dve, weights_ready, n - 1)
                        nc.vector.tensor_tensor(expd[par][:, :].rearrange("p (e s) -> p e s", s=SLOTS),
                                                ps_logits[:, :].rearrange("p (e s) -> p e s", s=SLOTS),
                                                peak[:, 0, :].unsqueeze(1).to_broadcast([P, SEXPERTS, SLOTS]),
                                                ALU.subtract).then_inc(shifted, 1)

                    def invert(n, par):
                        dve.wait_ge(exp_done, n + 1)
                        above_zero(dve, weights_ready, n)
                        nc.vector.tensor_reduce(total[:, 0, :], expd[par][:, :].rearrange("p (e s) -> p s e", s=SLOTS),
                                                AX.X, ALU.add).then_inc(total_ready, 1)
                        dve.wait_ge(total_ready, n + 1)
                        nc.vector.reciprocal(total[:, 0, :], total[:, 0, :]).then_inc(inverse_ready, 1)

                    def add(n):
                        dve.wait_ge(mixed, n + 1)
                        x = X[:, bass.ds(n, 1), :].rearrange("p o d -> p (o d)")
                        nc.vector.tensor_tensor(x, ps_out[:, 0:D], x, ALU.add).then_inc(added, 1)

                    def step(n, par):
                        if there(n):
                            half_peak(n, 1)
                            shift(n, par)
                        if there(n - 2 if isinstance(n, int) else n):
                            add(n - 2)
                        if there(n + 1 if isinstance(n, int) else n):
                            half_peak(n + 1, 0)
                        if there(n):
                            invert(n, par)

                    half_peak(0, 0)
                    tiles_in_pairs(dve, step, 2)

                @block.scalar
                def _(act):
                    def fetch(n, par):
                        above_zero(act, logits_made, 2 * (n - 1))
                        nc.scalar.activation(rowsT[par][0][:, :], xnT[:, bass.ds(P * n, P)], ACT.Copy).then_inc(rowsT_high_ready, 1)

                    def step(n, par):
                        if there(n):
                            act.wait_ge(shifted, n + 1)
                            nc.scalar.activation(expd[par][:, :], expd[par][:, :], ACT.Exp).then_inc(exp_done, 1)
                        if there(n + 2 if isinstance(n, int) else n):
                            fetch(n + 2, par)
                        if there(n - 1 if isinstance(n, int) else n):
                            for bank in range(BANKS):
                                copy(n - 1, 1 - par, bank)

                    def copy(n, par, bank):
                        act.wait_ge(turned, BANKS * n + bank + 1)
                        above_zero(act, mixed, n - 1)
                        tiles = slice(bank * BANK_TILES, (bank + 1) * BANK_TILES)
                        nc.scalar.activation(weightsT[par][:, tiles, :],
                                             ps_turn[:, bank % 2, :].rearrange("p (s t) -> p s t", t=P), ACT.Copy)\
                            .then_inc(weightsT_ready, 1)

                    fetch(0, 0)
                    fetch(1, 1)
                    tiles_in_pairs(act, step, 1)

                @block.tensor
                def _(pe):
                    mm = nc.tensor.matmul

                    def turn(n, par, bank):
                        above_zero(pe, weightsT_ready, BANKS * n + bank - 1)
                        for j in range(BANK_TILES):
                            s = bank * BANK_TILES + j
                            last = nc.tensor.transpose(ps_turn[:, bank % 2, j * P:(j + 1) * P], weights[par][:, s * P:(s + 1) * P],
                                                       ident[:, :])
                        last.then_inc(turned, 1)

                    def step(n, par):
                        back = there(n - 2 if isinstance(n, int) else n)
                        m = n - 2
                        if there(n):
                            pe.wait_ge(rowsT_ready, n + 1)
                            above_zero(pe, shifted, n)
                        for half in range(2):
                            if there(n):
                                logits(mm, ps_logits, rowsT[par], 2 * half)
                                logits(mm, ps_logits, rowsT[par], 2 * half + 1).then_inc(logits_made, 1)
                            if back and half == 0:
                                pe.wait_ge(weights_ready, m + 1)
                            if back:
                                turn(m, par, 2 * half)
                                turn(m, par, 2 * half + 1)
                        if back:
                            pe.wait_ge(weightsT_ready, BANKS * (m + 1))
                            above_zero(pe, added, m)
                            for s in range(SLOT_TILES):
                                last = mm(ps_out[:, 0:D], weightsT[par][:, s, :], slot_out[:, s, :],
                                          start=(s == 0), stop=(s == SLOT_TILES - 1))
                            last.then_inc(mixed, 1)

                    tiles_in_pairs(pe, step, 2)


def build(nc, x_in, w, c, out):
    with ExitStack() as ctx:
        mem = Memory(nc, ctx)
        X = mem.sb("x_rows", [P, BATCHES * TILES, D])
        ident = mem.sb("ident", [P, P])
        stage_causal_attention(nc, X, ident, x_in, w, c)
        stage_experts(nc, X, ident, w, c)
        stage_cosine_attention(nc, X, ident, w, c)
        stage_slots(nc, X, ident, w, c, out)


def laid_out(a):
    import numpy as np

    bfloat16 = "bfloat16"

    w = {}
    w["wqT"], w["wkT"], w["woT"] = (np.ascontiguousarray(a[f"L0_attn_W{n}"].T) for n in "qko")
    wv = np.zeros((D, HEADS, VW), np.float32)
    wv[:, :, :HD] = a["L0_attn_Wv"].T.reshape(D, HEADS, HD)
    w["wvT"] = wv.reshape(D, HEADS * VW)
    bv = np.ones((HEADS, VW), np.float32)
    bv[:, :HD] = a["L0_attn_bv"].reshape(HEADS, HD)
    w["bv"] = bv.reshape(HEADS * VW)
    w["bq"], w["bk"] = (a[f"L0_attn_b{n}"].reshape(D, 1) for n in "qk")
    w["bo"] = a["L0_attn_bo"].reshape(1, D)

    c = {}
    c["ident"] = np.eye(P, dtype=np.float32)
    c["ident_bf16"] = np.eye(P).astype(bfloat16)
    after = np.triu(np.ones((P, P)), 1)
    c["mask_qk"] = (-1e30 * after).astype(bfloat16)
    c["mask_kq"] = (-1e30 * after.T).astype(bfloat16)
    slopes = np.array([2.0 ** (-(h + 1) / 2) for h in range(HEADS)], np.float32)
    decay = slopes[:, None] * np.arange(SEQ, dtype=np.float32)
    rows = []
    for _ in range(3):
        rows.append(decay.astype(bfloat16))
        decay = decay - rows[-1].astype(np.float32)
    one = np.ones((HEADS, SEQ), bfloat16)
    c["rows_k"] = np.stack([*rows, one, one])
    c["rows_q"] = np.stack([one, one, one])
    more_layouts(a, w, c)
    return w, c


def kernel(**inputs):
    import numpy as np
    import concourse.bacc as bacc
    from concourse.bass_utils import run_bass_kernel_spmd

    a = {n: np.asarray(x) for n, x in inputs.items()}
    w, c = laid_out(a)
    nc = bacc.Bacc("TRN2", target_bir_lowering=False, num_devices=1)
    arrays, aps = {}, {}
    for kind, named in (("x", {"x": a["L0_attn_x"]}), ("w", w), ("c", c)):
        for n, x in named.items():
            x = np.ascontiguousarray(x)
            arrays[f"in_{kind}_{n}"] = x
            aps[kind, n] = nc.dram_tensor(f"in_{kind}_{n}", x.shape, mybir.dt.from_np(x.dtype), kind="ExternalInput").ap()
    out = nc.dram_tensor("out_dram", a["L0_attn_x"].shape, F32, kind="ExternalOutput").ap()
    build(nc, aps["x", "x"], {n: aps["w", n] for n in w}, {n: aps["c", n] for n in c}, out)
    return run_bass_kernel_spmd(nc, [arrays], core_ids=[0]).results[0]["out_dram"]


def more_layouts(a, w, c):
    import numpy as np

    w["rw1"], w["W1"], w["W2"], w["b2"], w["rw2"] = (a[f"L0_ffn_{n}"] for n in ("rw1", "W1", "W2", "b2", "rw2"))
    w["rb2"] = a["L0_ffn_rb2"].reshape(1, EXPERTS)
    b1 = np.concatenate([a["L0_ffn_rb1"][None], a["L0_ffn_b1"]]).reshape(UNITS, FF_TILES, P)
    w["b1"] = np.ascontiguousarray(b1.transpose(2, 0, 1))
    c["earlier"] = np.tril(np.ones((EXPERTS, EXPERTS), np.float32), -1)

    w["qkv"] = a["L1_attn_w_qkv"]
    out = np.zeros((VC, CHEADS, D + 1), np.float32)
    out[:CHD, :, :D] = a["L1_attn_w_out"].reshape(CHEADS, CHD, D).transpose(1, 0, 2)
    out[CHD, :, D] = 1
    w["out"] = out
    w["b_out"] = a["L1_attn_b_out"]
    w["log_scale"] = a["L1_attn_logit_scale"].reshape(CHEADS)
    w["phiT"] = np.ascontiguousarray(a["L1_ffn_phi_w"].T)
    w["phi_b"] = a["L1_ffn_phi_b"].reshape(1, ALL_SLOTS)
    w["expert_w"], w["expert_b"] = a["L1_ffn_expert_w"], a["L1_ffn_expert_b"]
```

```python
import math
from contextlib import ExitStack

import concourse.bass as bass
from concourse import mybir

ALU = mybir.AluOpType
ACT = mybir.ActivationFunctionType
AX = mybir.AxisListType
F32 = mybir.dt.float32
BF16 = mybir.dt.bfloat16
F16 = mybir.dt.float16
F32R = mybir.dt.float32r

P = 128
D = 128
BATCHES = 16
SEQ = 512
TILES = SEQ // P
HEADS = 16
LN_EPS = 1e-5

HD = D // HEADS
PARTS_Q = (0, 0, 0, 1, 1, 2)
PARTS_K = (0, 1, 2, 0, 1, 0)
ROW_ALIBI = len(PARTS_Q) * HD
ROW_MAX = ROW_ALIBI + 3
ROWS = ROW_MAX + 2
ST_AT = {0: 0, 1: 512, 3: 896, 2: 1024}
ST_COLS = 1280
VW = HD + 1
GROUP = 4
GROUPS = HEADS // GROUP
GW = P // GROUP
REPLICAS = len(PARTS_Q) + len(PARTS_K)
WEIGHT_LOADS = 11 + 1 + 4
MAX_HEADS = range(4, 11)
MAX_UNITS = [(qt, h, max(1, 4 // (qt + 1))) for qt in range(TILES) for h in range(0, HEADS, max(1, 4 // (qt + 1)))]


def order_of_work(after, front, back, first):
    units = iter(range(len(MAX_UNITS)))
    spread = sum(len(steps_of_head(h)) for h in MAX_HEADS)
    steps, taken = 0, 0
    work = []
    for h in range(HEADS):
        between = []
        if h == 0 and back:
            between.append(("values", 0))
        if h == 1 and back and not first:
            between.append(("turn_out", 0))
        if h == 2 and back and not first:
            between.append(("project", 0))
        if h == 12 and front:
            between.append(("turn_shifts", 0))
        if h == 13 and after:
            between.append(("turn_rows", 0))
        if h == 14 and after:
            between.append(("queries_keys", 0))
        for n, step in enumerate(steps_of_head(h)):
            if back:
                work.append(step)
            if n == 0:
                work += between
            if front and h in MAX_HEADS:
                steps += 1
                upto = steps * len(MAX_UNITS) // spread
                work += [("max", next(units)) for _ in range(upto - taken)]
                taken = upto
        if back and h % GROUP == 2 and h > GROUP:
            work.append(("turn", h // GROUP - 1))
        if h == MAX_HEADS[-1]:
            work += [("shifts", 0)] * front + [("rows", 0)] * after
    if back:
        work += [("attend", (GROUPS - 1, kt)) for kt in range(TILES)] + [("turn", GROUPS - 1)]
    return work


def steps_of_head(h):
    attends = [("attend", (h // GROUP - 1, kt)) for kt in range(TILES)] if h % GROUP == 0 and h else []
    return [("scores", h), *attends[:2], ("second_scores", h), *attends[2:], ("last_scores", h)]


def above_zero(eng, sem, value):
    if not isinstance(value, int) or value > 0:
        eng.wait_ge(sem, value)


class Memory:

    def __init__(self, nc, ctx):
        self.nc, self.ctx, self.sems = nc, ctx, []
        ctx.callback(self.give_back_semaphores)

    def sb(self, name, shape, dt=F32):
        return self.ctx.enter_context(self.nc.sbuf_tensor(name, shape, dt))

    def ps(self, name, shape, dt=F32):
        return self.ctx.enter_context(self.nc.psum_tensor(name, shape, dt))

    def sem(self, name):
        self.sems.append(self.nc.alloc_semaphore(name))
        return self.sems[-1]

    def give_back_semaphores(self):
        if self.sems:
            self.nc.clear_and_free_semaphores(self.sems)
            self.nc.all_engine_barrier()


class LayerNorm:

    def __init__(self, mem, tag, tiles=TILES):
        self.tiles = tiles
        self.stats = mem.sb(f"{tag}_stats", [P, tiles, 6])
        self.mv = mem.sb(f"{tag}_mv", [P, tiles, 2])
        self.rstd = mem.sb(f"{tag}_rstd", [P, tiles])
        self.stats_ready = mem.sem(f"{tag}_stats_ready")
        self.mv_ready = mem.sem(f"{tag}_mv_ready")
        self.var = mem.sb(f"{tag}_var", [P, tiles])
        self.power = mem.sb(f"{tag}_power", [P, tiles])
        self.eps = mem.sb(f"{tag}_eps", [P, tiles])
        self.carrier = mem.sb(f"{tag}_carrier", [P, 1])
        self.power_ready = mem.sem(f"{tag}_power_ready")
        self.var_ready = mem.sem(f"{tag}_var_ready")
        self.rstd_ready = mem.sem(f"{tag}_rstd_ready")
        self.ready = mem.sem(f"{tag}_ready")

    def set_up(self, nc, pool):
        nc.gpsimd.memset(self.power[:, :], -0.5).then_inc(self.power_ready, 1)
        nc.gpsimd.memset(self.eps[:, :], LN_EPS).then_inc(self.power_ready, 1)
        pool.wait_ge(self.power_ready, 2)

    def take_rstd(self, nc, pool, b):
        pool.wait_ge(self.mv_ready, b + 1)
        nc.gpsimd.tensor_tensor(self.var[:, :], self.mv[:, :, 1], self.eps[:, :], ALU.add).then_inc(self.var_ready, 1)
        pool.wait_ge(self.var_ready, b + 1)
        nc.gpsimd.tensor_tensor(self.rstd[:, :], self.var[:, :], self.power[:, :], ALU.pow).then_inc(self.rstd_ready, 1)

    def run(self, nc, dve, rows, out, b):
        self.take_statistics(nc, dve, rows, b)
        self.normalise(nc, dve, rows, out, b)

    def take_statistics(self, nc, dve, rows, b):
        for t in range(self.tiles):
            last = nc.vector.bn_stats(self.stats[:, t, :], rows(t))
        last.then_inc(self.stats_ready, 1)
        dve.wait_ge(self.stats_ready, b + 1)
        nc.vector.tensor_copy(self.carrier[:, :], self.stats[:, 0, 0:1])
        for t in range(self.tiles):
            last = nc.vector.bn_aggr(self.mv[:, t, :], self.stats[:, t, :])
        last.then_inc(self.mv_ready, 1)

    def normalise(self, nc, dve, rows, out, b):
        dve.wait_ge(self.rstd_ready, b + 1)
        for t in range(self.tiles):
            last = nc.vector.tensor_scalar(out[:, t, :], rows(t), self.mv[:, t, 0:1], self.rstd[:, t:t + 1],
                                           ALU.subtract, ALU.mult)
        last.then_inc(self.ready, 1)


def stage_causal_attention(nc, X, ident, x_in, w, c, loads_for_later):
    with ExitStack() as ctx:
        mem = Memory(nc, ctx)
        sb, ps, sem = mem.sb, mem.ps, mem.sem
        wq, wk, wo = (sb(n, [D, D]) for n in ("a_wq", "a_wk", "a_wo"))
        wv = sb("a_wv", [D, HEADS * VW])
        bq, bk = sb("a_bq", [P, 1]), sb("a_bk", [P, 1])
        bv = sb("a_bv", [P, HEADS * VW])
        bo = sb("a_bo", [1, D])
        ones = sb("a_ones", [1, P])
        identb = sb("a_identb", [P, P], BF16)
        mask_qk = sb("a_mask_qk", [P, P], BF16)
        mask_kq = sb("a_mask_kq", [P, P], BF16)
        xn = sb("a_xn", [P, TILES, D])
        xnT = [sb(f"a_xnT{i}", [D, SEQ]) for i in range(2)]
        full = [sb(f"a_full_{n}", [P, SEQ]) for n in "qk"]
        rest = [sb(f"a_rest_{n}", [P, SEQ]) for n in "qk"]
        parts = [sb(f"a_parts_{n}", [P, 3, SEQ], BF16) for n in "qk"]
        heads_q = [sb(f"a_heads_q{i}", [ROWS, HEADS, SEQ], BF16) for i in range(2)]
        heads_k = [sb(f"a_heads_k{i}", [ROWS, HEADS, SEQ], BF16) for i in range(2)]
        parts_dram = nc.dram_tensor("a_parts_dram", [2, P, 3, SEQ], BF16).ap()
        v = sb("a_v", [P, TILES, HEADS * GW])
        neg_max = sb("a_neg_max", [P, TILES, HEADS])
        max_parts = sb("a_max_parts", [P, TILES, 2, HEADS], BF16)
        maxT = sb("a_maxT", [2 * HEADS, SEQ], BF16)
        probs = [sb(f"a_probs{i}", [P, GROUP, ST_COLS]) for i in range(2)]
        group_out = [sb(f"a_group_out{i}", [P, SEQ]) for i in range(2)]
        rsum = sb("a_rsum", [P, TILES, GROUP])
        heads_out = sb("a_heads_out", [P, TILES, D])
        outT = sb("a_outT", [D, SEQ])
        ps_st = ps("a_ps_st", [P, 3 * 512])
        ps_max = ps("a_ps_max", [P, 2, 512])
        ps_out = ps("a_ps_out", [P, 2, 512])
        ps_misc = ps("a_ps_misc", [P, 512])

        ln = LayerNorm(mem, "a_ln")
        x0_loaded, x_loaded, w_loaded = sem("a_x0_loaded"), sem("a_x_loaded"), sem("a_w_loaded")
        later_loaded = sem("a_later_loaded")
        ones_ready = sem("a_ones_ready")
        xnT_made, xnT_ready = sem("a_xnT_made"), sem("a_xnT_ready")
        q_made, k_made = sem("a_q_made"), sem("a_k_made")
        made = [q_made, k_made]
        full_ready = [sem(f"a_full_{n}_ready") for n in "qk"]
        hi_ready = [sem(f"a_hi_{n}_ready") for n in "qk"]
        rest_ready = [sem(f"a_rest_{n}_ready") for n in "qk"]
        mid_ready = [sem(f"a_mid_{n}_ready") for n in "qk"]
        lo_ready = [sem(f"a_lo_{n}_ready") for n in "qk"]
        parts_stored = sem("a_parts_stored")
        heads_loaded = [sem(f"a_heads_loaded{i}") for i in range(2)]
        max_made, max_taken = sem("a_max_made"), sem("a_max_taken")
        max_hi_ready, max_parts_ready = sem("a_max_hi_ready"), sem("a_max_parts_ready")
        maxT_made, maxT_ready = sem("a_maxT_made"), sem("a_maxT_ready")
        max_rows_loaded = [sem(f"a_max_rows_loaded{i}") for i in range(2)]
        v_made, v_ready = sem("a_v_made"), sem("a_v_ready")
        st_a_made, st_b_made = sem("a_st_a_made"), sem("a_st_b_made")
        exp_a_done, exp_b_done = sem("a_exp_a_done"), sem("a_exp_b_done")
        av_done = sem("a_av_done")
        v_zeroed = sem("a_v_zeroed")
        group_out_ready, group_turned = sem("a_group_out_ready"), sem("a_group_turned")
        rsum_ready, heads_out_ready = sem("a_rsum_ready"), sem("a_heads_out_ready")
        outT_made, outT_ready = sem("a_outT_made"), sem("a_outT_ready")
        proj_made, x_added = sem("a_proj_made"), sem("a_x_added")

        loads = [(wq, w["wqT"]), (wk, w["wkT"]), (wo, w["woT"]), (wv, w["wvT"]), (bq, w["bq"]), (bk, w["bk"]),
                 (bo, w["bo"]), (identb, c["ident_bf16"]), (mask_qk, c["mask_qk"]), (mask_kq, c["mask_kq"]),
                 (ident, c["ident"])]
        x_view = x_in.rearrange("b (t p) d -> p (b t) d", p=P)

        with nc.Block() as block:

            def pipeline(eng, step):
                step(0, None, None, 1, 0, None, None)
                step(1, 0, None, 0, 0, 0, None)
                step(2, 1, 0, 1, 1, 0, 0)
                with eng.Fori(0, (BATCHES - 4) // 2) as i:
                    step(2 * i + 3, 2 * i + 2, 2 * i + 1, 0, i + 1, i + 1, i)
                    step(2 * i + 4, 2 * i + 3, 2 * i + 2, 1, i + 2, i + 1, i + 1)
                step(BATCHES - 1, BATCHES - 2, BATCHES - 3, 0, BATCHES // 2 - 1, BATCHES // 2 - 1, BATCHES // 2 - 2)
                step(None, BATCHES - 1, BATCHES - 2, 1, None, BATCHES // 2 - 1, BATCHES // 2 - 1)
                step(None, None, BATCHES - 1, 0, None, None, BATCHES // 2 - 1)

            def work_of(after, front, back):
                return order_of_work(after is not None, front is not None, back is not None,
                                     isinstance(back, int) and back == 0)

            @block.sync
            def _(sp):
                sp.dma_start(X[:, 0:TILES, :], x_view[:, 0:TILES, :]).then_inc(x0_loaded, 16)
                for dst, src in loads:
                    sp.dma_start(dst[:, :], src).then_inc(w_loaded, 16)
                sp.dma_start(bv[:, :], w["bv"].partition_broadcast(P)).then_inc(w_loaded, 16)
                for i in range(2):
                    sp.dma_start(heads_k[i][ROW_ALIBI:ROWS, :, :], c["rows_k"]).then_inc(w_loaded, 16)
                    sp.dma_start(heads_q[i][ROW_ALIBI:ROW_MAX, :, :], c["rows_q"]).then_inc(w_loaded, 16)
                sp.dma_start(X[:, TILES:, :], x_view[:, TILES:, :]).then_inc(x_loaded, 16)

                def step(after, b, bb, par, ka, kb, kbb):
                    if b is not None:
                        sp.wait_ge(maxT_ready, b + 1)
                        for part in range(2):
                            sp.dma_start(heads_q[par][ROW_MAX + part:ROW_MAX + part + 1, :, :],
                                         maxT[part * HEADS:(part + 1) * HEADS, :])\
                                .then_inc(max_rows_loaded[par], 16)
                    if after is not None:
                        for n in range(2):
                            sp.wait_ge(lo_ready[n], after + 1)
                            sp.dma_start(parts_dram[n], parts[n][:, :, :]).then_inc(parts_stored, 16)
                        sp.wait_ge(parts_stored, 32 * (after + 1))
                        for n, which in enumerate((PARTS_Q, PARTS_K)):
                            dst = (heads_q, heads_k)[n][1 - par]
                            for g, part in enumerate(which):
                                sp.dma_start(dst[g * HD:(g + 1) * HD, :, :],
                                             parts_dram[n, :, part, :].rearrange("(h d) t -> d h t", d=HD))\
                                    .then_inc(heads_loaded[1 - par], 16)

                pipeline(sp, step)
                for dst, src in loads_for_later:
                    sp.dma_start(dst, src).then_inc(later_loaded, 16)
                sp.wait_ge(later_loaded, 16 * len(loads_for_later))

            @block.gpsimd
            def _(pool):
                nc.gpsimd.memset(ones[:, :], 1.0).then_inc(ones_ready, 1)
                nc.gpsimd.memset(v[:, :, :], 0.0).then_inc(v_zeroed, 1)
                ln.set_up(nc, pool)

                def step(after, b, bb, par, ka, kb, kbb):
                    if after is None:
                        return
                    ln.take_rstd(nc, pool, after)
                    if b is not None:
                        pool.wait_ge(heads_loaded[par], 16 * REPLICAS * (kb + 1))
                    for n in range(2):
                        pool.wait_ge(mid_ready[n], after + 1)
                        if n == 1 and bb is not None:
                            pool.wait_ge(st_b_made, HEADS * (bb + 1))
                        nc.gpsimd.tensor_tensor(parts[n][:, 2, :], rest[n][:, :], parts[n][:, 1, :], ALU.subtract)\
                            .then_inc(lo_ready[n], 1)

                pipeline(pool, step)

            @block.vector
            def _(dve):
                dve.wait_ge(x0_loaded, 16)
                dve.wait_ge(w_loaded, 16 * WEIGHT_LOADS)
                dve.wait_ge(v_zeroed, 1)

                def norm_group(b, j):
                    seen = GROUPS * b + j
                    dve.wait_ge(group_turned, seen + 1)
                    out = ps_misc[:, :].rearrange("p (t g c) -> p t g c", g=GROUP, c=GW)
                    nc.vector.reciprocal(rsum[:, :, :], out[:, :, :, HD]).then_inc(rsum_ready, 1)
                    dve.wait_ge(rsum_ready, seen + 1)
                    if j == 0:
                        above_zero(dve, outT_made, b)
                    dst = heads_out[:, :, j * GROUP * HD:(j + 1) * GROUP * HD].rearrange("p t (g d) -> p t g d", d=HD)
                    nc.vector.tensor_tensor(dst, out[:, :, :, 0:HD],
                                            rsum[:, :, :].unsqueeze(3).to_broadcast([P, TILES, GROUP, HD]),
                                            ALU.mult).then_inc(heads_out_ready, 1)

                def add_to_x(b):
                    dve.wait_ge(proj_made, b + 1)
                    rows = X[:, bass.ds(TILES * b, TILES), :]
                    nc.vector.tensor_tensor(rows, ps_misc[:, :].rearrange("p (t d) -> p t d", t=TILES), rows, ALU.add)\
                        .then_inc(x_added, 1)

                def split_shifts(b):
                    dve.wait_ge(max_taken, len(MAX_UNITS) * (b + 1))
                    above_zero(dve, maxT_made, b)
                    nc.vector.tensor_copy(max_parts[:, :, 0, :], neg_max[:, :, :]).then_inc(max_hi_ready, 1)
                    dve.wait_ge(max_hi_ready, b + 1)
                    nc.vector.tensor_tensor(max_parts[:, :, 1, :], neg_max[:, :, :], max_parts[:, :, 0, :],
                                            ALU.subtract).then_inc(max_parts_ready, 1)

                def keep_values(bb):
                    dve.wait_ge(v_made, bb + 1)
                    for half in range(2):
                        for t in range(2):
                            last = nc.vector.tensor_tensor(
                                v[:, 2 * half + t, :].rearrange("p (h c) -> p h c", c=GW)[:, :, 0:VW],
                                ps_out[:, half, t * HEADS * VW:(t + 1) * HEADS * VW].rearrange("p (h c) -> p h c", c=VW),
                                bv[:, :].rearrange("p (h c) -> p h c", c=VW), ALU.add)
                    last.then_inc(v_ready, 1)

                def step(after, b, bb, par, ka, kb, kbb):
                    for what, u in work_of(after, b, bb):
                        if what == "values":
                            keep_values(bb)
                        if what == "project":
                            add_to_x(bb - 1)
                        if what == "max":
                            qt, h, k = MAX_UNITS[u]
                            dve.wait_ge(max_made, len(MAX_UNITS) * b + u + 1)
                            cols = (qt + 1) * P
                            nc.vector.tensor_reduce(
                                neg_max[:, qt, h:h + k],
                                ps_max[:, u % 2, 0:k * cols].rearrange("p (h c) -> p h c", c=cols),
                                AX.X, ALU.max, negate=True).then_inc(max_taken, 1)
                        if what == "shifts":
                            split_shifts(b)
                        if what == "rows":
                            if isinstance(after, int) and after == 1:
                                dve.wait_ge(x_loaded, 16)
                            above_zero(dve, xnT_made, after)
                            ln.run(nc, dve, lambda t: X[:, bass.ds(TILES * after + t, 1), :].rearrange("p o d -> p (o d)"),
                                   xn, after)
                        if what == "queries_keys":
                            for n, (bias, scale) in enumerate(((bq, HD ** -0.5), (bk, 1.0))):
                                dve.wait_ge(made[n], after + 1)
                                above_zero(dve, rest_ready[n], after)
                                nc.vector.tensor_scalar(full[n][:, :], ps_max[:, n, :], bias[:, 0:1], scale, ALU.add, ALU.mult)\
                                    .then_inc(full_ready[n], 1)
                            for n in range(2):
                                dve.wait_ge(hi_ready[n], after + 1)
                                above_zero(dve, lo_ready[n], after)
                                nc.vector.tensor_tensor(rest[n][:, :], full[n][:, :], parts[n][:, 0, :], ALU.subtract)\
                                    .then_inc(rest_ready[n], 1)
                        if what == "turn":
                            norm_group(bb, u)

                pipeline(dve, step)
                add_to_x(BATCHES - 1)

            @block.scalar
            def _(act):
                def group_to_sbuf(b, j):
                    seen = GROUPS * b + j
                    act.wait_ge(av_done, seen + 1)
                    above_zero(act, group_turned, seen - 1)
                    nc.scalar.activation(group_out[j % 2][:, :], ps_out[:, j % 2, :], ACT.Copy).then_inc(group_out_ready, 1)

                def outT_to_sbuf(b):
                    act.wait_ge(outT_made, b + 1)
                    above_zero(act, proj_made, b)
                    nc.scalar.activation(outT[:, :], ps_misc[:, :], ACT.Copy).then_inc(outT_ready, 1)

                def shifts_to_sbuf(b, par, kbb):
                    act.wait_ge(maxT_made, b + 1)
                    if kbb is not None:
                        act.wait_ge(max_rows_loaded[1 - par], 32 * (kbb + 1))
                    nc.scalar.activation(maxT[:, :], ps_misc[0:2 * HEADS, 0:SEQ // 2].bitcast(BF16), ACT.Copy)\
                        .then_inc(maxT_ready, 1)

                def rows_to_sbuf(after, par):
                    act.wait_ge(xnT_made, after + 1)
                    nc.scalar.activation(xnT[1 - par][:, :], ps_misc[:, :], ACT.Copy).then_inc(xnT_ready, 1)

                def exponentials(bb, h):
                    seen, j = HEADS * bb + h, h // GROUP
                    if h % GROUP == 0:
                        above_zero(act, av_done, GROUPS * bb + j - 1)
                    dst = probs[j % 2][:, h % GROUP, :]
                    act.wait_ge(st_a_made, seen + 1)
                    nc.scalar.activation(dst[:, 0:512], ps_st[:, 0:512], ACT.Exp).then_inc(exp_a_done, 1)
                    act.wait_ge(st_b_made, seen + 1)
                    nc.scalar.activation(dst[:, 512:ST_COLS], ps_st[:, 512:ST_COLS], ACT.Exp)\
                        .then_inc(exp_b_done, 1)

                def step(after, b, bb, par, ka, kb, kbb):
                    for what, n in work_of(after, b, bb):
                        if what == "scores":
                            if n % GROUP == 2 and n > GROUP:
                                group_to_sbuf(bb, n // GROUP - 1)
                            exponentials(bb, n)
                        if what == "turn_out":
                            outT_to_sbuf(bb - 1)
                        if what == "turn_shifts":
                            shifts_to_sbuf(b, par, kbb)
                        if what == "turn_rows":
                            rows_to_sbuf(after, par)
                        if what == "queries_keys":
                            for k in range(2):
                                act.wait_ge(full_ready[k], after + 1)
                                above_zero(act, parts_stored, 32 * after)
                                nc.scalar.activation(parts[k][:, 0, :], full[k][:, :], ACT.Copy).then_inc(hi_ready[k], 1)
                    if after is not None:
                        for n in range(2):
                            act.wait_ge(rest_ready[n], after + 1)
                            nc.scalar.activation(parts[n][:, 1, :], rest[n][:, :], ACT.Copy).then_inc(mid_ready[n], 1)
                    if bb is not None:
                        group_to_sbuf(bb, GROUPS - 1)

                pipeline(act, step)
                outT_to_sbuf(BATCHES - 1)

            @block.tensor
            def _(pe):
                mm = nc.tensor.matmul
                pe.wait_ge(w_loaded, 16 * WEIGHT_LOADS)
                pe.wait_ge(ones_ready, 1)
                pe.wait_ge(v_zeroed, 1)

                def turn_out(b):
                    pe.wait_ge(heads_out_ready, GROUPS * (b + 1))
                    for t in range(TILES):
                        last = nc.tensor.transpose(ps_misc[:, t * P:(t + 1) * P], heads_out[:, t, :], ident[:, :])
                    last.then_inc(outT_made, 1)

                def project(b):
                    pe.wait_ge(outT_ready, b + 1)
                    for t in range(TILES):
                        dst = ps_misc[:, t * D:(t + 1) * D]
                        mm(dst, outT[:, t * P:(t + 1) * P], wo[:, :], start=True, stop=False)
                        last = mm(dst, ones[0:1, :], bo[:, :], start=False, stop=True)
                    last.then_inc(proj_made, 1)

                def take_max(b, par, u):
                    qt, h0, k = MAX_UNITS[u]
                    cols = (qt + 1) * P
                    if u >= 2:
                        pe.wait_ge(max_taken, len(MAX_UNITS) * b + u - 1)
                    for j in range(k):
                        h, at = h0 + j, j * cols
                        mm(ps_max[:, u % 2, at:at + cols], heads_q[par][0:ROW_MAX, h, qt * P:(qt + 1) * P],
                           heads_k[par][0:ROW_MAX, h, 0:cols], start=True, stop=False)
                        last = mm(ps_max[:, u % 2, at + cols - P:at + cols], identb[:, :], mask_qk[:, :],
                                  start=False, stop=True)
                    last.then_inc(max_made, 1)

                def transposed_scores(bb, par, h, which):
                    seen = HEADS * bb + h
                    q, k = heads_q[par], heads_k[par]

                    def tile(kt):
                        at, cols = ST_AT[kt], SEQ - kt * P
                        mm(ps_st[:, at:at + cols], k[0:ROWS, h, kt * P:(kt + 1) * P], q[0:ROWS, h, kt * P:SEQ],
                           start=True, stop=False)
                        return mm(ps_st[:, at:at + P], identb[:, :], mask_kq[:, :], start=False, stop=True)

                    if which == "scores":
                        above_zero(pe, exp_a_done, seen)
                        tile(0).then_inc(st_a_made, 1)
                    elif which == "second_scores":
                        above_zero(pe, exp_b_done, seen)
                        tile(1)
                    else:
                        tile(3)
                        tile(2).then_inc(st_b_made, 1)

                def attend(bb, j, kt):
                    seen = GROUPS * bb + j
                    if kt == 0:
                        operands_of_attention(bb, j, seen)
                    for g in range(GROUP):
                        h = j * GROUP + g
                        last = mm(ps_out[g * GW:(g + 1) * GW, j % 2, kt * P:SEQ], v[:, kt, h * GW:(h + 1) * GW],
                                  probs[j % 2][:, g, ST_AT[kt]:ST_AT[kt] + SEQ - kt * P],
                                  start=(kt == 0), stop=(kt == TILES - 1))
                    if kt == TILES - 1:
                        last.then_inc(av_done, 1)

                def operands_of_attention(bb, j, seen):
                    if j == 0:
                        pe.wait_ge(v_ready, bb + 1)
                    pe.wait_ge(exp_a_done, HEADS * bb + (j + 1) * GROUP)
                    pe.wait_ge(exp_b_done, HEADS * bb + (j + 1) * GROUP)
                    above_zero(pe, group_out_ready, seen - 1)

                def turn(after, b, bb, j):
                    seen = GROUPS * bb + j
                    pe.wait_ge(group_out_ready, seen + 1)
                    above_zero(pe, heads_out_ready, seen)
                    if j == 0:
                        above_zero(pe, x_added, bb)
                    if j == 2 and after is not None:
                        pe.wait_ge(xnT_ready, after + 1)
                    elif j == 2 and b is not None:
                        pe.wait_ge(maxT_ready, b + 1)
                    for t in range(TILES):
                        last = nc.tensor.transpose(ps_misc[:, t * P:(t + 1) * P], group_out[j % 2][:, t * P:(t + 1) * P],
                                                   ident[:, :])
                    last.then_inc(group_turned, 1)

                def make_values(bb, par):
                    above_zero(pe, group_out_ready, GROUPS * bb)
                    for t in range(TILES):
                        at = (t % 2) * HEADS * VW
                        last = mm(ps_out[:, t // 2, at:at + HEADS * VW], xnT[par][:, t * P:(t + 1) * P], wv[:, :],
                                  start=True, stop=True)
                    last.then_inc(v_made, 1)

                def turn_shifts(b, bb):
                    pe.wait_ge(max_parts_ready, b + 1)
                    if bb is not None:
                        pe.wait_ge(heads_out_ready, GROUPS * bb + 2)
                    for t in range(TILES):
                        last = nc.tensor.transpose(
                            ps_misc[0:2 * HEADS, t * P // 2:(t + 1) * P // 2].bitcast(BF16),
                            max_parts[:, t, :, :].rearrange("p a h -> p (a h)"), identb[:, :])
                    last.then_inc(maxT_made, 1)

                def turn_rows(after, b):
                    pe.wait_ge(ln.ready, after + 1)
                    if b is not None:
                        pe.wait_ge(maxT_ready, b + 1)
                    for t in range(TILES):
                        last = nc.tensor.transpose(ps_misc[:, t * P:(t + 1) * P], xn[:, t, :], ident[:, :])
                    last.then_inc(xnT_made, 1)

                def queries_keys(after, par):
                    pe.wait_ge(xnT_ready, after + 1)
                    above_zero(pe, max_taken, len(MAX_UNITS) * after)
                    mm(ps_max[:, 0, :], wq[:, :], xnT[par][:, :], start=True, stop=True).then_inc(q_made, 1)
                    mm(ps_max[:, 1, :], wk[:, :], xnT[par][:, :], start=True, stop=True).then_inc(k_made, 1)

                def step(after, b, bb, par, ka, kb, kbb):
                    if bb is not None:
                        pe.wait_ge(max_rows_loaded[1 - par], 32 * (kbb + 1))
                    for what, n in work_of(after, b, bb):
                        if what in ("scores", "second_scores", "last_scores"):
                            transposed_scores(bb, 1 - par, n, what)
                        if what == "values":
                            make_values(bb, 1 - par)
                        if what == "turn_out":
                            turn_out(bb - 1)
                        if what == "project":
                            project(bb - 1)
                        if what == "attend":
                            attend(bb, *n)
                        if what == "turn":
                            turn(after, b, bb, n)
                        if what == "max":
                            if n == 0:
                                operands_there(b, par, kb)
                            take_max(b, par, n)
                        if what == "turn_shifts":
                            turn_shifts(b, bb)
                        if what == "turn_rows":
                            turn_rows(after, b)
                        if what == "queries_keys":
                            queries_keys(after, 1 - par)

                def operands_there(b, par, kb):
                    pe.wait_ge(heads_loaded[par], 16 * REPLICAS * (kb + 1))
                    for n in range(2):
                        pe.wait_ge(full_ready[n], b + 1)

                pipeline(pe, step)
                turn_out(BATCHES - 1)
                project(BATCHES - 1)


EXPERTS = 8
FF = 512
FF_TILES = FF // P
UNITS = 1 + EXPERTS
HIDDEN_RING = 3
ACT_TILES = 3
TOP_K = 2


def first_layers(mem, w):
    w1_in = mem.sb("b_w1_in", [D, UNITS, FF])
    return w1_in, [(w1_in[:, 0, :], w["rw1"]), (w1_in[:, 1:, :], w["W1"].rearrange("e d f -> d e f"))]


def stage_experts(nc, X, ident, w, c, w1_in):
    with ExitStack() as ctx:
        mem = Memory(nc, ctx)
        sb, ps, sem = mem.sb, mem.ps, mem.sem
        w1 = [sb(f"b_w1{n}", [D, UNITS, FF], F32R) for n in ("_high", "_low")]
        b1 = sb("b_b1", [P, UNITS, FF_TILES])
        w2 = sb("b_w2", [P, EXPERTS, FF_TILES, D])
        b2 = sb("b_b2", [EXPERTS, D])
        rw2 = sb("b_rw2", [P, FF_TILES, EXPERTS])
        rb2 = sb("b_rb2", [1, EXPERTS])
        earlier = sb("b_earlier", [P, EXPERTS, EXPERTS])
        ones = sb("b_ones", [1, P])
        xn = sb("b_xn", [P, TILES, D])
        xnT = [sb(f"b_xnT{n}", [D, SEQ], F32R) for n in ("_high", "_low")]
        hidden = [sb(f"b_hidden{i}", [P, FF_TILES, SEQ]) for i in range(HIDDEN_RING)]
        score = sb("b_score", [P, TILES, EXPERTS])
        above = sb("b_above", [P, TILES, EXPERTS, EXPERTS])
        tied = sb("b_tied", [P, TILES, EXPERTS, EXPERTS])
        rank = sb("b_rank", [P, TILES, EXPERTS])
        best = sb("b_best", [P, TILES])
        shifted = sb("b_shifted", [P, TILES, EXPERTS])
        expd = sb("b_expd", [P, TILES, EXPERTS])
        chosen = sb("b_chosen", [P, TILES, EXPERTS])
        total = sb("b_total", [P, TILES])
        gate = sb("b_gate", [P, TILES, EXPERTS])
        gateT = sb("b_gateT", [EXPERTS, SEQ])

        ps_hidden = ps("b_ps_hidden", [P, FF_TILES, 512])
        ps_y = ps("b_ps_y", [P, 2, 512])
        ps_rows = ps("b_ps_rows", [P, 512])
        ps_score = ps("b_ps_score", [P, 512])

        ln = LayerNorm(mem, "b_ln")
        w_loaded, ones_ready = sem("b_w_loaded"), sem("b_ones_ready")
        router_loaded = sem("b_router_loaded")
        w_high_ready, w_ready = sem("b_w_high_ready"), sem("b_w_ready")
        xnT_made, xnT_high_ready, xnT_ready = sem("b_xnT_made"), sem("b_xnT_high_ready"), sem("b_xnT_ready")
        hidden_made = sem("b_hidden_made")
        act_rectified, dve_rectified = sem("b_act_rectified"), sem("b_dve_rectified")
        unit_done = sem("b_unit_done")
        score_ready, compared, ties_broken, rank_ready = (
            sem("b_score_ready"), sem("b_compared"), sem("b_ties_broken"), sem("b_rank_ready"))
        ties_broken_added = sem("b_ties_broken_added")
        best_ready, shifted_ready, exp_done = sem("b_best_ready"), sem("b_shifted_ready"), sem("b_exp_done")
        chosen_ready, total_ready, inverse_ready, gate_ready = (
            sem("b_chosen_ready"), sem("b_total_ready"), sem("b_inverse_ready"), sem("b_gate_ready"))
        gateT_made, gateT_ready, bias_made = sem("b_gateT_made"), sem("b_gateT_ready"), sem("b_bias_made")
        added = sem("b_added")
        ADDS = EXPERTS + 1

        router_loads = [(b1[:, :, :], w["b1"])]
        loads = [(w2[:, :, :, :].rearrange("p e f d -> p (e f) d"), w["W2"].rearrange("e (f p) d -> p (e f) d", p=P)),
                 (b2[:, :], w["b2"]), (rw2[:, :, :], w["rw2"].rearrange("(f p) e -> p f e", p=P)), (rb2[:, :], w["rb2"]),
                 (earlier[:, :, :], c["earlier"].partition_broadcast(P))]

        BIAS_AFTER, ROWS_AFTER = 2, 4

        with nc.Block() as block:

            @block.sync
            def _(sp):
                for dst, src in router_loads:
                    sp.dma_start(dst, src).then_inc(router_loaded, 16)
                for dst, src in loads:
                    sp.dma_start(dst, src).then_inc(w_loaded, 16)

            @block.gpsimd
            def _(pool):
                nc.gpsimd.memset(ones[:, :], 1.0).then_inc(ones_ready, 1)
                ln.set_up(nc, pool)
                ln.take_rstd(nc, pool, 0)
                with pool.Fori(1, BATCHES) as b:
                    ln.take_rstd(nc, pool, b)

            @block.vector
            def _(dve):
                def rows(b):
                    return lambda t: X[:, bass.ds(TILES * b + t, 1), :].rearrange("p o d -> p (o d)")

                def rectify(b, u):
                    above_zero(dve, unit_done, UNITS * b + u - 2)
                    for f in range(ACT_TILES, FF_TILES):
                        dve.wait_ge(hidden_made, FF_TILES * (UNITS * b + u) + f + 1)
                        nc.vector.tensor_scalar(hidden[u % HIDDEN_RING][:, f, :], ps_hidden[:, f, :], b1[:, u, f:f + 1],
                                                0.0, ALU.add, ALU.max).then_inc(dve_rectified, 1)

                def take_gate(b):
                    shape = [P, TILES, EXPERTS, EXPERTS]
                    dve.wait_ge(unit_done, UNITS * b + 1)
                    nc.vector.tensor_copy(score[:, :, :],
                                          ps_score[:, 0:TILES * EXPERTS].rearrange("p (t e) -> p t e", t=TILES))\
                        .then_inc(score_ready, 1)
                    dve.wait_ge(score_ready, b + 1)
                    other = score[:, :, :].unsqueeze(2).to_broadcast(shape)
                    own = score[:, :, :].unsqueeze(3).to_broadcast(shape)
                    nc.vector.tensor_tensor(above[:, :, :, :], other, own, ALU.is_gt)
                    nc.vector.tensor_tensor(tied[:, :, :, :], other, own, ALU.is_equal).then_inc(compared, 1)
                    nc.vector.tensor_reduce(best[:, :], score[:, :, :], AX.X, ALU.max).then_inc(best_ready, 1)
                    if isinstance(b, int) and b == 0:
                        dve.wait_ge(w_loaded, 16 * len(loads))
                    dve.wait_ge(compared, b + 1)
                    nc.vector.tensor_tensor(tied[:, :, :, :], tied[:, :, :, :],
                                            earlier[:, :, :].unsqueeze(1).to_broadcast(shape), ALU.mult)\
                        .then_inc(ties_broken, 1)
                    dve.wait_ge(best_ready, b + 1)
                    nc.vector.tensor_tensor(shifted[:, :, :], score[:, :, :],
                                            best[:, :].unsqueeze(2).to_broadcast([P, TILES, EXPERTS]),
                                            ALU.subtract).then_inc(shifted_ready, 1)
                    dve.wait_ge(ties_broken, b + 1)
                    nc.vector.tensor_tensor(above[:, :, :, :], above[:, :, :, :], tied[:, :, :, :], ALU.add)\
                        .then_inc(ties_broken_added, 1)
                    dve.wait_ge(ties_broken_added, b + 1)
                    nc.vector.tensor_reduce(rank[:, :, :], above[:, :, :, :], AX.X, ALU.add).then_inc(rank_ready, 1)
                    dve.wait_ge(rank_ready, b + 1)
                    dve.wait_ge(exp_done, b + 1)
                    nc.vector.scalar_tensor_tensor(chosen[:, :, :], rank[:, :, :], TOP_K - 0.5, expd[:, :, :],
                                                   ALU.is_lt, ALU.mult).then_inc(chosen_ready, 1)
                    dve.wait_ge(chosen_ready, b + 1)
                    nc.vector.tensor_reduce(total[:, :], chosen[:, :, :], AX.X, ALU.add).then_inc(total_ready, 1)
                    dve.wait_ge(total_ready, b + 1)
                    nc.vector.reciprocal(total[:, :], total[:, :]).then_inc(inverse_ready, 1)
                    dve.wait_ge(inverse_ready, b + 1)
                    above_zero(dve, gateT_made, b)
                    nc.vector.tensor_tensor(gate[:, :, :], chosen[:, :, :],
                                            total[:, :].unsqueeze(2).to_broadcast([P, TILES, EXPERTS]), ALU.mult)\
                        .then_inc(gate_ready, 1)

                def add_expert(b, e):
                    if e == 0:
                        dve.wait_ge(gate_ready, b + 1)
                    dve.wait_ge(unit_done, UNITS * b + e + 2)
                    above_zero(dve, added, ADDS * b + e + (1 if e > BIAS_AFTER else 0))
                    for t in range(TILES):
                        x = rows(b)(t)
                        last = nc.vector.scalar_tensor_tensor(x, ps_y[:, e % 2, t * D:(t + 1) * D], gate[:, t, e:e + 1],
                                                              x, ALU.mult, ALU.add)
                    last.then_inc(added, 1)

                def add_bias(b):
                    dve.wait_ge(bias_made, b + 1)
                    dve.wait_ge(added, ADDS * b + BIAS_AFTER + 1)
                    x = X[:, bass.ds(TILES * b, TILES), :]
                    nc.vector.tensor_tensor(x, ps_rows[:, :].rearrange("p (t d) -> p t d", t=TILES), x, ALU.add)\
                        .then_inc(added, 1)

                def batch(b, last):
                    rectify(b, 0)
                    rectify(b, 1)
                    take_gate(b)
                    for e in range(EXPERTS):
                        if e + 2 < UNITS:
                            rectify(b, e + 2)
                        add_expert(b, e)
                        if e == BIAS_AFTER:
                            add_bias(b)
                        if e == ROWS_AFTER and not last:
                            dve.wait_ge(xnT_made, b + 1)
                            ln.run(nc, dve, rows(b + 1), xn, b + 1)
                    if not last:
                        rows_rest(b + 1)

                def rows_rest(b):
                    dve.wait_ge(xnT_high_ready, b + 1)
                    nc.vector.tensor_tensor(xnT[1][:, :], ps_rows[:, :], xnT[0][:, :], ALU.subtract).then_inc(xnT_ready, 1)

                ln.run(nc, dve, rows(0), xn, 0)
                rows_rest(0)
                dve.wait_ge(router_loaded, 16 * len(router_loads))
                for u in range(UNITS):
                    nc.vector.tensor_copy(w1[0][:, u, :], w1_in[:, u, :]).then_inc(w_high_ready, 1)
                    dve.wait_ge(w_high_ready, u + 1)
                    nc.vector.tensor_tensor(w1[1][:, u, :], w1_in[:, u, :], w1[0][:, u, :], ALU.subtract).then_inc(w_ready, 1)
                batch(0, False)
                with dve.Fori(1, BATCHES - 1) as b:
                    batch(b, False)
                batch(BATCHES - 1, True)

            @block.scalar
            def _(act):
                def rectify(b, u):
                    above_zero(act, unit_done, UNITS * b + u - 2)
                    for f in range(ACT_TILES):
                        act.wait_ge(hidden_made, FF_TILES * (UNITS * b + u) + f + 1)
                        nc.scalar.activation(hidden[u % HIDDEN_RING][:, f, :], ps_hidden[:, f, :], ACT.Relu,
                                             bias=b1[:, u, f:f + 1]).then_inc(act_rectified, 1)

                def rows_to_sbuf(b):
                    act.wait_ge(xnT_made, b + 1)
                    above_zero(act, hidden_made, FF_TILES * UNITS * b)
                    nc.scalar.activation(xnT[0][:, :], ps_rows[:, :], ACT.Copy).then_inc(xnT_high_ready, 1)

                def batch(b, last):
                    rectify(b, 0)
                    rectify(b, 1)
                    act.wait_ge(shifted_ready, b + 1)
                    nc.scalar.activation(expd[:, :, :], shifted[:, :, :], ACT.Exp).then_inc(exp_done, 1)
                    for u in range(2, UNITS):
                        rectify(b, u)
                        if u == BIAS_AFTER + 2:
                            act.wait_ge(gateT_made, b + 1)
                            nc.scalar.activation(gateT[:, :], ps_rows[0:EXPERTS, :], ACT.Copy).then_inc(gateT_ready, 1)
                    if not last:
                        rows_to_sbuf(b + 1)

                rows_to_sbuf(0)
                act.wait_ge(router_loaded, 16 * len(router_loads))
                batch(0, False)
                with act.Fori(1, BATCHES - 1) as b:
                    batch(b, False)
                batch(BATCHES - 1, True)

            @block.tensor
            def _(pe):
                mm = nc.tensor.matmul

                def turn_rows(b):
                    pe.wait_ge(ln.ready, b + 1)
                    above_zero(pe, added, ADDS * (b - 1) + BIAS_AFTER + 2 if not isinstance(b, int) or b else 0)
                    for t in range(TILES):
                        last = nc.tensor.transpose(ps_rows[:, t * P:(t + 1) * P], xn[:, t, :], ident[:, :])
                    last.then_inc(xnT_made, 1)

                def first_layer(b, u):
                    if isinstance(b, int) and b == 0:
                        pe.wait_ge(w_ready, u + 1)
                    for f in range(FF_TILES):
                        if f < ACT_TILES:
                            above_zero(pe, act_rectified, ACT_TILES * (UNITS * b + u - 1) + f + 1 if not (isinstance(b, int) and b == 0 and u == 0) else 0)
                        else:
                            above_zero(pe, dve_rectified, (FF_TILES - ACT_TILES) * (UNITS * b + u - 1) + f - ACT_TILES + 1)
                        left = [part[:, u, f * P:(f + 1) * P] for part in w1]
                        mm(ps_hidden[:, f, :], left[0], xnT[0][:, :], start=True, stop=False)
                        mm(ps_hidden[:, f, :], left[0], xnT[1][:, :], start=False, stop=False)
                        mm(ps_hidden[:, f, :], left[1], xnT[0][:, :], start=False, stop=True).then_inc(hidden_made, 1)

                def second_layer(b, u):
                    pe.wait_ge(act_rectified, ACT_TILES * (UNITS * b + u + 1))
                    pe.wait_ge(dve_rectified, (FF_TILES - ACT_TILES) * (UNITS * b + u + 1))
                    h, e = hidden[u % HIDDEN_RING], u - 1
                    if u == 0:
                        above_zero(pe, score_ready, b)
                    else:
                        if e >= 2:
                            above_zero(pe, added, ADDS * b + e - 1 + (1 if e - 2 > BIAS_AFTER else 0))
                        else:
                            above_zero(pe, added, ADDS * b)
                    for t in range(TILES):
                        for f in range(FF_TILES):
                            if u == 0:
                                mm(ps_score[:, t * EXPERTS:(t + 1) * EXPERTS], h[:, f, t * P:(t + 1) * P], rw2[:, f, :],
                                   start=(f == 0), stop=False)
                            else:
                                last = mm(ps_y[:, e % 2, t * D:(t + 1) * D], h[:, f, t * P:(t + 1) * P], w2[:, e, f, :],
                                          start=(f == 0), stop=(f == FF_TILES - 1))
                        if u == 0:
                            last = mm(ps_score[:, t * EXPERTS:(t + 1) * EXPERTS], ones[:, :], rb2[:, :],
                                      start=False, stop=True)
                    last.then_inc(unit_done, 1)

                def gated_bias(b):
                    pe.wait_ge(gate_ready, b + 1)
                    for t in range(TILES):
                        last = nc.tensor.transpose(ps_rows[0:EXPERTS, t * P:(t + 1) * P], gate[:, t, :], ident[:, :])
                    last.then_inc(gateT_made, 1)
                    pe.wait_ge(gateT_ready, b + 1)
                    for t in range(TILES):
                        last = mm(ps_rows[:, t * D:(t + 1) * D], gateT[:, t * P:(t + 1) * P], b2[:, :], start=True, stop=True)
                    last.then_inc(bias_made, 1)

                def batch(b, last):
                    pe.wait_ge(xnT_ready, b + 1)
                    first_layer(b, 0)
                    for u in range(1, UNITS):
                        first_layer(b, u)
                        if isinstance(b, int) and b == 0 and u == 1:
                            pe.wait_ge(w_loaded, 16 * len(loads))
                        if u == UNITS - 1 and not last:
                            turn_rows(b + 1)
                        second_layer(b, u - 1)
                        if u - 2 == BIAS_AFTER:
                            gated_bias(b)
                    second_layer(b, UNITS - 1)

                pe.wait_ge(ones_ready, 1)
                turn_rows(0)
                batch(0, False)
                with pe.Fori(1, BATCHES - 1) as b:
                    batch(b, False)
                batch(BATCHES - 1, True)


CHEADS = 16
CHD = 64
CINNER = CHEADS * CHD
PAIR_TILES = CINNER // P
NORM_FLOOR = 1e-12
MAX_SCALE = 100.0
LOG_MAX_SCALE = math.log(MAX_SCALE)
EXP_ROOM = 75.0
BANK_HEADS = 512 // CHD
BANK_PAIRS = 512 // P
RAWS = 4
QK_TILES = 2 * PAIR_TILES
QK_BANKS = 2 * CINNER // 512
V_BANKS = TILES * CINNER // 512
VC = CHD + 1
STEPS = CHEADS
LEAD = 2
UNIT = 256.0
STATISTICS_STEP = 7
NORMALISE_STEP = 9
TURN_STEP = STEPS - LEAD - 1


def stage_cosine_attention(nc, X, ident, w, c):
    with ExitStack() as ctx:
        mem = Memory(nc, ctx)
        sb, ps, sem = mem.sb, mem.ps, mem.sem
        w_qk = [sb(f"c_w_qk{n}", [D, 2 * CINNER], F32R) for n in ("_high", "_low")]
        w_v = [sb(f"c_w_v{n}", [D, CINNER], F32R) for n in ("_high", "_low")]
        w_out = sb("c_w_out", [VC, CHEADS, D + 1])
        b_out = sb("c_b_out", [P, D])
        log_scale = sb("c_log_scale", [P, CHEADS])
        scale = sb("c_scale", [P, CHEADS])
        unit_scale = sb("c_unit_scale", [P, CHEADS])
        shift = sb("c_shift", [P, CHEADS])
        xn = sb("c_xn", [P, TILES, D])
        xnT = [[sb(f"c_xnT{i}{n}", [D, SEQ], F32R) for n in ("_high", "_low")] for i in range(2)]
        raw = [sb(f"c_raw{i}", [P, SEQ]) for i in range(RAWS)]
        square = [sb(f"c_square{i}", [P, SEQ]) for i in range(2)]
        norm2 = [sb(f"c_norm2{i}", [P, BANK_HEADS]) for i in range(2)]
        power = sb("c_power", [P, BANK_HEADS])
        inverse = [sb(f"c_inverse{i}", [P, BANK_HEADS]) for i in range(2)]
        keys = [sb(f"c_keys{i}", [P, PAIR_TILES, 2, SEQ], F16) for i in range(2)]
        queries = [sb(f"c_queries{i}", [P, PAIR_TILES, 2, SEQ], F16) for i in range(2)]
        queries_low = [sb(f"c_queries_low{i}", [P, PAIR_TILES, SEQ], F16) for i in range(2)]
        v = sb("c_v", [P, TILES, CHEADS, VC])
        probs = [sb(f"c_probs{i}", [P, TILES, SEQ]) for i in range(2)]
        w_qk_in, w_v_in = probs[0][:, :, :].rearrange("p t k -> p (t k)"), probs[1][:, 0:2, :].rearrange("p t k -> p (t k)")
        outT = [sb(f"c_outT{i}", [VC, SEQ]) for i in range(2)]
        rsum = sb("c_rsum", [P, 2])

        ps_scores = ps("c_ps_scores", [P, TILES, 512])
        ps_out = ps("c_ps_out", [P, 512])
        ps_front = ps("c_ps_front", [P, 512])
        ps_y = ps("c_ps_y", [P, 2, 512])

        ln = LayerNorm(mem, "c_ln")
        w_loaded, set_up = sem("c_w_loaded"), sem("c_set_up")
        w_high_ready, w_ready = sem("c_w_high_ready"), sem("c_w_ready")
        xnT_high_ready, qkT_high_ready = sem("c_xnT_high_ready"), sem("c_qkT_high_ready")
        queries_doubled = sem("c_queries_doubled")
        limited, scale_ready, shifted, shift_ready = sem("c_limited"), sem("c_scale_ready"), sem("c_shifted"), sem("c_shift_ready")
        xnT_made, xnT_ready, bias_added = sem("c_xnT_made"), sem("c_xnT_ready"), sem("c_bias_added")
        tile_made, raw_ready, square_ready = sem("c_tile_made"), sem("c_raw_ready"), sem("c_square_ready")
        norm2_ready, limited_ready, inverse_ready, unit_ready, turned, qkT_ready = (
            sem("c_norm2_ready"), sem("c_limited_ready"), sem("c_inverse_ready"), sem("c_unit_ready"), sem("c_turned"), sem("c_qkT_ready"))
        v_made, v_ready = sem("c_v_made"), sem("c_v_ready")
        scores_made, exp_done = sem("c_scores_made"), sem("c_exp_done")
        out_made, outT_ready = sem("c_out_made"), sem("c_outT_ready")
        act_outT_ready = sem("c_act_outT_ready")
        y_made, rsum_ready, y_added = sem("c_y_made"), sem("c_rsum_ready"), sem("c_y_added")

        loads = [(w_qk_in, w["qkv"][:, 0:2 * CINNER]), (w_v_in, w["qkv"][:, 2 * CINNER:]),
                 (w_out[:, :, :], w["out"]), (b_out[:, :], w["b_out"].partition_broadcast(P)),
                 (log_scale[:, :], w["log_scale"].partition_broadcast(P))]

        ROWS_OF = (slice(0, CHD), slice(CHD, P))

        def turn_bank(back):
            return ps_out if back is None else ps_front

        def place(i):
            t, g = i // QK_BANKS, i % QK_BANKS
            is_key, g = g >= QK_BANKS // 2, g % (QK_BANKS // 2)
            return slice(g * BANK_PAIRS, (g + 1) * BANK_PAIRS), slice(t * P, (t + 1) * P), is_key

        def values_piece(front, back, s):
            half = 1 if s < STEPS // 2 else 0
            b = back if half else front
            if s % 2 == 0 or b is None:
                return None
            t = s % (STEPS // 2) // 2
            return b, t, half, V_BANKS * b + TILES * half + t

        def pipeline(eng, step):
            step(0, None, None, None, 1)
            step(1, 0, None, None, 0)
            step(2, 1, 0, None, 1)
            with eng.Fori(0, (BATCHES - 4) // 2) as i:
                step(2 * i + 3, 2 * i + 2, 2 * i + 1, 2 * i, 0)
                step(2 * i + 4, 2 * i + 3, 2 * i + 2, 2 * i + 1, 1)
            step(BATCHES - 1, BATCHES - 2, BATCHES - 3, BATCHES - 4, 0)
            step(None, BATCHES - 1, BATCHES - 2, BATCHES - 3, 1)
            step(None, None, BATCHES - 1, BATCHES - 2, 0)
            step(None, None, None, BATCHES - 1, 1)

        def piece(after, front, i):
            b, i = (front, i) if i < QK_TILES else (after, i - QK_TILES)
            return None if b is None else (b, i, QK_TILES * b + i)

        def head(back, old, h):
            b, h = (back, h) if h >= 0 else (old, h + CHEADS)
            return None if b is None else (b, h, CHEADS * b + h)

        with nc.Block() as block:

            @block.sync
            def _(sp):
                for dst, src in loads:
                    sp.dma_start(dst, src).then_inc(w_loaded, 16)

            @block.gpsimd
            def _(pool):
                nc.gpsimd.memset(power[:, :], -0.5).then_inc(set_up, 1)
                nc.gpsimd.memset(v[:, :, :, CHD:VC], 1.0).then_inc(set_up, 1)
                ln.set_up(nc, pool)
                pool.wait_ge(set_up, 2)

                def add_bias(b):
                    if isinstance(b, int) and b == 0:
                        pool.wait_ge(w_loaded, 16 * len(loads))
                    pool.wait_ge(ln.ready, b + 1)
                    x = X[:, bass.ds(TILES * b, TILES), :]
                    nc.gpsimd.tensor_tensor(x, x, b_out[:, :].unsqueeze(1).to_broadcast([P, TILES, D]), ALU.add)\
                        .then_inc(bias_added, 1)

                def step(after, b, bb, old, par):
                    for s in range(STEPS):
                        if after is not None and s == NORMALISE_STEP + 1:
                            add_bias(after)
                        made, summed = piece(after, b, s + LEAD), piece(after, b, s + 1)
                        if made:
                            _, i, seen = made
                            pool.wait_ge(raw_ready, seen + 1)
                            above_zero(pool, norm2_ready, seen - 1)
                            nc.gpsimd.tensor_tensor(square[i % 2][:, :], raw[i % RAWS][:, :],
                                                    raw[i % RAWS][:, :], ALU.mult).then_inc(square_ready, 1)
                        if summed:
                            _, i, seen = summed
                            pool.wait_ge(limited_ready, seen + 1)
                            above_zero(pool, unit_ready, seen - 1)
                            nc.gpsimd.tensor_tensor(inverse[i % 2][:, :], norm2[i % 2][:, :], power[:, :], ALU.pow)\
                                .then_inc(inverse_ready, 1)
                        if after is not None and s == STATISTICS_STEP:
                            ln.take_rstd(nc, pool, after)

                pipeline(pool, step)

            @block.vector
            def _(dve):
                def rows_of(b):
                    return lambda t: X[:, bass.ds(TILES * b + t, 1), :].rearrange("p o d -> p (o d)")

                def step(after, b, bb, old, par):
                    for s in range(STEPS):
                        done, summed = head(bb, old, s - 2), piece(after, b, s + 1)
                        if summed:
                            square_sum(*summed)
                        if b is not None:
                            unit_length(b, s)
                        if done:
                            add_head(*done, 0)
                            add_head(*done, 1)
                        if b is not None:
                            piece_to_sbuf(b, bb, par, s)
                        if done:
                            add_head(*done, 2)
                            add_head(*done, 3)
                        if s % 2 == 0 and head(bb, old, s - 1):
                            head_to_sbuf(*head(bb, old, s - 1))
                        if after is not None and s == STATISTICS_STEP:
                            ln.take_statistics(nc, dve, rows_of(after), after)
                        if after is not None and s == NORMALISE_STEP:
                            above_zero(dve, xnT_made, after)
                            ln.normalise(nc, dve, rows_of(after), xn, after)
                            if b is None:
                                prepare_weights()
                        if after is not None and s == TURN_STEP:
                            low, high = xnT[1 - par][1], xnT[1 - par][0]
                            dve.wait_ge(xnT_high_ready, after + 1)
                            nc.vector.tensor_tensor(low[:, :], ps_front[:, :], high[:, :], ALU.subtract).then_inc(xnT_ready, 1)

                def prepare_weights():
                    dve.wait_ge(w_loaded, 16 * len(loads))
                    for i, (part, whole) in enumerate(((w_qk, w_qk_in), (w_v, w_v_in))):
                        nc.vector.tensor_copy(part[0][:, :], whole).then_inc(w_high_ready, 1)
                        dve.wait_ge(w_high_ready, i + 1)
                        nc.vector.tensor_tensor(part[1][:, :], whole, part[0][:, :], ALU.subtract).then_inc(w_ready, 1)
                    nc.vector.tensor_scalar(log_scale[:, :], log_scale[:, :], LOG_MAX_SCALE, None, ALU.min).then_inc(limited, 1)
                    dve.wait_ge(scale_ready, 1)
                    nc.vector.tensor_scalar(unit_scale[:, :], scale[:, :], UNIT ** -2, None, ALU.mult).then_inc(shifted, 1)
                    nc.vector.tensor_scalar(shift[:, :], scale[:, :], -1.0, EXP_ROOM, ALU.mult, ALU.add).then_inc(shifted, 1)
                    dve.wait_ge(shifted, 2)
                    nc.vector.tensor_scalar(shift[:, :], shift[:, :], 0.0, None, ALU.min).then_inc(shift_ready, 1)

                def square_sum(b, i, seen):
                    dve.wait_ge(square_ready, seen + 1)
                    above_zero(dve, inverse_ready, seen - 1)
                    nc.vector.tensor_reduce(norm2[i % 2][:, :], square[i % 2][:, :].rearrange("p (h d) -> p h d", d=CHD),
                                            AX.X, ALU.add).then_inc(norm2_ready, 1)
                    dve.wait_ge(norm2_ready, seen + 1)
                    nc.vector.tensor_scalar(norm2[i % 2][:, :], norm2[i % 2][:, :], NORM_FLOOR ** 2, UNIT ** -2, ALU.max, ALU.mult)\
                        .then_inc(limited_ready, 1)

                def unit_length(b, i):
                    dve.wait_ge(inverse_ready, QK_TILES * b + i + 1)
                    rows = raw[i % RAWS][:, :].rearrange("p (h d) -> p h d", d=CHD)
                    nc.vector.tensor_tensor(rows, rows, inverse[i % 2][:, :].unsqueeze(2).to_broadcast([P, BANK_HEADS, CHD]),
                                            ALU.mult).then_inc(unit_ready, 1)

                def piece_to_sbuf(b, bb, par, i):
                    pairs, tokens, is_key = place(i)
                    whole = turn_bank(bb)[:, :].rearrange("p (j t) -> p j t", j=BANK_PAIRS)
                    high = (keys if is_key else queries)[par]
                    dve.wait_ge(qkT_high_ready, QK_TILES * b + i + 1)
                    for odd in range(2):
                        own, other = ROWS_OF[odd], ROWS_OF[1 - odd]
                        low = keys[par][other, pairs, odd, tokens] if is_key else queries_low[par][own, pairs, tokens]
                        last = nc.vector.tensor_tensor(low, whole[own, :, :], high[own, pairs, odd, tokens], ALU.subtract)
                    last.then_inc(qkT_ready, 1)
                    if not is_key:
                        for odd in range(2):
                            last = nc.vector.tensor_copy(high[ROWS_OF[1 - odd], pairs, odd, tokens],
                                                         high[ROWS_OF[odd], pairs, odd, tokens])
                        last.then_inc(queries_doubled, 1)

                def add_head(b, h, number, t):
                    seen = TILES * number + t
                    if h == 0 and t == 0:
                        dve.wait_ge(bias_added, b + 1)
                    dve.wait_ge(y_made, seen + 1)
                    nc.vector.reciprocal(rsum[:, t % 2:t % 2 + 1], ps_y[:, t % 2, D:D + 1]).then_inc(rsum_ready, 1)
                    dve.wait_ge(rsum_ready, seen + 1)
                    x = X[:, bass.ds(TILES * b + t, 1), :].rearrange("p o d -> p (o d)")
                    above_zero(dve, y_added, seen - TILES + 1)
                    nc.vector.scalar_tensor_tensor(x, ps_y[:, t % 2, 0:D], rsum[:, t % 2:t % 2 + 1], x, ALU.mult, ALU.add)\
                        .then_inc(y_added, 1)

                def head_to_sbuf(b, h, number):
                    dve.wait_ge(out_made, number + 1)
                    above_zero(dve, y_made, TILES * (number - 1))
                    nc.vector.tensor_copy(outT[h % 2][:, :], ps_out[0:VC, :]).then_inc(outT_ready, 1)

                pipeline(dve, step)

            @block.scalar
            def _(act):
                act.wait_ge(limited, 1)
                nc.scalar.activation(scale[:, :], log_scale[:, :], ACT.Exp).then_inc(scale_ready, 1)
                act.wait_ge(scale_ready, 1)
                act.wait_ge(shift_ready, 1)
                act.wait_ge(w_ready, 2)

                def piece_to_sbuf(b, bb, par, i):
                    pairs, tokens, is_key = place(i)
                    whole = turn_bank(bb)[:, :].rearrange("p (j t) -> p j t", j=BANK_PAIRS)
                    high = (keys if is_key else queries)[par]
                    act.wait_ge(turned, QK_TILES * b + i + 1)
                    for odd in range(2):
                        own = ROWS_OF[odd]
                        last = nc.scalar.activation(high[own, pairs, odd, tokens], whole[own, :, :], ACT.Copy)
                    last.then_inc(qkT_high_ready, 1)

                def exponentials(bb, h, half):
                    act.wait_ge(scores_made, 2 * (CHEADS * bb + h) + half + 1)
                    above_zero(act, out_made, CHEADS * bb + h - 1)
                    nc.scalar.activation(probs[h % 2][:, 2 * half:2 * half + 2, :], ps_scores[:, 2 * half:2 * half + 2, :],
                                         ACT.Exp, bias=shift[:, h:h + 1], scale=unit_scale[:, h:h + 1]).then_inc(exp_done, 1)

                def step(after, b, bb, old, par):
                    for s in range(STEPS):
                        made = piece(after, b, s + LEAD)
                        if bb is not None:
                            exponentials(bb, s, 0)
                        if made:
                            _, i, seen = made
                            act.wait_ge(tile_made, seen + 1)
                            above_zero(act, turned, seen - RAWS + 1)
                            nc.scalar.activation(raw[i % RAWS][:, :], ps_front[:, :], ACT.Copy).then_inc(raw_ready, 1)
                        if bb is not None:
                            exponentials(bb, s, 1)
                        if b is not None:
                            piece_to_sbuf(b, bb, par, s)
                        if bb is not None and s % 2 == 1:
                            seen = CHEADS * bb + s - 1
                            act.wait_ge(out_made, seen + 1)
                            above_zero(act, y_made, TILES * (seen - 1))
                            nc.scalar.activation(outT[(s - 1) % 2][:, :], ps_out[0:VC, :], ACT.Copy).then_inc(act_outT_ready, 1)
                        values = values_piece(b, bb, s)
                        if values:
                            _, t, half, seen = values
                            act.wait_ge(v_made, seen + 1)
                            if half:
                                above_zero(act, out_made, CHEADS * bb)
                            elif bb is not None:
                                act.wait_ge(out_made, CHEADS * bb + CHEADS // 2)
                            heads = slice(half * BANK_HEADS, (half + 1) * BANK_HEADS)
                            nc.scalar.activation(v[:, t, heads, 0:CHD], ps_front[:, :].rearrange("p (h d) -> p h d", d=CHD),
                                                 ACT.Copy).then_inc(v_ready, 1)
                        if after is not None and s == TURN_STEP:
                            act.wait_ge(xnT_made, after + 1)
                            nc.scalar.activation(xnT[1 - par][0][:, :], ps_front[:, :], ACT.Copy).then_inc(xnT_high_ready, 1)

                pipeline(act, step)

            @block.tensor
            def _(pe):
                mm = nc.tensor.matmul
                pe.wait_ge(w_loaded, 16 * len(loads))
                pe.wait_ge(set_up, 2)
                pe.wait_ge(w_ready, 2)

                def in_parts(out, left, right):
                    mm(out, left[0], right[0], start=True, stop=False)
                    mm(out, left[0], right[1], start=False, stop=False)
                    return mm(out, left[1], right[0], start=False, stop=True)

                def scores(bb, par, h, half):
                    own, pair, odd = ROWS_OF[h % 2], h // 2, h % 2
                    above_zero(pe, exp_done, 2 * (CHEADS * bb + h) + half - 1)
                    for kt in range(2 * half, 2 * half + 2):
                        key, out = keys[par][:, pair, odd, kt * P:(kt + 1) * P], ps_scores[:, kt, :]
                        mm(out, key, queries[par][:, pair, odd, :], start=True, stop=False)
                        last = mm(out, keys[par][own, pair, odd, kt * P:(kt + 1) * P], queries_low[par][own, pair, :],
                                  start=False, stop=True)
                    last.then_inc(scores_made, 1)

                def attend(bb, h):
                    pe.wait_ge(exp_done, 2 * (CHEADS * bb + h + 1))
                    if h % BANK_HEADS == 0:
                        pe.wait_ge(v_ready, V_BANKS * bb + TILES * (h // BANK_HEADS + 1))
                    head_there(bb, h - 1)
                    for kt in range(TILES):
                        last = mm(ps_out[0:VC, :], v[:, kt, h, :], probs[h % 2][:, kt, :],
                                  start=(kt == 0), stop=(kt == TILES - 1))
                    last.then_inc(out_made, 1)

                def head_there(bb, h):
                    half = CHEADS // 2
                    if h < 0:
                        above_zero(pe, outT_ready, half * bb)
                    elif h % 2:
                        pe.wait_ge(outT_ready, half * bb + h // 2 + 1)
                    else:
                        pe.wait_ge(act_outT_ready, half * bb + h // 2 + 1)

                def project(bb, h, number, t):
                    seen = TILES * number + t
                    if t == 0:
                        head_there(bb, h)
                    above_zero(pe, y_added, seen - 1)
                    mm(ps_y[:, t % 2, 0:D + 1], outT[h % 2][:, t * P:(t + 1) * P], w_out[:, h, :], start=True, stop=True)\
                        .then_inc(y_made, 1)

                def last_step_left(b, bb, s):
                    values = values_piece(b, bb, s - 1)
                    if values:
                        pe.wait_ge(v_ready, values[3] + 1)
                    elif bb is None:
                        pe.wait_ge(raw_ready, QK_TILES * b + s + LEAD)
                    else:
                        pe.wait_ge(qkT_ready, QK_TILES * b + s)

                def make_piece(after, b, bb, par, s):
                    owner, i, _ = piece(after, b, s + LEAD)
                    source = xnT[par] if owner is b else xnT[1 - par]
                    if s == 0:
                        pe.wait_ge(raw_ready, QK_TILES * b + LEAD)
                        if bb is not None:
                            pe.wait_ge(v_ready, V_BANKS * bb + TILES)
                    elif s == TURN_STEP + 1:
                        pe.wait_ge(xnT_ready, after + 1)
                    elif b is None:
                        pe.wait_ge(raw_ready, QK_TILES * after + i)
                    else:
                        last_step_left(b, bb, s)
                    t, g = i // QK_BANKS, i % QK_BANKS
                    in_parts(ps_front[:, :], [part[:, t * P:(t + 1) * P] for part in source],
                             [part[:, g * 512:(g + 1) * 512] for part in w_qk]).then_inc(tile_made, 1)

                def turn_piece(after, b, bb, s):
                    pe.wait_ge(unit_ready, QK_TILES * b + s + 1)
                    if bb is None:
                        above_zero(pe, qkT_ready, QK_TILES * b + s)
                    elif piece(after, b, s + LEAD):
                        pe.wait_ge(raw_ready, QK_TILES * b + s + LEAD + 1)
                    else:
                        last_step_left(b, bb, s)
                    for j in range(BANK_PAIRS):
                        last = nc.tensor.transpose(turn_bank(bb)[:, j * P:(j + 1) * P], raw[s % RAWS][:, j * P:(j + 1) * P], ident[:, :])
                    last.then_inc(turned, 1)

                def step(after, b, bb, old, par):
                    for s in range(STEPS):
                        projected, attended = head(bb, old, s - 2), head(bb, old, s - 1)
                        if bb is not None and s == 0:
                            pe.wait_ge(qkT_ready, QK_TILES * (bb + 1))
                            pe.wait_ge(queries_doubled, QK_TILES // 2 * (bb + 1))
                        if bb is not None:
                            scores(bb, 1 - par, s, 0)
                        if piece(after, b, s + LEAD):
                            make_piece(after, b, bb, par, s)
                        if projected:
                            project(*projected, 0)
                        if bb is not None:
                            scores(bb, 1 - par, s, 1)
                        if projected:
                            project(*projected, 1)
                        if b is not None:
                            turn_piece(after, b, bb, s)
                        if projected:
                            project(*projected, 2)
                        if attended:
                            attend(attended[0], attended[1])
                        if projected:
                            project(*projected, 3)
                        values = values_piece(b, bb, s)
                        if values:
                            _, t, half, _ = values
                            source = xnT[1 - par if half else par]
                            if bb is None:
                                pe.wait_ge(raw_ready, QK_TILES * b + s + LEAD + 1)
                            elif b is not None:
                                pe.wait_ge(qkT_ready, QK_TILES * b + s + 1)
                            elif s > 1:
                                pe.wait_ge(v_ready, V_BANKS * bb + TILES + t)
                            in_parts(ps_front[:, :], [part[:, t * P:(t + 1) * P] for part in source],
                                     [part[:, half * 512:(half + 1) * 512] for part in w_v]).then_inc(v_made, 1)
                        if after is not None and s == TURN_STEP:
                            pe.wait_ge(ln.ready, after + 1)
                            if b is not None:
                                pe.wait_ge(v_ready, values[3] + 1)
                            for t in range(TILES):
                                last = nc.tensor.transpose(ps_front[:, t * P:(t + 1) * P], xn[:, t, :], ident[:, :])
                            last.then_inc(xnT_made, 1)

                pipeline(pe, step)


SEXPERTS = 64
SLOTS = 32
ALL_SLOTS = SEXPERTS * SLOTS
SLOT_TILES = ALL_SLOTS // P
TILE_EXPERTS = P // SLOTS
ROW_TILES = BATCHES * TILES
HALF = ALL_SLOTS // 2
BANK = 512
BANKS = ALL_SLOTS // BANK
BANK_TILES = BANK // P
SLOT_LOW, SLOT_HIGH = -33000.0, 65000.0


def stage_slots(nc, X, ident, w, c, out):
    with ExitStack() as whole:
        mem = Memory(nc, whole)
        sb, ps, sem = mem.sb, mem.ps, mem.sem
        phiT = [sb(f"d_phiT{n}", [D, ALL_SLOTS], F32R) for n in ("_high", "_low")]
        bias = sb("d_bias", [3, ALL_SLOTS], BF16)
        ones = sb("d_ones", [3, P], BF16)
        xnT = sb("d_xnT", [D, ROW_TILES * P])
        rowsT = [[sb(f"d_rowsT{i}{n}", [D, P], F32R) for n in ("_high", "_low")] for i in range(3)]
        expd = [sb(f"d_expd{i}", [P, ALL_SLOTS]) for i in range(2)]
        slot_out = sb("d_slot_out", [P, SLOT_TILES, D])
        bias_row, bias_rest = expd[0][0:1, :], expd[1][0:1, :]
        peak = sb("d_peak", [P, 2, SEXPERTS // 2])
        total = sb("d_total", [P, 2, SEXPERTS // 2])
        w_loaded, experts_loaded = sem("d_w_loaded"), sem("d_experts_loaded")
        bias_split, bias_loaded = sem("d_bias_split"), sem("d_bias_loaded")
        ones_ready = sem("d_ones_ready")

        def logits(mm, ps_logits, rows, bank):
            cols = slice(bank * BANK, (bank + 1) * BANK)
            mm(ps_logits[:, cols], rows[0][:, :], phiT[0][:, cols], start=True, stop=False)
            mm(ps_logits[:, cols], rows[0][:, :], phiT[1][:, cols], start=False, stop=False)
            mm(ps_logits[:, cols], rows[1][:, :], phiT[0][:, cols], start=False, stop=False)
            return mm(ps_logits[:, cols], ones[:, :], bias[:, cols], start=False, stop=True)

        def tiles_in_pairs(eng, step, lag):
            for n in range(4):
                step(n, n % 2)
            with eng.Fori(2, ROW_TILES // 2 - 1) as i:
                step(2 * i, 0)
                step(2 * i + 1, 1)
            for n in range(ROW_TILES - 2, ROW_TILES + lag):
                step(n, n % 2)

        def tiles_in_threes(eng, step, lag):
            for n in range(4):
                step(n, n % 3)
            with eng.Fori(0, (ROW_TILES - 7) // 3) as i:
                for j in range(4, 7):
                    step(3 * i + j, j % 3)
            for n in range(ROW_TILES - 3, ROW_TILES + lag):
                step(n, n % 3)

        def rows_rest(pool, sems, n, i):
            high_ready, ready = sems
            pool.wait_ge(high_ready, n + 1)
            nc.gpsimd.tensor_tensor(rowsT[i][1][:, :], xnT[:, bass.ds(P * n, P)], rowsT[i][0][:, :], ALU.subtract)\
                .then_inc(ready, 1)

        def there(n):
            return not isinstance(n, int) or 0 <= n < ROW_TILES

        with ExitStack() as ctx:
            mem = Memory(nc, ctx)
            sb, ps, sem = mem.sb, mem.ps, mem.sem
            xn_all = sb("d_xn_all", [P, ROW_TILES, D])
            expert_w = sb("d_expert_w", [D, SEXPERTS, D])
            expert_b = sb("d_expert_b", [P, SLOT_TILES, D])
            zeros = sb("d_zeros", [P, BANK], BF16)
            slots = sb("d_slots", [P, SLOT_TILES, D])
            expd3 = [*expd, sb("d_expd2", [P, ALL_SLOTS])]
            phiT_in = expd3[2]
            stats = sb("d_slot_stats", [P, SLOT_TILES, 6])
            mv = sb("d_slot_mv", [P, SLOT_TILES, 2])
            var = sb("d_slot_var", [P, SLOT_TILES])
            power = sb("d_slot_power", [P, 2, SLOT_TILES])
            rstd = sb("d_slot_rstd", [P, SLOT_TILES])
            first_parts = slot_out[0:1, :, :].rearrange("p s d -> p (s d)").bitcast(BF16)
            bias_parts = [first_parts[:, 0:ALL_SLOTS], first_parts[:, ALL_SLOTS:2 * ALL_SLOTS],
                          slots[0:1, :, :].rearrange("p s d -> p (s d)").bitcast(BF16)[:, 0:ALL_SLOTS]]
            ps_logits = ps("d_ps_logits", [P, ALL_SLOTS])
            ps_slots = ps("d_ps_slots", [P, SLOT_TILES, D])

            LN_GROUPS = 4
            GROUP_BATCHES = BATCHES // LN_GROUPS
            ln = LayerNorm(mem, "d_ln", GROUP_BATCHES * TILES)
            xnT_made, xnT_ready = sem("d_xnT_made"), sem("d_xnT_ready")
            zeros_ready, rowsT_high_ready, rowsT_ready = sem("d_zeros_ready"), sem("d_rowsT_high_ready"), sem("d_rowsT_ready")
            phiT_high_ready, phiT_ready = sem("d_phiT_high_ready"), sem("d_phiT_ready")
            logits_made, peak_ready, shifted, exp_done = (
                sem("d_logits_made"), sem("d_peak_ready"), sem("d_shifted"), sem("d_exp_done"))
            total_ready, inverse_ready, weights_ready, mixed = (
                sem("d_total_ready"), sem("d_inverse_ready"), sem("d_weights_ready"), sem("d_mixed"))
            slots_made = sem("d_slots_made")
            clipped, slot_stats, slot_mv, slot_var, slot_rstd, slot_normed, slot_tanh = (
                sem(f"d_{n}") for n in ("clipped", "slot_stats_ready", "slot_mv_ready", "slot_var_ready", "slot_rstd_ready",
                                        "slot_normed", "slot_tanh"))
            slotsT_made, slotsT_ready, experts_made, slot_out_ready = (
                sem(f"d_{n}") for n in ("slotsT_made", "slotsT_ready", "experts_made", "slot_out_ready"))
            slotsT = expd[0]

            loads = [(phiT_in[:, :], w["phiT"]), (bias_row, w["phi_b"])]

            with nc.Block() as block:

                @block.sync
                def _(sp):
                    for dst, src in loads:
                        sp.dma_start(dst, src).then_inc(w_loaded, 16)
                    sp.wait_ge(bias_split, 5)
                    for part in range(3):
                        sp.dma_start(bias[part:part + 1, :], bias_parts[part]).then_inc(bias_loaded, 16)
                    for j in range(TILE_EXPERTS):
                        src = w["expert_b"].rearrange("(s j) h -> j s h", j=TILE_EXPERTS)[j]
                        sp.dma_start(expert_b[j * SLOTS:(j + 1) * SLOTS, :, :], src.partition_broadcast(SLOTS))\
                            .then_inc(experts_loaded, 16)
                    sp.dma_start(expert_w[:, :, :], w["expert_w"].rearrange("n d h -> d n h")).then_inc(experts_loaded, 16)

                @block.gpsimd
                def _(pool):
                    nc.gpsimd.memset(ones[:, :], 1.0).then_inc(ones_ready, 1)
                    nc.gpsimd.memset(zeros[:, :], 0.0).then_inc(zeros_ready, 1)
                    nc.gpsimd.memset(power[:, 0, :], -0.5).then_inc(ones_ready, 1)
                    nc.gpsimd.memset(power[:, 1, :], LN_EPS).then_inc(ones_ready, 1)
                    ln.set_up(nc, pool)
                    ln.take_rstd(nc, pool, 0)
                    pool.wait_ge(phiT_high_ready, 1)
                    nc.gpsimd.tensor_tensor(phiT[1][:, :], phiT_in[:, :], phiT[0][:, :], ALU.subtract).then_inc(phiT_ready, 1)
                    pool.wait_ge(bias_split, 1)
                    nc.gpsimd.tensor_tensor(bias_rest, bias_row, bias_parts[0], ALU.subtract).then_inc(bias_split, 1)
                    ln.take_rstd(nc, pool, 1)
                    pool.wait_ge(bias_split, 3)
                    nc.gpsimd.tensor_tensor(bias_row, bias_rest, bias_parts[1], ALU.subtract).then_inc(bias_split, 1)
                    for g in range(2, LN_GROUPS):
                        ln.take_rstd(nc, pool, g)

                    rest = (rowsT_high_ready, rowsT_ready)
                    rows_rest(pool, rest, 0, 0)
                    rows_rest(pool, rest, 1, 1)

                    def step(n, buf):
                        for half in range(2):
                            pool.wait_ge(exp_done, 2 * n + half + 1)
                            pool.wait_ge(inverse_ready, 2 * n + half + 1)
                            e = expd3[buf][:, half * HALF:(half + 1) * HALF].rearrange("p (e s) -> p e s", s=SLOTS)
                            nc.gpsimd.tensor_tensor(e, e, total[:, half, :].unsqueeze(2).to_broadcast([P, SEXPERTS // 2, SLOTS]),
                                                    ALU.mult).then_inc(weights_ready, 1)
                            if half == 0 and there(n + 2 if isinstance(n, int) else n):
                                rows_rest(pool, rest, n + 2, (buf + 2) % 3)

                    tiles_in_threes(pool, step, 0)
                    pool.wait_ge(slot_mv, 1)
                    nc.gpsimd.tensor_tensor(var[:, :], mv[:, :, 1], power[:, 1, :], ALU.add).then_inc(slot_var, 1)
                    pool.wait_ge(slot_var, 1)
                    nc.gpsimd.tensor_tensor(rstd[:, :], var[:, :], power[:, 0, :], ALU.pow).then_inc(slot_rstd, 1)

                @block.vector
                def _(dve):
                    for g in range(LN_GROUPS):
                        first = ln.tiles * g
                        ln.run(nc, dve, lambda t: X[:, first + t, :], xn_all[:, first:first + ln.tiles, :], g)
                    dve.wait_ge(bias_split, 5)
                    dve.wait_ge(bias_loaded, 48)

                    def shift(n, buf, half):
                        seen = 2 * n + half
                        cols = slice(half * HALF, (half + 1) * HALF)
                        experts = ps_logits[:, cols].rearrange("p (e s) -> p e s", s=SLOTS)
                        dve.wait_ge(logits_made, seen + 1)
                        nc.vector.tensor_reduce(peak[:, half, :], experts, AX.X, ALU.max).then_inc(peak_ready, 1)
                        dve.wait_ge(peak_ready, seen + 1)
                        above_zero(dve, mixed, n - 2)
                        nc.vector.tensor_tensor(expd3[buf][:, cols].rearrange("p (e s) -> p e s", s=SLOTS), experts,
                                                peak[:, half, :].unsqueeze(2).to_broadcast([P, SEXPERTS // 2, SLOTS]),
                                                ALU.subtract).then_inc(shifted, 1)

                    def invert(n, buf, half):
                        seen = 2 * n + half
                        dve.wait_ge(exp_done, seen + 1)
                        above_zero(dve, weights_ready, seen - 1)
                        e = expd3[buf][:, half * HALF:(half + 1) * HALF].rearrange("p (e s) -> p e s", s=SLOTS)
                        nc.vector.tensor_reduce(total[:, half, :], e, AX.X, ALU.add).then_inc(total_ready, 1)
                        dve.wait_ge(total_ready, seen + 1)
                        nc.vector.reciprocal(total[:, half, :], total[:, half, :]).then_inc(inverse_ready, 1)

                    def step(n, buf):
                        if there(n):
                            shift(n, buf, 0)
                        if there(n - 1 if isinstance(n, int) else n):
                            invert(n - 1, (buf + 2) % 3, 1)
                        if there(n):
                            shift(n, buf, 1)
                            invert(n, buf, 0)

                    tiles_in_threes(dve, step, 1)

                    dve.wait_ge(slots_made, 1)
                    nc.vector.tensor_scalar(slots[:, :, :], ps_slots[:, :, :], SLOT_LOW, SLOT_HIGH, ALU.max, ALU.min).then_inc(clipped, 1)
                    dve.wait_ge(clipped, 1)
                    for s in range(SLOT_TILES):
                        last = nc.vector.bn_stats(stats[:, s, :], slots[:, s, :])
                    last.then_inc(slot_stats, 1)
                    dve.wait_ge(slot_stats, 1)
                    for s in range(SLOT_TILES):
                        last = nc.vector.bn_aggr(mv[:, s, :], stats[:, s, :])
                    last.then_inc(slot_mv, 1)
                    dve.wait_ge(slot_rstd, 1)
                    for s in range(SLOT_TILES):
                        last = nc.vector.tensor_scalar(slots[:, s, :], slots[:, s, :], mv[:, s, 0:1], rstd[:, s:s + 1],
                                                       ALU.subtract, ALU.mult)
                    last.then_inc(slot_normed, 1)
                    dve.wait_ge(experts_loaded, 16 * (TILE_EXPERTS + 1))
                    for bank in range(BANKS):
                        tiles = slice(bank * BANK_TILES, (bank + 1) * BANK_TILES)
                        dve.wait_ge(experts_made, bank + 1)
                        last = nc.vector.tensor_tensor(slot_out[:, tiles, :], ps_slots[:, tiles, :], expert_b[:, tiles, :], ALU.add)
                    last.then_inc(slot_out_ready, 1)

                @block.scalar
                def _(act):
                    act.wait_ge(w_loaded, 16 * len(loads))
                    nc.scalar.activation(phiT[0][:, :], phiT_in[:, :], ACT.Copy).then_inc(phiT_high_ready, 1)
                    nc.scalar.activation(bias_parts[0], bias_row, ACT.Copy).then_inc(bias_split, 1)
                    for b in range(BATCHES):
                        act.wait_ge(xnT_made, b + 1)
                        nc.scalar.activation(xnT[:, SEQ * b:SEQ * (b + 1)], ps_logits[:, b % BANKS * BANK:(b % BANKS + 1) * BANK],
                                             ACT.Copy).then_inc(xnT_ready, 1)
                        if b == GROUP_BATCHES - 1:
                            act.wait_ge(bias_split, 2)
                            nc.scalar.activation(bias_parts[1], bias_rest, ACT.Copy).then_inc(bias_split, 1)
                        if b == 2 * GROUP_BATCHES - 1:
                            act.wait_ge(bias_split, 4)
                            nc.scalar.activation(bias_parts[2], bias_row, ACT.Copy).then_inc(bias_split, 1)
                    act.wait_ge(xnT_ready, BATCHES)

                    act.wait_ge(phiT_ready, 1)

                    def fetch(n, buf):
                        above_zero(act, logits_made, 2 * (n - 2))
                        nc.scalar.activation(rowsT[buf][0][:, :], xnT[:, bass.ds(P * n, P)], ACT.Copy).then_inc(rowsT_high_ready, 1)

                    def step(n, buf):
                        for half in range(2):
                            cols = slice(half * HALF, (half + 1) * HALF)
                            act.wait_ge(shifted, 2 * n + half + 1)
                            nc.scalar.activation(expd3[buf][:, cols], expd3[buf][:, cols], ACT.Exp).then_inc(exp_done, 1)
                            if half == 0 and there(n + 2 if isinstance(n, int) else n):
                                fetch(n + 2, (buf + 2) % 3)

                    fetch(0, 0)
                    fetch(1, 1)
                    tiles_in_threes(act, step, 0)

                    act.wait_ge(slot_normed, 1)
                    nc.scalar.activation(slots[:, :, :], slots[:, :, :], ACT.Tanh).then_inc(slot_tanh, 1)
                    act.wait_ge(slotsT_made, 1)
                    nc.scalar.activation(slotsT[:, :], ps_logits[:, :], ACT.Copy).then_inc(slotsT_ready, 1)

                @block.tensor
                def _(pe):
                    mm = nc.tensor.matmul

                    for b in range(BATCHES):
                        pe.wait_ge(ln.ready, b // GROUP_BATCHES + 1)
                        above_zero(pe, xnT_ready, b - BANKS + 1)
                        for t in range(TILES):
                            at = b % BANKS * BANK + t * P
                            last = nc.tensor.transpose(ps_logits[:, at:at + P], xn_all[:, TILES * b + t, :], ident[:, :])
                        last.then_inc(xnT_made, 1)
                    pe.wait_ge(xnT_ready, BATCHES)
                    pe.wait_ge(bias_loaded, 48)
                    pe.wait_ge(phiT_ready, 1)
                    pe.wait_ge(ones_ready, 3)
                    pe.wait_ge(zeros_ready, 1)

                    def all_slots_plus_nothing(start, stop):
                        for bank in range(BANKS):
                            last = mm(ps_slots[:, bank * BANK_TILES:(bank + 1) * BANK_TILES, :].rearrange("p s d -> p (s d)"),
                                      zeros[:, 0:P], zeros[:, :], start=start, stop=stop)
                        return last

                    all_slots_plus_nothing(True, False)

                    def step(n, buf):
                        m = n - 2
                        for half in range(2):
                            if there(n):
                                pe.wait_ge(rowsT_ready, n + 1)
                                above_zero(pe, shifted, 2 * n + half - 1)
                                logits(mm, ps_logits, rowsT[buf], 2 * half)
                                logits(mm, ps_logits, rowsT[buf], 2 * half + 1).then_inc(logits_made, 1)
                            if there(m if isinstance(n, int) else n):
                                pe.wait_ge(weights_ready, 2 * m + half + 1)
                                for s in range(half * SLOT_TILES // 2, (half + 1) * SLOT_TILES // 2):
                                    last = mm(ps_slots[:, s, :], expd3[(buf + 1) % 3][:, s * P:(s + 1) * P],
                                              xn_all[:, bass.ds(m, 1), :].rearrange("p o d -> p (o d)"), start=False, stop=False)
                                if half == 1:
                                    last.then_inc(mixed, 1)

                    tiles_in_threes(pe, step, 2)
                    all_slots_plus_nothing(False, True).then_inc(slots_made, 1)
                    pe.wait_ge(slot_tanh, 1)
                    for s in range(SLOT_TILES):
                        last = nc.tensor.transpose(ps_logits[:, s * P:(s + 1) * P], slots[:, s, :], ident[:, :])
                    last.then_inc(slotsT_made, 1)
                    pe.wait_ge(slotsT_ready, 1)
                    pe.wait_ge(experts_loaded, 16 * (TILE_EXPERTS + 1))
                    for n in range(SEXPERTS):
                        s, j = n // TILE_EXPERTS, n % TILE_EXPERTS
                        last = mm(ps_slots[j * SLOTS:(j + 1) * SLOTS, s, :], slotsT[:, n * SLOTS:(n + 1) * SLOTS],
                                  expert_w[:, n, :], start=True, stop=True)
                        if n % (SEXPERTS // BANKS) == SEXPERTS // BANKS - 1:
                            last.then_inc(experts_made, 1)

        with ExitStack() as ctx:
            mem = Memory(nc, ctx)
            sb, ps, sem = mem.sb, mem.ps, mem.sem
            largest = sb("d_largest", [P, SLOTS])
            weights = [sb(f"d_weights{i}", [P, ALL_SLOTS]) for i in range(2)]
            weightsT = [sb(f"d_weightsT{i}", [P, SLOT_TILES, P]) for i in range(2)]
            ps_logits = ps("d_ps_logits2", [P, ALL_SLOTS])
            ps_turn = ps("d_ps_turn", [P, 2, BANK])
            ps_out = ps("d_ps_out", [P, BANK])
            rowsT_high_ready, rowsT_ready, logits_made, peak_ready, shifted, exp_done = (
                sem(f"d2_{n}") for n in ("rowsT_high_ready", "rowsT_ready", "logits_made", "peak_ready", "shifted", "exp_done"))
            total_ready, inverse_ready, weights_ready, turned, weightsT_ready, mixed, added = (
                sem(f"d2_{n}") for n in ("total_ready", "inverse_ready", "weights_ready", "turned", "weightsT_ready", "mixed", "added"))
            stored, half_peak_ready = sem("d2_stored"), sem("d2_half_peak_ready")
            out_view = out.rearrange("b (t p) d -> p (b t) d", p=P)

            with nc.Block() as block:

                @block.sync
                def _(sp):
                    def store(n):
                        sp.wait_ge(added, n + 1)
                        sp.dma_start(out_view[:, bass.ds(n, 1), :], X[:, bass.ds(n, 1), :]).then_inc(stored, 16)

                    store(0)
                    with sp.Fori(1, ROW_TILES) as n:
                        store(n)
                    sp.wait_ge(stored, 16 * ROW_TILES)

                @block.gpsimd
                def _(pool):
                    rest = (rowsT_high_ready, rowsT_ready)
                    rows_rest(pool, rest, 0, 0)
                    rows_rest(pool, rest, 1, 1)

                    def step(n, par):
                        if there(n + 2 if isinstance(n, int) else n):
                            rows_rest(pool, rest, n + 2, par)
                        if there(n):
                            pool.wait_ge(inverse_ready, n + 1)
                            pool.wait_ge(exp_done, 2 * (n + 1))
                            above_zero(pool, turned, BANKS * (n - 1))
                            nc.gpsimd.tensor_tensor(
                                weights[par][:, :].rearrange("p (e s) -> p e s", s=SLOTS),
                                expd[par][:, :].rearrange("p (e s) -> p e s", s=SLOTS),
                                total[:, 0, :].unsqueeze(1).to_broadcast([P, SEXPERTS, SLOTS]), ALU.mult).then_inc(weights_ready, 1)

                    tiles_in_pairs(pool, step, 0)

                @block.vector
                def _(dve):
                    def half_peak(n, half):
                        dve.wait_ge(logits_made, 2 * n + half + 1)
                        nc.vector.tensor_reduce(peak[:, half, :], ps_logits[:, half * HALF:(half + 1) * HALF]
                                                .rearrange("p (e s) -> p s e", s=SLOTS), AX.X, ALU.max).then_inc(half_peak_ready, 1)

                    def shift(n, par):
                        dve.wait_ge(half_peak_ready, 2 * (n + 1))
                        nc.vector.tensor_tensor(largest[:, :], peak[:, 0, :], peak[:, 1, :], ALU.max).then_inc(peak_ready, 1)
                        dve.wait_ge(peak_ready, n + 1)
                        above_zero(dve, weights_ready, n - 1)
                        for half in range(2):
                            cols = slice(half * HALF, (half + 1) * HALF)
                            nc.vector.tensor_tensor(expd[par][:, cols].rearrange("p (e s) -> p e s", s=SLOTS),
                                                    ps_logits[:, cols].rearrange("p (e s) -> p e s", s=SLOTS),
                                                    largest[:, :].unsqueeze(1).to_broadcast([P, SEXPERTS // 2, SLOTS]),
                                                    ALU.subtract).then_inc(shifted, 1)

                    def invert(n, par):
                        dve.wait_ge(exp_done, 2 * (n + 1))
                        above_zero(dve, weights_ready, n)
                        nc.vector.tensor_reduce(total[:, 0, :], expd[par][:, :].rearrange("p (e s) -> p s e", s=SLOTS),
                                                AX.X, ALU.add).then_inc(total_ready, 1)
                        dve.wait_ge(total_ready, n + 1)
                        nc.vector.reciprocal(total[:, 0, :], total[:, 0, :]).then_inc(inverse_ready, 1)

                    def add(n):
                        dve.wait_ge(mixed, n + 1)
                        x = X[:, bass.ds(n, 1), :].rearrange("p o d -> p (o d)")
                        nc.vector.tensor_tensor(x, ps_out[:, 0:D], x, ALU.add).then_inc(added, 1)

                    def step(n, par):
                        if there(n):
                            half_peak(n, 1)
                            shift(n, par)
                        if there(n - 2 if isinstance(n, int) else n):
                            add(n - 2)
                        if there(n + 1 if isinstance(n, int) else n):
                            half_peak(n + 1, 0)
                        if there(n):
                            invert(n, par)

                    half_peak(0, 0)
                    tiles_in_pairs(dve, step, 2)

                @block.scalar
                def _(act):
                    def fetch(n, par):
                        above_zero(act, logits_made, 2 * (n - 1))
                        nc.scalar.activation(rowsT[par][0][:, :], xnT[:, bass.ds(P * n, P)], ACT.Copy).then_inc(rowsT_high_ready, 1)

                    def step(n, par):
                        if there(n):
                            for half in range(2):
                                cols = slice(half * HALF, (half + 1) * HALF)
                                act.wait_ge(shifted, 2 * n + half + 1)
                                nc.scalar.activation(expd[par][:, cols], expd[par][:, cols], ACT.Exp).then_inc(exp_done, 1)
                        if there(n + 2 if isinstance(n, int) else n):
                            fetch(n + 2, par)
                        if there(n - 1 if isinstance(n, int) else n):
                            for bank in range(BANKS):
                                copy(n - 1, 1 - par, bank)

                    def copy(n, par, bank):
                        act.wait_ge(turned, BANKS * n + bank + 1)
                        above_zero(act, mixed, n - 1)
                        tiles = slice(bank * BANK_TILES, (bank + 1) * BANK_TILES)
                        nc.scalar.activation(weightsT[par][:, tiles, :],
                                             ps_turn[:, bank % 2, :].rearrange("p (s t) -> p s t", t=P), ACT.Copy)\
                            .then_inc(weightsT_ready, 1)

                    fetch(0, 0)
                    fetch(1, 1)
                    tiles_in_pairs(act, step, 1)

                @block.tensor
                def _(pe):
                    mm = nc.tensor.matmul

                    def turn(n, par, bank):
                        above_zero(pe, weightsT_ready, BANKS * n + bank - 1)
                        for j in range(BANK_TILES):
                            s = bank * BANK_TILES + j
                            last = nc.tensor.transpose(ps_turn[:, bank % 2, j * P:(j + 1) * P], weights[par][:, s * P:(s + 1) * P],
                                                       ident[:, :])
                        last.then_inc(turned, 1)

                    def step(n, par):
                        back = there(n - 2 if isinstance(n, int) else n)
                        m = n - 2
                        if there(n):
                            pe.wait_ge(rowsT_ready, n + 1)
                        for half in range(2):
                            if there(n):
                                above_zero(pe, shifted, 2 * n + half - 1)
                                logits(mm, ps_logits, rowsT[par], 2 * half)
                                logits(mm, ps_logits, rowsT[par], 2 * half + 1).then_inc(logits_made, 1)
                            if back and half == 0:
                                pe.wait_ge(weights_ready, m + 1)
                            if back:
                                turn(m, par, 2 * half)
                                turn(m, par, 2 * half + 1)
                        if back:
                            above_zero(pe, added, m)
                            for s in range(SLOT_TILES):
                                if s % BANK_TILES == 0:
                                    pe.wait_ge(weightsT_ready, BANKS * m + s // BANK_TILES + 1)
                                last = mm(ps_out[:, 0:D], weightsT[par][:, s, :], slot_out[:, s, :],
                                          start=(s == 0), stop=(s == SLOT_TILES - 1))
                            last.then_inc(mixed, 1)

                    tiles_in_pairs(pe, step, 2)


def build(nc, x_in, w, c, out):
    with ExitStack() as ctx:
        mem = Memory(nc, ctx)
        X = mem.sb("x_rows", [P, BATCHES * TILES, D])
        ident = mem.sb("ident", [P, P])
        with ExitStack() as first:
            w1_in, w1_loads = first_layers(Memory(nc, first), w)
            stage_causal_attention(nc, X, ident, x_in, w, c, w1_loads)
            stage_experts(nc, X, ident, w, c, w1_in)
        stage_cosine_attention(nc, X, ident, w, c)
        stage_slots(nc, X, ident, w, c, out)


def laid_out(a):
    import numpy as np

    bfloat16 = "bfloat16"

    w = {}
    w["wqT"], w["wkT"], w["woT"] = (np.ascontiguousarray(a[f"L0_attn_W{n}"].T) for n in "qko")
    wv = np.zeros((D, HEADS, VW), np.float32)
    wv[:, :, :HD] = a["L0_attn_Wv"].T.reshape(D, HEADS, HD)
    w["wvT"] = wv.reshape(D, HEADS * VW)
    bv = np.ones((HEADS, VW), np.float32)
    bv[:, :HD] = a["L0_attn_bv"].reshape(HEADS, HD)
    w["bv"] = bv.reshape(HEADS * VW)
    w["bq"], w["bk"] = (a[f"L0_attn_b{n}"].reshape(D, 1) for n in "qk")
    w["bo"] = a["L0_attn_bo"].reshape(1, D)

    c = {}
    c["ident"] = np.eye(P, dtype=np.float32)
    c["ident_bf16"] = np.eye(P).astype(bfloat16)
    after = np.triu(np.ones((P, P)), 1)
    c["mask_qk"] = (-1e30 * after).astype(bfloat16)
    c["mask_kq"] = (-1e30 * after.T).astype(bfloat16)
    slopes = np.array([2.0 ** (-(h + 1) / 2) for h in range(HEADS)], np.float32)
    decay = slopes[:, None] * np.arange(SEQ, dtype=np.float32)
    rows = []
    for _ in range(3):
        rows.append(decay.astype(bfloat16))
        decay = decay - rows[-1].astype(np.float32)
    one = np.ones((HEADS, SEQ), bfloat16)
    c["rows_k"] = np.stack([*rows, one, one])
    c["rows_q"] = np.stack([one, one, one])
    more_layouts(a, w, c)
    return w, c


def kernel(**inputs):
    import numpy as np
    import concourse.bacc as bacc
    from concourse.bass_utils import run_bass_kernel_spmd

    a = {n: np.asarray(x) for n, x in inputs.items()}
    w, c = laid_out(a)
    nc = bacc.Bacc("TRN2", target_bir_lowering=False, num_devices=1)
    arrays, aps = {}, {}
    for kind, named in (("x", {"x": a["L0_attn_x"]}), ("w", w), ("c", c)):
        for n, x in named.items():
            x = np.ascontiguousarray(x)
            arrays[f"in_{kind}_{n}"] = x
            aps[kind, n] = nc.dram_tensor(f"in_{kind}_{n}", x.shape, mybir.dt.from_np(x.dtype), kind="ExternalInput").ap()
    out = nc.dram_tensor("out_dram", a["L0_attn_x"].shape, F32, kind="ExternalOutput").ap()
    build(nc, aps["x", "x"], {n: aps["w", n] for n in w}, {n: aps["c", n] for n in c}, out)
    return run_bass_kernel_spmd(nc, [arrays], core_ids=[0]).results[0]["out_dram"]


def more_layouts(a, w, c):
    import numpy as np

    w["rw1"], w["W1"], w["W2"], w["b2"], w["rw2"] = (a[f"L0_ffn_{n}"] for n in ("rw1", "W1", "W2", "b2", "rw2"))
    w["rb2"] = a["L0_ffn_rb2"].reshape(1, EXPERTS)
    b1 = np.concatenate([a["L0_ffn_rb1"][None], a["L0_ffn_b1"]]).reshape(UNITS, FF_TILES, P)
    w["b1"] = np.ascontiguousarray(b1.transpose(2, 0, 1))
    c["earlier"] = np.tril(np.ones((EXPERTS, EXPERTS), np.float32), -1)

    w["qkv"] = a["L1_attn_w_qkv"]
    out = np.zeros((VC, CHEADS, D + 1), np.float32)
    out[:CHD, :, :D] = a["L1_attn_w_out"].reshape(CHEADS, CHD, D).transpose(1, 0, 2)
    out[CHD, :, D] = 1
    w["out"] = out
    w["b_out"] = a["L1_attn_b_out"]
    w["log_scale"] = a["L1_attn_logit_scale"].reshape(CHEADS)
    w["phiT"] = np.ascontiguousarray(a["L1_ffn_phi_w"].T)
    w["phi_b"] = a["L1_ffn_phi_b"].reshape(1, ALL_SLOTS)
    w["expert_w"], w["expert_b"] = a["L1_ffn_expert_w"], a["L1_ffn_expert_b"]
```
